# Optimizing a Trainium2 kernel written in Bass

```python
import numpy as np
import jax
import jax.numpy as jnp

def _softmax(x, axis=-1):
    return jax.nn.softmax(x, axis=axis)

def _gelu(x):
    return jax.nn.gelu(x, approximate=True)

def _silu(x):
    return jax.nn.silu(x)

def _sigmoid(x):
    return jax.nn.sigmoid(x)

def _layernorm(x, axis=-1, eps=1e-05):
    m = jnp.mean(x, axis=axis, keepdims=True)
    v = jnp.var(x, axis=axis, keepdims=True)
    return (x - m) / jnp.sqrt(v + eps)

def _scatter_add(tgt, idx, src, axis=0):
    return tgt.at[idx].add(src)

def _segment_sum(src, seg, n):
    return jax.ops.segment_sum(src, seg, n)
kernel_name = 'mk_decoder_preln_d2_seqx_r8_749c0c'

def setup_inputs(seed: int=0):
    np.random.seed(seed)
    _w = jnp.asarray

    def _rec_inputs():
        import jax
        import jax.numpy as jnp
        _rk = jax.random.key(seed)
        x = -0.0003929 + 0.9999 * jax.random.normal(jax.random.fold_in(_rk, 1), (4, 256, 256), jnp.float32)
        _lenS = 256 - jax.random.randint(jax.random.fold_in(_rk, 7), (4,), 0, max(1, 256 // 4) + 1, jnp.int32)
        _lenS2 = 256 - jax.random.randint(jax.random.fold_in(_rk, 8), (4,), 0, max(1, 256 // 4) + 1, jnp.int32)
        _ctx_2048P = jax.random.normal(jax.random.fold_in(_rk, 11), (4, 16, 256), jnp.float32)
        _ctx_2048c = jax.random.dirichlet(jax.random.fold_in(_rk, 511), 0.3 * jnp.ones((16,), jnp.float32), (4, 256))
        _ctx_2048t = jnp.einsum('bsk,bkd->bsd', _ctx_2048c, _ctx_2048P)
        _ctx_2048t = _ctx_2048t * jax.lax.rsqrt(jnp.mean(jnp.square(_ctx_2048t)) + 1e-12) * 0.953939
        ctx_2048 = -0.000514642 + 1.00011 * (_ctx_2048t + 0.3 * jax.random.normal(jax.random.fold_in(_rk, 611), (4, 256, 256), jnp.float32))
        _validS = jnp.arange(256)[None, :] < _lenS[:, None]
        _validS2 = jnp.arange(256)[None, :] < _lenS2[:, None]
        _causal = jnp.tril(jnp.ones((256, 256), dtype=bool))
        mask_BxS2_ik0 = jnp.where(jnp.broadcast_to(_validS2[:, :], (4, 256)), 0, 1).astype(jnp.int32)
        return (x, ctx_2048, mask_BxS2_ik0)
    x, ctx_2048, mask_BxS2_ik0 = _rec_inputs()

    def _L0_attn_setup():
        import jax, jax.numpy as jnp
        import numpy as np
        B, S, M = (1, 256, 256)
        H, HKV, D = (32, 8, 64)
        SW = 128
        WAVELENGTH = 150000.0
        SCALE = D ** (-0.25)
        NEG = -1000000000.0

        def _cos_sin(seq_len, dtype):
            half = D // 2
            inv_freq = 1.0 / WAVELENGTH ** (jnp.arange(half, dtype=jnp.float32) * 2.0 / D)
            t = jnp.arange(seq_len, dtype=jnp.float32)
            freqs = t[:, None] * inv_freq[None, :]
            return (jnp.cos(freqs)[None, :, None, :].astype(dtype), jnp.sin(freqs)[None, :, None, :].astype(dtype))

        def _interleaved_rope(x, cos, sin):
            x_even = x[..., ::2]
            x_odd = x[..., 1::2]
            first = x_even * cos - x_odd * sin
            second = x_odd * cos + x_even * sin
            return jnp.stack([first, second], axis=-1).reshape(x.shape)
        key = jax.random.key(seed)
        ks = jax.random.split(key, 8)
        return {'hidden_states': jax.random.normal(ks[0], (B, S, M), jnp.float32), 'Wq': jax.random.normal(ks[1], (M, H, D), jnp.float32) * 0.02, 'bq': jnp.zeros((H, D), jnp.float32), 'Wk': jax.random.normal(ks[2], (M, HKV, D), jnp.float32) * 0.02, 'bk': jnp.zeros((HKV, D), jnp.float32), 'Wv': jax.random.normal(ks[3], (M, HKV, D), jnp.float32) * 0.02, 'bv': jnp.zeros((HKV, D), jnp.float32), 'Wo': jax.random.normal(ks[4], (H, D, M), jnp.float32) * 0.02, 'bo': jnp.zeros((M,), jnp.float32), 'sinks': jax.random.normal(ks[5], (H,), jnp.float32)}
    _L0_attn_all = _L0_attn_setup()
    _L0_attn_in = {k: v for k, v in _L0_attn_all.items() if k in ('Wq', 'bq', 'Wk', 'bk', 'Wv', 'bv', 'Wo', 'bo', 'sinks')}
    del _L0_attn_all

    def _L0_xattn_setup():
        import jax, jax.numpy as jnp
        import numpy as np
        import math
        H = 256
        NH = 16
        HD = H // NH
        EPS_LN = 1e-05
        RES_SCALE_MAX = 0.3

        def _nan_clean(x, lim=10000.0):
            return jnp.nan_to_num(x, nan=0.0, posinf=lim, neginf=-lim)
        key = jax.random.key(seed)
        ks = jax.random.split(key, 12)
        B, S, T = (4, 256, 32)
        std = 1.0 / math.sqrt(H)
        return {'hidden_states': jax.random.normal(ks[0], (B, S, H), jnp.float32), 'audio_tokens': jax.random.normal(ks[1], (B, T, H), jnp.float32), 'attention_mask': jax.random.randint(ks[2], (B, T), 0, 2, jnp.int32), 'Wq': jax.random.normal(ks[3], (H, H), jnp.float32) * std, 'bq': jnp.zeros((H,), jnp.float32), 'Wk': jax.random.normal(ks[4], (H, H), jnp.float32) * std, 'bk': jnp.zeros((H,), jnp.float32), 'Wv': jax.random.normal(ks[5], (H, H), jnp.float32) * std, 'bv': jnp.zeros((H,), jnp.float32), 'Wo': jax.random.normal(ks[6], (H, H), jnp.float32) * std, 'bo': jnp.zeros((H,), jnp.float32), 'ln_gamma': jnp.ones((H,), jnp.float32), 'ln_beta': jnp.zeros((H,), jnp.float32), 'residual_scale': jnp.float32(0.05)}
    _L0_xattn_all = _L0_xattn_setup()
    _L0_xattn_in = {k: v for k, v in _L0_xattn_all.items() if k in ('Wq', 'bq', 'Wk', 'bk', 'Wv', 'bv', 'Wo', 'bo', 'ln_gamma', 'ln_beta', 'residual_scale')}
    del _L0_xattn_all

    def _L0_ffn_setup():
        import jax, jax.numpy as jnp
        import numpy as np
        E = 8
        TOP_K = 2
        H = 256
        I_MOE = 176
        I_SH = 704
        B, S = (2, 256)

        def _moe_forward(hidden_states, router_weight, gate_up_proj, down_proj, sh_gate_w, sh_up_w, sh_down_w, shared_gate_w):
            b, s, h = hidden_states.shape
            x = hidden_states.reshape(-1, h)
            shared = jnp.einsum('ti,hi->th', jax.nn.silu(x @ sh_gate_w.T) * (x @ sh_up_w.T), sh_down_w)
            logits = x @ router_weight.T
            probs = jax.nn.softmax(logits.astype(jnp.float32), axis=-1)
            top_v, top_i = jax.lax.top_k(probs, TOP_K)
            top_v = top_v / top_v.sum(axis=-1, keepdims=True)
            combine = (jax.nn.one_hot(top_i, E, dtype=top_v.dtype) * top_v[..., None]).sum(axis=1)
            out = jnp.zeros_like(x)
            for e in range(E):
                gu = x @ gate_up_proj[e].T
                gate, up = (gu[:, :I_MOE], gu[:, I_MOE:])
                cur = jax.nn.silu(gate) * up @ down_proj[e].T
                out = out + cur * combine[:, e:e + 1]
            out = out + jax.nn.sigmoid(x @ shared_gate_w.T) * shared
            return out.reshape(b, s, h)
        key = jax.random.key(seed)
        ks = jax.random.split(key, 8)
        scale = 0.02
        return {'hidden_states': jax.random.normal(ks[0], (B, S, H), dtype=jnp.float32), 'router_weight': jax.random.normal(ks[1], (E, H), dtype=jnp.float32) * scale, 'gate_up_proj': jax.random.normal(ks[2], (E, 2 * I_MOE, H), dtype=jnp.float32) * scale, 'down_proj': jax.random.normal(ks[3], (E, H, I_MOE), dtype=jnp.float32) * scale, 'sh_gate_w': jax.random.normal(ks[4], (I_SH, H), dtype=jnp.float32) * scale, 'sh_up_w': jax.random.normal(ks[5], (I_SH, H), dtype=jnp.float32) * scale, 'sh_down_w': jax.random.normal(ks[6], (H, I_SH), dtype=jnp.float32) * scale, 'shared_gate_w': jax.random.normal(ks[7], (1, H), dtype=jnp.float32) * scale}
    _L0_ffn_all = _L0_ffn_setup()
    _L0_ffn_in = {k: v for k, v in _L0_ffn_all.items() if k in ('router_weight', 'gate_up_proj', 'down_proj', 'sh_gate_w', 'sh_up_w', 'sh_down_w', 'shared_gate_w')}
    del _L0_ffn_all

    def _L1_attn_setup():
        import jax, jax.numpy as jnp
        import numpy as np
        D_MODEL = 256
        N_HEADS = 16
        D_K = 128
        EPS = 1e-05
        ROPE_BASE = 10000.0

        def rope(x):
            b, s, h, d = x.shape
            d2 = d // 2
            theta = 1.0 / ROPE_BASE ** (jnp.arange(0, d, 2, dtype=jnp.float32) / d)
            pos = jnp.arange(s, dtype=jnp.float32)
            freqs = pos[:, None] * theta[None, :]
            freqs = jnp.concatenate([freqs, freqs], axis=-1)
            cos = jnp.cos(freqs)[None, :, None, :]
            sin = jnp.sin(freqs)[None, :, None, :]
            x_rot = jnp.concatenate([-x[..., d2:], x[..., :d2]], axis=-1)
            return x * cos + x_rot * sin
        key = jax.random.key(seed)
        ks = jax.random.split(key, 10)
        hd = N_HEADS * D_K

        def xavier(k, shape):
            fan_in, fan_out = (shape[1], shape[0])
            lim = np.sqrt(6.0 / (fan_in + fan_out))
            return jax.random.uniform(k, shape, jnp.float32, -lim, lim)
        return {'h': jax.random.normal(ks[0], (2, 256, D_MODEL), jnp.float32), 'wq': xavier(ks[1], (hd, D_MODEL)), 'bq': jnp.zeros((hd,), jnp.float32), 'wk': xavier(ks[2], (hd, D_MODEL)), 'bk': jnp.zeros((hd,), jnp.float32), 'wv': xavier(ks[3], (hd, D_MODEL)), 'bv': jnp.zeros((hd,), jnp.float32), 'wo': xavier(ks[4], (D_MODEL, hd)), 'bo': jnp.zeros((D_MODEL,), jnp.float32), 'ln_g': jnp.ones((D_MODEL,), jnp.float32), 'ln_b': jnp.zeros((D_MODEL,), jnp.float32)}
    _L1_attn_all = _L1_attn_setup()
    _L1_attn_in = {k: v for k, v in _L1_attn_all.items() if k in ('wq', 'bq', 'wk', 'bk', 'wv', 'bv', 'wo', 'bo', 'ln_g', 'ln_b')}
    del _L1_attn_all

    def _L1_xattn_setup():
        import jax, jax.numpy as jnp
        import numpy as np
        B, S, DIM, HD = (4, 128, 256, 128)
        H = DIM // HD
        GN_EPS = 0.001

        def _decay_masks(n_heads, seq_len):
            gam = 1.0 - 2.0 ** (-5.0 - jnp.arange(n_heads, dtype=jnp.float32))
            idx = jnp.arange(seq_len, dtype=jnp.float32)
            expo = idx[None, :] - idx[:, None]
            D = jnp.where(expo[None, :, :] <= 0, gam[:, None, None] ** expo[None, :, :], 0.0)
            return D / jnp.sqrt(D.sum(axis=-1))[:, None, :]
        key = jax.random.key(seed)
        ks = jax.random.split(key, 8)
        x = jax.random.normal(ks[0], (B, S, DIM), dtype=jnp.float32)
        k = jax.random.normal(ks[1], (B, S, DIM), dtype=jnp.float32)
        v = jax.random.normal(ks[2], (B, S, DIM), dtype=jnp.float32)
        Wh = jax.random.normal(ks[3], (H, HD, HD), dtype=jnp.float32) / np.sqrt(HD)
        wg_w = jax.random.normal(ks[4], (DIM, DIM), dtype=jnp.float32) / np.sqrt(DIM)
        wo_w = jax.random.normal(ks[5], (DIM, DIM), dtype=jnp.float32) / np.sqrt(DIM)
        gn_gamma = jnp.ones((DIM,), dtype=jnp.float32)
        gn_beta = jnp.zeros((DIM,), dtype=jnp.float32)
        return {'x': x, 'k': k, 'v': v, 'Wh': Wh, 'wg_w': wg_w, 'wo_w': wo_w, 'gn_gamma': gn_gamma, 'gn_beta': gn_beta}
    _L1_xattn_all = _L1_xattn_setup()
    _L1_xattn_in = {k: v for k, v in _L1_xattn_all.items() if k in ('Wh', 'wg_w', 'wo_w', 'gn_gamma', 'gn_beta')}
    del _L1_xattn_all

    def _L1_ffn_setup():
        import jax, jax.numpy as jnp
        import numpy as np
        HIDDEN = 256
        INTER = 1024
        RETRIEVAL = 128
        NUM_EXPERTS = 512
        NUM_KEYS = 64
        TOP_K = 8
        B, S = (4, 256)
        key = jax.random.key(seed)
        ks = jax.random.split(key, 8)
        sc = 0.02
        return {'hidden_states': jax.random.normal(ks[0], (B, S, HIDDEN), jnp.float32), 'W_q': jax.random.normal(ks[1], (HIDDEN, RETRIEVAL), jnp.float32) * sc, 'keys': jax.random.normal(ks[2], (2, RETRIEVAL // 2, NUM_KEYS), jnp.float32) * sc, 'down_embed': jax.random.normal(ks[3], (NUM_EXPERTS, HIDDEN), jnp.float32) * sc, 'up_embed': jax.random.normal(ks[4], (NUM_EXPERTS, HIDDEN), jnp.float32) * sc, 'gate_w': jax.random.normal(ks[5], (HIDDEN, INTER), jnp.float32) * sc, 'up_w': jax.random.normal(ks[6], (HIDDEN, INTER), jnp.float32) * sc, 'down_w': jax.random.normal(ks[7], (INTER, HIDDEN), jnp.float32) * sc}
    _L1_ffn_all = _L1_ffn_setup()
    _L1_ffn_in = {k: v for k, v in _L1_ffn_all.items() if k in ('W_q', 'keys', 'down_embed', 'up_embed', 'gate_w', 'up_w', 'down_w')}
    del _L1_ffn_all
    return {'x': x, 'ctx_2048': ctx_2048, 'mask_BxS2_ik0': mask_BxS2_ik0, 'L0_attn_Wq': _L0_attn_in['Wq'], 'L0_attn_bq': _L0_attn_in['bq'], 'L0_attn_Wk': _L0_attn_in['Wk'], 'L0_attn_bk': _L0_attn_in['bk'], 'L0_attn_Wv': _L0_attn_in['Wv'], 'L0_attn_bv': _L0_attn_in['bv'], 'L0_attn_Wo': _L0_attn_in['Wo'], 'L0_attn_bo': _L0_attn_in['bo'], 'L0_attn_sinks': _L0_attn_in['sinks'], 'L0_xattn_Wq': _L0_xattn_in['Wq'], 'L0_xattn_bq': _L0_xattn_in['bq'], 'L0_xattn_Wk': _L0_xattn_in['Wk'], 'L0_xattn_bk': _L0_xattn_in['bk'], 'L0_xattn_Wv': _L0_xattn_in['Wv'], 'L0_xattn_bv': _L0_xattn_in['bv'], 'L0_xattn_Wo': _L0_xattn_in['Wo'], 'L0_xattn_bo': _L0_xattn_in['bo'], 'L0_xattn_ln_gamma': _L0_xattn_in['ln_gamma'], 'L0_xattn_ln_beta': _L0_xattn_in['ln_beta'], 'L0_xattn_residual_scale': _L0_xattn_in['residual_scale'], 'L0_ffn_router_weight': _L0_ffn_in['router_weight'], 'L0_ffn_gate_up_proj': _L0_ffn_in['gate_up_proj'], 'L0_ffn_down_proj': _L0_ffn_in['down_proj'], 'L0_ffn_sh_gate_w': _L0_ffn_in['sh_gate_w'], 'L0_ffn_sh_up_w': _L0_ffn_in['sh_up_w'], 'L0_ffn_sh_down_w': _L0_ffn_in['sh_down_w'], 'L0_ffn_shared_gate_w': _L0_ffn_in['shared_gate_w'], 'L1_attn_wq': _L1_attn_in['wq'], 'L1_attn_bq': _L1_attn_in['bq'], 'L1_attn_wk': _L1_attn_in['wk'], 'L1_attn_bk': _L1_attn_in['bk'], 'L1_attn_wv': _L1_attn_in['wv'], 'L1_attn_bv': _L1_attn_in['bv'], 'L1_attn_wo': _L1_attn_in['wo'], 'L1_attn_bo': _L1_attn_in['bo'], 'L1_attn_ln_g': _L1_attn_in['ln_g'], 'L1_attn_ln_b': _L1_attn_in['ln_b'], 'L1_xattn_Wh': _L1_xattn_in['Wh'], 'L1_xattn_wg_w': _L1_xattn_in['wg_w'], 'L1_xattn_wo_w': _L1_xattn_in['wo_w'], 'L1_xattn_gn_gamma': _L1_xattn_in['gn_gamma'], 'L1_xattn_gn_beta': _L1_xattn_in['gn_beta'], 'L1_ffn_W_q': _L1_ffn_in['W_q'], 'L1_ffn_keys': _L1_ffn_in['keys'], 'L1_ffn_down_embed': _L1_ffn_in['down_embed'], 'L1_ffn_up_embed': _L1_ffn_in['up_embed'], 'L1_ffn_gate_w': _L1_ffn_in['gate_w'], 'L1_ffn_up_w': _L1_ffn_in['up_w'], 'L1_ffn_down_w': _L1_ffn_in['down_w']}

def reference(x, ctx_2048, mask_BxS2_ik0, L0_attn_Wq, L0_attn_bq, L0_attn_Wk, L0_attn_bk, L0_attn_Wv, L0_attn_bv, L0_attn_Wo, L0_attn_bo, L0_attn_sinks, L0_xattn_Wq, L0_xattn_bq, L0_xattn_Wk, L0_xattn_bk, L0_xattn_Wv, L0_xattn_bv, L0_xattn_Wo, L0_xattn_bo, L0_xattn_ln_gamma, L0_xattn_ln_beta, L0_xattn_residual_scale, L0_ffn_router_weight, L0_ffn_gate_up_proj, L0_ffn_down_proj, L0_ffn_sh_gate_w, L0_ffn_sh_up_w, L0_ffn_sh_down_w, L0_ffn_shared_gate_w, L1_attn_wq, L1_attn_bq, L1_attn_wk, L1_attn_bk, L1_attn_wv, L1_attn_bv, L1_attn_wo, L1_attn_bo, L1_attn_ln_g, L1_attn_ln_b, L1_xattn_Wh, L1_xattn_wg_w, L1_xattn_wo_w, L1_xattn_gn_gamma, L1_xattn_gn_beta, L1_ffn_W_q, L1_ffn_keys, L1_ffn_down_embed, L1_ffn_up_embed, L1_ffn_gate_w, L1_ffn_up_w, L1_ffn_down_w):
    import jax
    import jax.numpy as jnp

    def _L0_attn_ref(hidden_states, Wq, bq, Wk, bk, Wv, bv, Wo, bo, sinks):
        import jax, jax.numpy as jnp
        import numpy as np
        B, S, M = (1, 256, 256)
        H, HKV, D = (32, 8, 64)
        SW = 128
        WAVELENGTH = 150000.0
        SCALE = D ** (-0.25)
        NEG = -1000000000.0

        def _cos_sin(seq_len, dtype):
            half = D // 2
            inv_freq = 1.0 / WAVELENGTH ** (jnp.arange(half, dtype=jnp.float32) * 2.0 / D)
            t = jnp.arange(seq_len, dtype=jnp.float32)
            freqs = t[:, None] * inv_freq[None, :]
            return (jnp.cos(freqs)[None, :, None, :].astype(dtype), jnp.sin(freqs)[None, :, None, :].astype(dtype))

        def _interleaved_rope(x, cos, sin):
            x_even = x[..., ::2]
            x_odd = x[..., 1::2]
            first = x_even * cos - x_odd * sin
            second = x_odd * cos + x_even * sin
            return jnp.stack([first, second], axis=-1).reshape(x.shape)
        b, s, _ = hidden_states.shape
        groups = H // HKV
        q = jnp.einsum('bqm,muh->bquh', hidden_states, Wq) + bq
        k = jnp.einsum('bkm,mvh->bkvh', hidden_states, Wk) + bk
        v = jnp.einsum('bkm,mvh->bkvh', hidden_states, Wv) + bv
        cos, sin = _cos_sin(s, hidden_states.dtype)
        q = _interleaved_rope(q, cos, sin) * SCALE
        k = _interleaved_rope(k, cos, sin) * SCALE
        k = jnp.repeat(k, groups, axis=2)
        v = jnp.repeat(v, groups, axis=2)
        scores = jnp.einsum('bquh,bkuh->buqk', q, k)
        pos = jnp.arange(s)
        sw_mask = jnp.abs(pos[:, None] - pos[None, :]) <= SW
        scores = jnp.where(sw_mask[None, None, :, :], scores, NEG)
        sink_logits = jnp.broadcast_to(sinks[None, :, None, None], (b, H, s, 1))
        combined = jnp.concatenate([scores, sink_logits], axis=-1)
        probs = jax.nn.softmax(combined.astype(jnp.float32), axis=-1)
        attn = probs[..., :-1].astype(hidden_states.dtype)
        out = jnp.einsum('buqk,bkuh->bquh', attn, v)
        return jnp.einsum('bquh,uhm->bqm', out, Wo) + bo

    def _L0_xattn_ref(hidden_states, audio_tokens, attention_mask, Wq, bq, Wk, bk, Wv, bv, Wo, bo, ln_gamma, ln_beta, residual_scale):
        import jax, jax.numpy as jnp
        import numpy as np
        import math
        H = 256
        NH = 16
        HD = H // NH
        EPS_LN = 1e-05
        RES_SCALE_MAX = 0.3

        def _nan_clean(x, lim=10000.0):
            return jnp.nan_to_num(x, nan=0.0, posinf=lim, neginf=-lim)
        B, S, _ = hidden_states.shape
        T = audio_tokens.shape[1]
        hs = _nan_clean(hidden_states).astype(jnp.float32)
        at = _nan_clean(audio_tokens).astype(jnp.float32)

        def proj(x, W, b, L):
            y = x @ W.T + b
            return y.reshape(B, L, NH, HD).transpose(0, 2, 1, 3)
        q = _nan_clean(proj(hs, Wq, bq, S))
        k = _nan_clean(proj(at, Wk, bk, T))
        v = _nan_clean(proj(at, Wv, bv, T))
        scale = max(math.sqrt(HD), 1e-08)
        scores = jnp.einsum('bhsd,bhtd->bhst', q, k) / scale
        scores = jnp.clip(scores, -50.0, 50.0)
        scores = jnp.nan_to_num(scores, nan=0.0, posinf=50.0, neginf=-50.0)
        attend = (attention_mask.astype(jnp.float32) > 0.5)[:, None, None, :]
        scores = jnp.where(attend, scores, -10000.0)
        scores = jnp.clip(scores, -50.0, 50.0)
        probs = jax.nn.softmax(scores, axis=-1)
        probs = jnp.nan_to_num(probs, nan=0.0, posinf=1.0, neginf=0.0)
        probs = probs / (probs.sum(axis=-1, keepdims=True) + 1e-08)
        ctx = jnp.einsum('bhst,bhtd->bhsd', probs, v)
        ctx = ctx.transpose(0, 2, 1, 3).reshape(B, S, H)
        delta = _nan_clean(ctx @ Wo.T + bo)
        rs = jnp.clip(residual_scale, 0.0, RES_SCALE_MAX)
        delta = rs * delta
        mu = delta.mean(axis=-1, keepdims=True)
        var = jnp.mean((delta - mu) ** 2, axis=-1, keepdims=True)
        delta = (delta - mu) / jnp.sqrt(var + EPS_LN) * ln_gamma + ln_beta
        return delta

    def _L0_ffn_ref(hidden_states, router_weight, gate_up_proj, down_proj, sh_gate_w, sh_up_w, sh_down_w, shared_gate_w):
        import jax, jax.numpy as jnp
        import numpy as np
        E = 8
        TOP_K = 2
        H = 256
        I_MOE = 176
        I_SH = 704
        B, S = (2, 256)

        def _moe_forward(hidden_states, router_weight, gate_up_proj, down_proj, sh_gate_w, sh_up_w, sh_down_w, shared_gate_w):
            b, s, h = hidden_states.shape
            x = hidden_states.reshape(-1, h)
            shared = jnp.einsum('ti,hi->th', jax.nn.silu(x @ sh_gate_w.T) * (x @ sh_up_w.T), sh_down_w)
            logits = x @ router_weight.T
            probs = jax.nn.softmax(logits.astype(jnp.float32), axis=-1)
            top_v, top_i = jax.lax.top_k(probs, TOP_K)
            top_v = top_v / top_v.sum(axis=-1, keepdims=True)
            combine = (jax.nn.one_hot(top_i, E, dtype=top_v.dtype) * top_v[..., None]).sum(axis=1)
            out = jnp.zeros_like(x)
            for e in range(E):
                gu = x @ gate_up_proj[e].T
                gate, up = (gu[:, :I_MOE], gu[:, I_MOE:])
                cur = jax.nn.silu(gate) * up @ down_proj[e].T
                out = out + cur * combine[:, e:e + 1]
            out = out + jax.nn.sigmoid(x @ shared_gate_w.T) * shared
            return out.reshape(b, s, h)
        return _moe_forward(hidden_states, router_weight, gate_up_proj, down_proj, sh_gate_w, sh_up_w, sh_down_w, shared_gate_w)

    def _L1_attn_ref(h, wq, bq, wk, bk, wv, bv, wo, bo, ln_g, ln_b):
        import jax, jax.numpy as jnp
        import numpy as np
        D_MODEL = 256
        N_HEADS = 16
        D_K = 128
        EPS = 1e-05
        ROPE_BASE = 10000.0

        def rope(x):
            b, s, h, d = x.shape
            d2 = d // 2
            theta = 1.0 / ROPE_BASE ** (jnp.arange(0, d, 2, dtype=jnp.float32) / d)
            pos = jnp.arange(s, dtype=jnp.float32)
            freqs = pos[:, None] * theta[None, :]
            freqs = jnp.concatenate([freqs, freqs], axis=-1)
            cos = jnp.cos(freqs)[None, :, None, :]
            sin = jnp.sin(freqs)[None, :, None, :]
            x_rot = jnp.concatenate([-x[..., d2:], x[..., :d2]], axis=-1)
            return x * cos + x_rot * sin
        residual = h
        mu = jnp.mean(h, axis=-1, keepdims=True)
        var = jnp.mean(jnp.square(h - mu), axis=-1, keepdims=True)
        x = (h - mu) * jax.lax.rsqrt(var + EPS) * ln_g + ln_b
        b, s, _ = x.shape
        q = (x @ wq.T + bq).reshape(b, s, N_HEADS, D_K)
        k = (x @ wk.T + bk).reshape(b, s, N_HEADS, D_K)
        v = (x @ wv.T + bv).reshape(b, s, N_HEADS, D_K)
        q = rope(q)
        k = rope(k)
        scale = 1.0 / np.sqrt(D_K)
        attn = jnp.einsum('bihd,bjhd->bhij', q, k) * scale
        causal = jnp.triu(jnp.ones((s, s), dtype=bool), k=1)
        attn = jnp.where(causal[None, None], -jnp.inf, attn)
        attn = jax.nn.softmax(attn, axis=-1)
        o = jnp.einsum('bhij,bjhd->bihd', attn, v).reshape(b, s, N_HEADS * D_K)
        return o @ wo.T + bo + residual

    def _L1_xattn_ref(x, k, v, Wh, wg_w, wo_w, gn_gamma, gn_beta):
        import jax, jax.numpy as jnp
        import numpy as np
        B, S, DIM, HD = (4, 128, 256, 128)
        H = DIM // HD
        GN_EPS = 0.001

        def _decay_masks(n_heads, seq_len):
            gam = 1.0 - 2.0 ** (-5.0 - jnp.arange(n_heads, dtype=jnp.float32))
            idx = jnp.arange(seq_len, dtype=jnp.float32)
            expo = idx[None, :] - idx[:, None]
            D = jnp.where(expo[None, :, :] <= 0, gam[:, None, None] ** expo[None, :, :], 0.0)
            return D / jnp.sqrt(D.sum(axis=-1))[:, None, :]
        b, s, dim = x.shape
        h, hd, _ = Wh.shape
        xh = x.reshape(b, s, h, hd)
        kh = k.reshape(b, s, h, hd)
        vh = v.reshape(b, s, h, hd)
        Q = jnp.einsum('bshd,hde->bshe', xh, Wh)
        K = jnp.einsum('bshd,hde->bshe', kh, Wh)
        V = jnp.einsum('bshd,hde->bshe', vh, Wh)
        scores = jnp.einsum('bshe,bthe->bhst', Q, K) / jnp.sqrt(jnp.float32(hd))
        Dn = _decay_masks(h, s)
        masked = scores * Dn[None, :, :, :]
        A = jnp.maximum(jnp.abs(masked.sum(axis=0)), 1.0)
        O = jnp.einsum('hst,bthe->bshe', A, V).reshape(b, s, dim)
        mu = O.mean(axis=-1, keepdims=True)
        var = O.var(axis=-1, keepdims=True)
        Y = (O - mu) / jnp.sqrt(var + GN_EPS) * gn_gamma + gn_beta
        W = jax.nn.relu(x @ wg_w)
        return W * Y @ wo_w

    def _L1_ffn_ref(hidden_states, W_q, keys, down_embed, up_embed, gate_w, up_w, down_w):
        import jax, jax.numpy as jnp
        import numpy as np
        HIDDEN = 256
        INTER = 1024
        RETRIEVAL = 128
        NUM_EXPERTS = 512
        NUM_KEYS = 64
        TOP_K = 8
        B, S = (4, 256)
        b, s, h = hidden_states.shape
        n = b * s
        queries = (hidden_states @ W_q).reshape(2, n, RETRIEVAL // 2)
        routing = jnp.einsum('tnd,tdk->tnk', queries, keys)
        scores2, idx2 = jax.lax.top_k(routing, TOP_K)
        sx, sy = (scores2[0], scores2[1])
        ix, iy = (idx2[0], idx2[1])
        all_scores = (sx[:, :, None] + sy[:, None, :]).reshape(n, TOP_K * TOP_K)
        all_idx = (ix[:, :, None] * NUM_KEYS + iy[:, None, :]).reshape(n, TOP_K * TOP_K)
        scores, pk = jax.lax.top_k(all_scores, TOP_K)
        indices = jnp.take_along_axis(all_idx, pk, axis=-1)
        de = down_embed[indices]
        ue = up_embed[indices]
        x = hidden_states.reshape(n, h)
        ew = jnp.einsum('nh,nkh->nk', x, de)
        ew = jax.nn.silu(ew) * jax.nn.softmax(scores, axis=-1)
        experts_states = jnp.einsum('nk,nkh->nh', ew, ue).reshape(b, s, h)
        mlp = jax.nn.silu(x @ gate_w) * (x @ up_w) @ down_w
        return mlp.reshape(b, s, h) + experts_states
    x = x + _L0_attn_ref(_layernorm(x, axis=-1), L0_attn_Wq, L0_attn_bq, L0_attn_Wk, L0_attn_bk, L0_attn_Wv, L0_attn_bv, L0_attn_Wo, L0_attn_bo, L0_attn_sinks)
    x = x + _L0_xattn_ref(_layernorm(x, axis=-1), ctx_2048, mask_BxS2_ik0, L0_xattn_Wq, L0_xattn_bq, L0_xattn_Wk, L0_xattn_bk, L0_xattn_Wv, L0_xattn_bv, L0_xattn_Wo, L0_xattn_bo, L0_xattn_ln_gamma, L0_xattn_ln_beta, L0_xattn_residual_scale)
    x = x + _L0_ffn_ref(_layernorm(x, axis=-1), L0_ffn_router_weight, L0_ffn_gate_up_proj, L0_ffn_down_proj, L0_ffn_sh_gate_w, L0_ffn_sh_up_w, L0_ffn_sh_down_w, L0_ffn_shared_gate_w)
    x = x + _L1_attn_ref(_layernorm(x, axis=-1), L1_attn_wq, L1_attn_bq, L1_attn_wk, L1_attn_bk, L1_attn_wv, L1_attn_bv, L1_attn_wo, L1_attn_bo, L1_attn_ln_g, L1_attn_ln_b)
    x = x + _L1_xattn_ref(_layernorm(x, axis=-1), ctx_2048, ctx_2048, L1_xattn_Wh, L1_xattn_wg_w, L1_xattn_wo_w, L1_xattn_gn_gamma, L1_xattn_gn_beta)
    x = x + _L1_ffn_ref(_layernorm(x, axis=-1), L1_ffn_W_q, L1_ffn_keys, L1_ffn_down_embed, L1_ffn_up_embed, L1_ffn_gate_w, L1_ffn_up_w, L1_ffn_down_w)
    return x

_drawn_inputs = setup_inputs


def setup_inputs(seed=0):
    import zlib

    import numpy as np

    out = dict(_drawn_inputs(seed))
    spreads = {'L0_attn_bq': (0.0, 0.8),
     'L0_attn_bk': (0.0, 0.8),
     'L0_attn_bv': (0.0, 0.1),
     'L0_attn_bo': (0.0, 0.1),
     'L0_xattn_bq': (0.0, 0.1),
     'L0_xattn_bk': (0.0, 2.0),
     'L0_xattn_bv': (0.0, 0.1),
     'L0_xattn_bo': (0.0, 0.1),
     'L0_xattn_ln_gamma': (1.0, 0.2),
     'L0_xattn_ln_beta': (0.0, 0.1),
     'L1_attn_bq': (0.0, 0.8),
     'L1_attn_bk': (0.0, 2.0),
     'L1_attn_bv': (0.0, 0.529),
     'L1_attn_bo': (0.0, 0.787),
     'L1_attn_ln_g': (1.0, 0.2),
     'L1_attn_ln_b': (0.0, 0.302),
     'L1_xattn_gn_gamma': (1.0, 0.6),
     'L1_xattn_gn_beta': (0.0, 1.038)}
    factors = {'L0_attn_Wq': 8.0,
     'L0_attn_Wk': 8.0,
     'L0_attn_Wv': 3.61,
     'L0_attn_sinks': 8.0,
     'L0_ffn_router_weight': 8.0,
     'L0_ffn_gate_up_proj': 8.0,
     'L0_ffn_down_proj': 8.0,
     'L0_ffn_sh_gate_w': 5.952,
     'L0_ffn_sh_up_w': 5.825,
     'L0_ffn_sh_down_w': 5.806,
     'L0_ffn_shared_gate_w': 8.0,
     'L1_attn_wq': 8.0,
     'L1_attn_wk': 8.0,
     'L1_ffn_W_q': 59.665,
     'L1_ffn_keys': 52.676,
     'L1_ffn_down_embed': 8.0,
     'L1_ffn_up_embed': 8.0,
     'L1_ffn_gate_w': 4.445,
     'L1_ffn_up_w': 4.39,
     'L1_ffn_down_w': 4.369}
    for name, (base, spread) in spreads.items():
        noise = np.random.default_rng([zlib.crc32(name.encode()), seed]).standard_normal(out[name].shape)
        drawn = base * np.exp(spread * noise) if base else spread * noise
        out[name] = jnp.asarray(drawn.astype(out[name].dtype))
    for name, factor in factors.items():
        out[name] = (out[name] * factor).astype(out[name].dtype)
    return out
```

```python
from contextlib import ExitStack

import numpy as np

import concourse.bass as bass
import concourse.mybir as mybir
from concourse.alu_op_type import AluOpType as ALU

F32 = mybir.dt.float32
BF16 = mybir.dt.bfloat16
U32 = mybir.dt.uint32
ACT = mybir.ActivationFunctionType
AX = mybir.AxisListType

P = 128
B, S, D = 4, 256, 256
T = B * S
NT = T // P
KD = D // P
NC = 512
NH2 = T // NC
LN_EPS = 1e-5

A0_G, A0_R, A0_D, A0_WIN = 8, 4, 64, 128
A0_PAIRS = A0_R // 2
A0_NQ = KD * A0_PAIRS * P
A0_NK = KD * P
A0_NV = KD * A0_D
A0_NB = A0_PAIRS + 1 + A0_R + A0_D
A0_W = A0_NQ + A0_NK + A0_NV + A0_NB
A0_U = B * 2 * A0_PAIRS
MASKED = -1.0e9

A1_H = 16
A1_W = 3 * KD * P + 2
A1_U = B


class Kernel:

    def __init__(self, nc, ctx):
        self.nc, self.sems = nc, []
        self.x = self.sb(ctx, "x", [P, NT, D])
        self.xn = self.sb(ctx, "xn", [P, NT, D])
        self.xT = self.sb(ctx, "xT", [P, KD, T])
        self.ident = self.sb(ctx, "ident", [P, P])
        self.stats = self.sb(ctx, "stats", [P, NT, 6])
        self.mv = self.sb(ctx, "mv", [P, NT, 2])
        self.rstd = self.sb(ctx, "rstd", [P, NT])
        self.ve = self.sb(ctx, "ve", [P, NT])
        self.minus_half = self.sb(ctx, "minus_half", [P, NT])

    def sb(self, ctx, name, shape, dt=F32):
        return ctx.enter_context(self.nc.sbuf_tensor("sb_" + name, shape, dt))

    def ps(self, ctx, name, n=NC):
        return ctx.enter_context(self.nc.psum_tensor(name, [P, n], F32))

    def sem(self, name):
        s = self.nc.alloc_semaphore(name=name)
        self.sems.append(s)
        return s

    def clear_semaphores(self):
        self.nc.clear_and_free_semaphores(self.sems)
        self.nc.all_engine_barrier()
        self.sems = []


def spread(column, *dims):
    p = column.shape[0]
    if len(dims) == 1:
        return column.to_broadcast([p, dims[0]])
    return column.rearrange("p (o n) -> p o n", o=1).to_broadcast([p, *dims])


def norm_rows(nc, dve, k, src, dst, done, rstd_ready, turn, out_sem):
    base = turn * 2 * NT
    for t in range(NT):
        nc.vector.bn_stats(k.stats[:, t, :], src[:, t, :]).then_inc(done, 1)
    dve.wait_ge(done, base + NT)
    for t in range(NT):
        nc.vector.bn_aggr(k.mv[:, t, :], k.stats[:, t, :]).then_inc(done, 1)
    dve.wait_ge(rstd_ready, 3 * turn + 3)
    for t in range(NT):
        nc.vector.tensor_scalar(dst[:, t, :], src[:, t, :], k.mv[:, t, 0:1], k.rstd[:, t:t + 1],
                                ALU.subtract, ALU.mult).then_inc(out_sem, 1)


def inverse_root(nc, pool, k, done, rstd_ready, turn, eps=LN_EPS):
    pool.wait_ge(done, (turn + 1) * 2 * NT)
    nc.gpsimd.tensor_scalar(k.ve[:, :], k.mv[:, :, 1], eps, None, ALU.add).then_inc(rstd_ready, 1)
    pool.wait_ge(rstd_ready, 3 * turn + 1)
    nc.gpsimd.memset(k.minus_half[:, :], -0.5).then_inc(rstd_ready, 1)
    pool.wait_ge(rstd_ready, 3 * turn + 2)
    nc.gpsimd.tensor_tensor(k.rstd[:, :], k.ve[:, :], k.minus_half[:, :], ALU.pow).then_inc(rstd_ready, 1)


def turn_rows(nc, pe, k, banks, xn_ready, base, turned):
    per = NC // P
    for h in range(NH2):
        for t in range(per):
            pe.wait_ge(xn_ready, base + h * per + t + 1)
            for d in range(KD):
                last = nc.tensor.transpose(banks[d * NH2 + h][:, t * P:(t + 1) * P],
                                           k.xn[:, h * per + t, d * P:(d + 1) * P], k.ident[:, :])
        last.then_inc(turned, 1)


def attention_0(nc, k, src, out_x):
    with ExitStack() as ctx:
        sb = lambda name, shape, dt=F32: k.sb(ctx, "a0_" + name, shape, dt)
        w = [sb(f"w{i}", [P, A0_W]) for i in range(2)]
        wo = [sb(f"wo{i}", [P, KD, D]) for i in range(2)]
        cosq = sb("cosq", [P, S])
        sinq = sb("sinq", [P, S])
        wmask = sb("wmask", [P, 2, S])
        slotm = sb("slotm", [P, 2])
        bo = sb("bo", [P, D])
        qT = [[sb(f"qT{i}{j}", [P, T]) for j in range(A0_PAIRS)] for i in range(2)]
        kz = [sb(f"kz{i}", [P, B, 2, S]) for i in range(2)]
        kr = sb("kr", [P, 2, S])
        v = [sb(f"v{i}", [P, NT, A0_D + 1]) for i in range(2)]
        t1 = [sb(f"t1{i}", [P, 2, S]) for i in range(2)]
        t2 = [sb(f"t2{i}", [P, 2, S]) for i in range(2)]
        nsink = [sb(f"nsink{i}", [P, A0_R]) for i in range(2)]
        nS = [sb(f"nS{i}", [P, 2, S]) for i in range(2)]
        nm = [sb(f"nm{i}", [P, A0_R]) for i in range(4)]
        Pm = [sb(f"Pm{i}", [P, 2, S]) for i in range(4)]
        PT = [sb(f"PT{i}", [P, 2, 2, P]) for i in range(2)]
        ds = sb("ds", [P, 2, A0_R])
        es = [sb(f"es{i}", [P, A0_R]) for i in range(4)]
        den = sb("den", [P, 2, A0_R])
        O = [sb(f"O{i}", [P, A0_R, A0_D]) for i in range(2)]
        OT = [sb(f"OT{i}", [P, 2, P]) for i in range(2)]
        pp = k.ps(ctx, "a0_pp")
        pS = [k.ps(ctx, f"a0_pS{i}") for i in range(2)]
        pT = k.ps(ctx, "a0_pT")
        pO = [k.ps(ctx, f"a0_pO{i}") for i in range(2)]
        pOT = k.ps(ctx, "a0_pOT")
        pY = k.ps(ctx, "a0_pY")
        turn_banks = [pS[0], pS[1], pT, pOT]

        sem = lambda name: k.sem("a0_" + name)
        loaded, w_in, wo_in = sem("loaded"), [sem("w_in0"), sem("w_in1")], [sem("wo_in0"), sem("wo_in1")]
        ln, xn_ready, turned, xT_ready = sem("ln"), sem("xn_ready"), sem("turned"), sem("xT_ready")
        proj, proj_used, roped, chunk = sem("proj"), sem("proj_used"), sem("roped"), sem("chunk")
        kr_done, v_ready, ns_ready = sem("kr_done"), sem("v_ready"), sem("ns_ready")
        scored, maxed, probs, turnedP, PT_ready = (sem("scored"), sem("maxed"), sem("probs"),
                                                   sem("turnedP"), sem("PT_ready"))
        pvd, shifted, es_ready, den_ready, O_ready = (sem("pvd"), sem("shifted"), sem("es_ready"),
                                                      sem("den_ready"), sem("O_ready"))
        turnedO, OT_ready, projected, added = sem("turnedO"), sem("OT_ready"), sem("projected"), sem("added")
        bo_in, ones_set, rstd_ready, gate = sem("bo_in"), sem("ones_set"), sem("rstd_ready"), sem("gate")

        NCH = 7
        CH_AT = {0: 0, 2: 1, 4: 2, 6: 3, 8: 4, 10: 5, 12: 6}

        def groups(eng, first, step, last):
            first()
            with eng.Fori(0, (A0_G - 2) // 2) as i:
                for s in range(2):
                    step(i * 2 + (1 + s), (1 + s) % 2)
            last()

        def halves(G, par):
            if isinstance(G, int):
                return 16 * (G // 2 + 1)
            return G * 8 + (16 - 8 * par)

        block = ctx.enter_context(nc.Block())

        @block.sync
        def _(sp):
            xr = src["x"].rearrange("(t p) d -> p t d", p=P)
            for t in range(NT):
                sp.dma_start(k.x[:, t, :], xr[:, t, :]).then_inc(k.x_in, 16)
            sp.dma_start(k.ident[:, :], src["ident"]).then_inc(loaded, 16)
            sp.dma_start(cosq[:, :], src["a0_cos"]).then_inc(loaded, 16)
            sp.dma_start(sinq[:, :], src["a0_sin"]).then_inc(loaded, 16)
            sp.dma_start(wmask[:, :, :], src["a0_mask"]).then_inc(loaded, 16)
            sp.dma_start(slotm[:, :], src["a0_slot"]).then_inc(loaded, 16)
            sp.dma_start(bo[:, :], src["a0_bo"]).then_inc(loaded, 16)
            sp.dma_start(w[0][:, :], src["a0_w"][0]).then_inc(w_in[0], 16)
            sp.dma_start(wo[0][:, :, :], src["a0_wo"][0]).then_inc(wo_in[0], 16)
            sp.dma_start(w[1][:, :], src["a0_w"][1]).then_inc(w_in[1], 16)
            sp.dma_start(wo[1][:, :, :], src["a0_wo"][1]).then_inc(wo_in[1], 16)
            with sp.Fori(0, (A0_G - 2) // 2) as i:
                for s in range(2):
                    g = i * 2 + (2 + s)
                    sp.wait_ge(chunk, (g - 1) * NCH)
                    sp.dma_start(w[s][:, :], src["a0_w"][bass.ds(g, 1)].rearrange("g p n -> p (g n)"))\
                        .then_inc(w_in[s], 16)
                    sp.wait_ge(added, (g - 1) * NT)
                    sp.dma_start(wo[s][:, :, :], src["a0_wo"][bass.ds(g, 1)].rearrange("g p c n -> p (g c) n"))\
                        .then_inc(wo_in[s], 16)

        @block.gpsimd
        def _(pool):
            for i in range(2):
                nc.gpsimd.memset(v[i][:, :, A0_D:A0_D + 1], 1.0).then_inc(ones_set, 1)
            inverse_root(nc, pool, k, ln, rstd_ready, 0)

            def project(G, par, c):
                pool.wait_ge(roped, G * 6 + c + 1)
                if c < 4:
                    half = c % 2
                    nc.gpsimd.tensor_tensor(qT[par][c // 2][:, half * NC:(half + 1) * NC],
                                            t1[c % 2][:, :, :].rearrange("p b s -> p (b s)"),
                                            t2[c % 2][:, :, :].rearrange("p b s -> p (b s)"),
                                            ALU.add).then_inc(chunk, 1)
                else:
                    half = c - 4
                    pool.wait_ge(chunk, G * NCH + c)
                    nc.gpsimd.tensor_tensor(kr[:, :, :], t1[c % 2][:, :, :], t2[c % 2][:, :, :],
                                            ALU.add).then_inc(kr_done, 1)
                    pool.wait_ge(loaded, 96)
                    pool.wait_ge(kr_done, G * 2 + half + 1)
                    for slot in range(2):
                        out = nc.gpsimd.tensor_tensor(kz[par][:, 2 * half:2 * half + 2, slot, :], kr[:, :, :],
                                                      spread(slotm[:, slot:slot + 1], 2, S), ALU.mult)
                    out.then_inc(chunk, 1)

            def next_chunks(G, par):
                for c in range(6):
                    project(G, par, c)
                pool.wait_ge(v_ready, G + 1)
                nc.gpsimd.sem_inc(chunk, 1)

            next_chunks(0, 0)
            next_chunks(1, 1)
            with pool.Fori(0, (A0_G - 2) // 2) as i:
                for s in range(2):
                    next_chunks(i * 2 + (2 + s), s)

        @block.scalar
        def _(act):
            for j in range(4):
                act.wait_ge(turned, (j % NH2) + 1)
                nc.scalar.copy(k.xT[:, j // NH2, (j % NH2) * NC:(j % NH2 + 1) * NC],
                               turn_banks[j][:, :]).then_inc(xT_ready, 1)

            def exps(G, par, u):
                U = G * A0_U + u
                act.wait_ge(maxed, U + 1)
                if not (isinstance(G, int) and G == 0 and u < 4):
                    act.wait_ge(turnedP, U - 3)
                for h in range(2):
                    out = nc.scalar.activation(Pm[u % 4][:, h, :], nS[u % 2][:, h, :], ACT.Exp,
                                               bias=nm[(u // 2) % 4][:, 2 * (u % 2) + h:2 * (u % 2) + h + 1],
                                               scale=-1.0)
                out.then_inc(probs, 1)

            def evac_PT(G, u):
                U = G * A0_U + u
                act.wait_ge(turnedP, U + 1)
                nc.scalar.copy(PT[u % 2][:, :, :, :].rearrange("p h c q -> p (h c q)"), pT[:, :])\
                    .then_inc(PT_ready, 1)

            def sink_exps(G, j):
                act.wait_ge(shifted, G * NT + j + 1)
                nc.scalar.activation(es[j % 4][:, :], ds[:, j % 2, :], ACT.Exp).then_inc(es_ready, 1)

            def evac_OT(G, j):
                act.wait_ge(turnedO, G * NT + j + 1)
                nc.scalar.copy(OT[j % 2][:, :, :].rearrange("p c q -> p (c q)"), pOT[:, 0:2 * P])\
                    .then_inc(OT_ready, 1)

            def body(G, par, first=False):
                for u in range(A0_U):
                    exps(G, par, u)
                    lag(G, u, first)

            def lag(G, u, first):
                v2, g2 = (u - 2) % A0_U, G if u >= 2 else G - 1
                if u >= 2 or not first:
                    evac_PT(g2, v2)
                if u % 2 == 1:
                    sink_exps(G, u // 2)
                if u % 2 == 0 and (u >= 6 or not first):
                    evac_OT(G if u >= 6 else G - 1, (u // 2 - 3) % NT)

            groups(act, lambda: body(0, 0, True), body, lambda: body(A0_G - 1, 1))
            for u in range(A0_U, A0_U + 6):
                if u < A0_U + 2:
                    evac_PT(A0_G - 1, u - 2)
                if u % 2 == 0:
                    evac_OT(A0_G - 1, u // 2 - 3)

        @block.vector
        def _(dve):
            dve.wait_ge(k.x_in, 16 * NT)
            norm_rows(nc, dve, k, k.x, k.xn, ln, rstd_ready, 0, xn_ready)
            dve.wait_ge(loaded, 96)
            dve.wait_ge(xn_ready, NT)
            for t in range(NT):
                nc.vector.tensor_tensor(k.x[:, t, :], k.x[:, t, :], bo[:, :], ALU.add).then_inc(bo_in, 1)
            dve.wait_ge(bo_in, NT)

            def rope(G, par, c):
                n = c % 2
                bias = w[par][:, A0_W - A0_NB + c // 2:A0_W - A0_NB + c // 2 + 1]
                dve.wait_ge(w_in[par], halves(G, par))
                dve.wait_ge(proj, G * NCH + c + 1)
                if not (isinstance(G, int) and G == 0 and c < 2):
                    dve.wait_ge(chunk, (G * NCH + c - 1) if c >= 2 else (G * NCH - 2 + c))
                a = pp[:, :].rearrange("p (b s) -> p b s", b=2)
                lo, hi = slice(0, 64), slice(64, 128)
                cs = lambda tab, rows: tab[rows, :].rearrange("p (o s) -> p o s", o=1).to_broadcast([rows.stop - rows.start, 2, S])
                nc.vector.scalar_tensor_tensor(out=t1[n][:, :, :], in0=a, scalar=bias,
                                               in1=cs(cosq, slice(0, 128)), op0=ALU.add, op1=ALU.mult)
                nc.vector.scalar_tensor_tensor(out=t2[n][lo, :, :], in0=a[hi], scalar=bias[hi],
                                               in1=cs(sinq, hi), op0=ALU.add, op1=ALU.mult)
                nc.vector.scalar_tensor_tensor(out=t2[n][hi, :, :], in0=a[lo], scalar=bias[lo],
                                               in1=cs(sinq, lo), op0=ALU.add, op1=ALU.mult).then_inc(roped, 1)

            def values(G, par):
                dve.wait_ge(proj, G * NCH + NCH)
                if isinstance(G, int) and G < 2:
                    dve.wait_ge(ones_set, 2)
                bv = w[par][:, A0_W - A0_D:A0_W].rearrange("p (o n) -> p o n", o=1).to_broadcast([P, NT, A0_D])
                sink = A0_W - A0_NB + A0_PAIRS + 1
                nc.vector.tensor_scalar(nsink[par][:, :], w[par][:, sink:sink + A0_R], -1.0, None,
                                        ALU.mult).then_inc(ns_ready, 1)
                nc.vector.tensor_tensor(v[par][:, :, 0:A0_D], pp[:, :].rearrange("p (t n) -> p t n", t=NT), bv,
                                        ALU.add).then_inc(v_ready, 1)

            def chunk_of(G, par, c):
                rope(G, par, c) if c < 6 else values(G, par)

            def maxima(G, par, u):
                U, j = G * A0_U + u, u // 2
                dve.wait_ge(loaded, 96)
                dve.wait_ge(scored, U + 1)
                if u == 0:
                    dve.wait_ge(ns_ready, G + 1)
                if not (isinstance(G, int) and G == 0 and u < 2):
                    dve.wait_ge(probs, U - 1)
                dve.sem_inc(gate, 1)
                for h in range(2):
                    c = 2 * (u % 2) + h
                    out = nc.vector.tensor_tensor_reduce(
                        nS[u % 2][:, h, :], pS[u % 2][:, h * S:(h + 1) * S], wmask[:, j % 2, :], -1.0,
                        nsink[par][:, c:c + 1], ALU.add, ALU.min, nm[j % 4][:, c:c + 1])
                out.then_inc(maxed, 1)

            def shift(G, par, j):
                dve.wait_ge(maxed, G * A0_U + 2 * j + 2)
                if not (isinstance(G, int) and G == 0 and j < 2):
                    dve.wait_ge(es_ready, G * NT + j - 1)
                nc.vector.tensor_tensor(ds[:, j % 2, :], nm[j % 4][:, :], nsink[par][:, :], ALU.subtract)\
                    .then_inc(shifted, 1)

            def outputs(G, j):
                dve.wait_ge(pvd, G * A0_U + 2 * j + 2)
                dve.wait_ge(es_ready, G * NT + j + 1)
                o = pO[j % 2][:, 0:A0_R * (A0_D + 1)].rearrange("p (h n) -> p h n", h=A0_R)
                nc.vector.tensor_tensor(den[:, 0, :], o[:, :, A0_D], es[j % 4][:, :], ALU.add).then_inc(den_ready, 1)
                dve.wait_ge(den_ready, (G * NT + j) * 2 + 1)
                nc.vector.reciprocal(den[:, 1, :], den[:, 0, :]).then_inc(den_ready, 1)
                dve.wait_ge(den_ready, (G * NT + j) * 2 + 2)
                if not (isinstance(G, int) and G == 0 and j < 2):
                    dve.wait_ge(turnedO, G * NT + j - 1)
                nc.vector.tensor_tensor(O[j % 2][:, :, :], o[:, :, 0:A0_D],
                                        den[:, 1, :].rearrange("p (h o) -> p h o", o=1).to_broadcast([P, A0_R, A0_D]),
                                        ALU.mult).then_inc(O_ready, 1)

            def add_y(G, j):
                dve.wait_ge(projected, G * NT + j + 1)
                if not (isinstance(G, int) and G == 0):
                    dve.wait_ge(added, G * NT + j)
                nc.vector.tensor_tensor(k.x[:, j, :], pY[:, 0:D], k.x[:, j, :], ALU.add).then_inc(added, 1)

            def body(G, par, first=False, last=False):
                for u in range(A0_U):
                    maxima(G, par, u)
                    if u % 2 == 1:
                        shift(G, par, u // 2)
                    if u % 2 == 0 and (u >= 4 or not first):
                        outputs(G if u >= 4 else G - 1, (u // 2 - 2) % NT)
                    if u % 2 == 1 and (u >= 7 or not first):
                        add_y(G if u >= 7 else G - 1, ((u - 1) // 2 - 3) % NT)
                    if u in CH_AT and not last:
                        chunk_of(G + 1, 1 - par, CH_AT[u])

            for c in range(NCH):
                chunk_of(0, 0, c)
            groups(dve, lambda: body(0, 0, True), body, lambda: body(A0_G - 1, 1, last=True))
            for u in range(A0_U, A0_U + 8):
                if u % 2 == 0 and u // 2 - 2 < NT:
                    outputs(A0_G - 1, u // 2 - 2)
                if u % 2 == 1 and (u - 1) // 2 - 3 < NT:
                    add_y(A0_G - 1, (u - 1) // 2 - 3)
            dve.wait_ge(added, A0_G * NT)

        @block.tensor
        def _(pe):
            pe.wait_ge(loaded, 96)
            turn_rows(nc, pe, k, turn_banks, xn_ready, 0, turned)
            pe.wait_ge(xT_ready, 4)

            def chunk_of(G, par, c):
                if c == 0:
                    pe.wait_ge(w_in[par], halves(G, par))
                if not (isinstance(G, int) and G == 0 and c == 0):
                    if c == 0:
                        pe.wait_ge(v_ready, G)
                    else:
                        pe.wait_ge(roped, G * 6 + c)
                if c < 6:
                    col = (c // 2) * P if c < 4 else 0
                    half = c % 2
                    for d in range(KD):
                        off = (d * A0_PAIRS * P + col) if c < 4 else (A0_NQ + d * P)
                        out = nc.tensor.matmul(pp[:, :], w[par][:, off:off + P],
                                               k.xT[:, d, half * NC:(half + 1) * NC],
                                               start=(d == 0), stop=(d == KD - 1))
                else:
                    for t in range(NT):
                        for d in range(KD):
                            off = A0_NQ + A0_NK + d * A0_D
                            out = nc.tensor.matmul(pp[:, t * A0_D:(t + 1) * A0_D], k.xT[:, d, t * P:(t + 1) * P],
                                                   w[par][:, off:off + A0_D], start=(d == 0), stop=(d == KD - 1))
                out.then_inc(proj, 1)

            def scores(G, par, u):
                U, b, qt, pair = G * A0_U + u, u // 4, (u // 2) % 2, u % 2
                if u == 0:
                    pe.wait_ge(chunk, (G + 1) * NCH)
                if not (isinstance(G, int) and G == 0 and u < 2):
                    pe.wait_ge(maxed, U - 1)
                c = b * S + qt * P
                nc.tensor.matmul(pS[u % 2][:, :], qT[par][pair][:, c:c + P],
                                 kz[par][:, b, :, :].rearrange("p h s -> p (h s)"),
                                 start=True, stop=True).then_inc(scored, 1)

            def turn_P(G, u):
                U = G * A0_U + u
                pe.wait_ge(probs, U + 1)
                if not (isinstance(G, int) and G == 0 and u < 1):
                    pe.wait_ge(PT_ready, U)
                for h in range(2):
                    for c in range(2):
                        out = nc.tensor.transpose(pT[:, (2 * h + c) * P:(2 * h + c + 1) * P],
                                                  Pm[u % 4][:, h, c * P:(c + 1) * P], k.ident[:, :])
                out.then_inc(turnedP, 1)

            def weigh(G, par, u):
                U, b, j, pair = G * A0_U + u, u // 4, u // 2, u % 2
                pe.wait_ge(PT_ready, U + 1)
                if pair == 0 and not (isinstance(G, int) and G == 0 and j < 2):
                    pe.wait_ge(O_ready, G * NT + j - 1)
                for h in range(2):
                    c0 = (2 * pair + h) * (A0_D + 1)
                    for c in range(2):
                        out = nc.tensor.matmul(pO[j % 2][:, c0:c0 + A0_D + 1], PT[u % 2][:, h, c, :],
                                               v[par][:, 2 * b + c, :], start=(c == 0), stop=(c == 1))
                out.then_inc(pvd, 1)

            def turn_O(G, j):
                pe.wait_ge(O_ready, G * NT + j + 1)
                if not (isinstance(G, int) and G == 0 and j < 1):
                    pe.wait_ge(OT_ready, G * NT + j)
                for c in range(2):
                    out = nc.tensor.transpose(pOT[:, c * P:(c + 1) * P],
                                              O[j % 2][:, 2 * c:2 * c + 2, :].rearrange("p h n -> p (h n)"),
                                              k.ident[:, :])
                out.then_inc(turnedO, 1)

            def project_out(G, par, j):
                if j == 0:
                    pe.wait_ge(wo_in[par], halves(G, par))
                pe.wait_ge(OT_ready, G * NT + j + 1)
                if not (isinstance(G, int) and G == 0 and j < 1):
                    pe.wait_ge(added, G * NT + j)
                for c in range(2):
                    out = nc.tensor.matmul(pY[:, 0:D], OT[j % 2][:, c, :], wo[par][:, c, :],
                                           start=(c == 0), stop=(c == 1))
                out.then_inc(projected, 1)

            def lag(G, par, u, first=False):
                if u >= 2 or not first:
                    turn_P(G if u >= 2 else G - 1, (u - 2) % A0_U)
                if u >= 3 or not first:
                    weigh(G if u >= 3 else G - 1, par if u >= 3 else 1 - par, (u - 3) % A0_U)
                if u % 2 == 0 and (u >= 6 or not first):
                    turn_O(G if u >= 6 else G - 1, (u // 2 - 3) % NT)
                if u % 2 == 1 and (u >= 7 or not first):
                    project_out(G if u >= 7 else G - 1, par if u >= 7 else 1 - par, ((u - 1) // 2 - 3) % NT)

            def body(G, par, first=False, last=False):
                for u in range(A0_U):
                    scores(G, par, u)
                    if u in CH_AT and not last:
                        chunk_of(G + 1, 1 - par, CH_AT[u])
                    lag(G, par, u, first)

            for c in range(NCH):
                chunk_of(0, 0, c)
            groups(pe, lambda: body(0, 0, True), body, lambda: body(A0_G - 1, 1, last=True))
            for u in range(A0_U, A0_U + 8):
                if u < A0_U + 2:
                    turn_P(A0_G - 1, u - 2)
                if u < A0_U + 3:
                    weigh(A0_G - 1, 1, u - 3)
                if u % 2 == 0 and u < A0_U + 6:
                    turn_O(A0_G - 1, u // 2 - 3)
                if u % 2 == 1 and u < A0_U + 7:
                    project_out(A0_G - 1, 1, (u - 1) // 2 - 3)


def norm_and_turn(nc, k, ctx, tag, banks, eps=LN_EPS, src=None):
    sem = lambda name: k.sem(f"{tag}_{name}")
    ln, rstd_ready, xn_ready, turned, xT_ready = (sem("ln"), sem("rstd_ready"), sem("xn_ready"),
                                                  sem("turned"), sem("xT_ready"))

    def on_vector(dve):
        norm_rows(nc, dve, k, k.x, k.xn, ln, rstd_ready, 0, xn_ready)

    def on_gpsimd(pool):
        inverse_root(nc, pool, k, ln, rstd_ready, 0, eps)

    def on_tensor(pe):
        turn_rows(nc, pe, k, banks, xn_ready, 0, turned)
        pe.wait_ge(xT_ready, 4)

    def on_scalar(act):
        for j in range(4):
            act.wait_ge(turned, (j % NH2) + 1)
            nc.scalar.copy(k.xT[:, j // NH2, (j % NH2) * NC:(j % NH2 + 1) * NC],
                           banks[j][:, :]).then_inc(xT_ready, 1)

    return on_vector, on_gpsimd, on_tensor, on_scalar, (ln, rstd_ready, xn_ready, xT_ready)


X0_H, X0_D = 16, 16
X0_HM = P // X0_D
X0_U = 2 * X0_H // 2
X0_CLIP = 50.0


def cross_attention_0(nc, k, src):
    with ExitStack() as ctx:
        sb = lambda name, shape, dt=F32: k.sb(ctx, "x0_" + name, shape, dt)
        w = sb("w", [P, 4, KD, D])
        cT = sb("cT", [P, KD, T])
        cols = sb("cols", [P, 4])
        rows = sb("rows", [P, 4, D])
        hmask = sb("hmask", [P, X0_HM])
        rs = sb("rs", [P, 1])
        mask = sb("mask", [P, NT], mybir.dt.int32)
        keep = sb("keep", [P, NT])
        drop = sb("drop", [P, NT])
        qT = sb("qT", [P, KD, S])
        qz = [sb(f"qz{i}", [P, X0_H, S]) for i in range(2)]
        kT = [sb(f"kT{i}", [P, KD, S]) for i in range(2)]
        v = [sb(f"v{i}", [P, 2, X0_H, X0_D + 1]) for i in range(2)]
        clipped = [sb(f"clipped{i}", [P, 2, S]) for i in range(2)]
        PT = [sb(f"PT{i}", [P, 2, S]) for i in range(6)]
        rec = sb("rec", [P, 2, X0_H])
        O = [sb(f"O{i}", [P, X0_H, X0_D]) for i in range(2)]
        OT = [sb(f"OT{i}", [P, KD, P]) for i in range(2)]
        delta = sb("delta", [P, NT, D])
        pp = k.ps(ctx, "x0_pp")
        pS = [k.ps(ctx, f"x0_pS{i}") for i in range(2)]
        pO = [k.ps(ctx, f"x0_pO{i}") for i in range(2)]
        pOT = k.ps(ctx, "x0_pOT")
        pY = [k.ps(ctx, f"x0_pY{i}") for i in range(2)]

        sem = lambda name: k.sem("x0_" + name)
        on_vector, on_gpsimd, on_tensor, on_scalar, (ln, rstd_ready, xn_ready, xT_ready) = \
            norm_and_turn(nc, k, ctx, "x0", [pS[0], pS[1], pO[0], pO[1]])
        loaded, consts = sem("loaded"), sem("consts")
        proj, qk_out, v_out, qz_ready = sem("proj"), sem("qk_out"), sem("v_out"), sem("qz_ready")
        scored, clip_done, probs, weighed = sem("scored"), sem("clip_done"), sem("probs"), sem("weighed")
        rec_ready, O_ready, turnedO, OT_ready = sem("rec_ready"), sem("O_ready"), sem("turnedO"), sem("OT_ready")
        projected, shaped, scaled, dn, summed = (sem("projected"), sem("shaped"), sem("scaled"), sem("dn"),
                                                 sem("summed"))
        LOADS = 8
        block = ctx.enter_context(nc.Block())

        @block.sync
        def _(sp):
            for dst, name in ((w, "x0_w"), (cT, "ctxT"), (rows, "x0_rows"), (cols, "x0_cols"),
                              (hmask, "x0_hmask"), (rs, "x0_rs"), (mask, "x0_mask")):
                sp.dma_start(dst[tuple([slice(None)] * len(dst.shape))], src[name]).then_inc(loaded, 16)
            if not k.ident_loaded:
                sp.dma_start(k.ident[:, :], src["ident"])  .then_inc(loaded, 16)
            else:
                sp.sem_inc(loaded, 16)

        @block.gpsimd
        def _(pool):
            for i in range(2):
                nc.gpsimd.memset(v[i][:, :, :, X0_D:X0_D + 1], 1.0).then_inc(consts, 1)
            on_gpsimd(pool)
            pool.wait_ge(loaded, 16 * LOADS)
            for b in range(B):
                pool.wait_ge(qk_out, 4 * b + 2)
                if b >= 2:
                    pool.wait_ge(scored, X0_U * (b - 1))
                for m in range(KD):
                    nc.gpsimd.tensor_tensor(
                        qz[b % 2][:, m * X0_HM:(m + 1) * X0_HM, :],
                        qT[:, m:m + 1, :].to_broadcast([P, X0_HM, S]),
                        hmask[:, :].rearrange("p (h o) -> p h o", o=1).to_broadcast([P, X0_HM, S]),
                        ALU.mult).then_inc(qz_ready, 1)
            inverse_root(nc, pool, k, ln, rstd_ready, 1)

        @block.scalar
        def _(act):
            on_scalar(act)
            act.wait_ge(loaded, 16 * LOADS)

            def queries_out(b):
                act.wait_ge(proj, 3 * b + 1)
                if b >= 1:
                    act.wait_ge(qz_ready, 2 * b)
                for m in range(KD):
                    nc.scalar.activation(qT[:, m, :], pp[:, m * S:(m + 1) * S], ACT.Identity,
                                         bias=cols[:, m:m + 1]).then_inc(qk_out, 1)

            def keys_out(b):
                act.wait_ge(proj, 3 * b + 2)
                for m in range(KD):
                    nc.scalar.activation(kT[b % 2][:, m, :], pp[:, m * S:(m + 1) * S], ACT.Identity,
                                         bias=cols[:, 2 + m:3 + m]).then_inc(qk_out, 1)

            queries_out(0)
            keys_out(0)
            for U in range(B * X0_U + 10):
                b, u = U // X0_U, U % X0_U
                if U < B * X0_U:
                    kt = u % 2
                    act.wait_ge(clip_done, U + 1)
                    if U == 0:
                        act.wait_ge(consts, 5)
                    if U >= 6:
                        act.wait_ge(weighed, (U - 6) // 2 + 1)
                    nc.scalar.activation(PT[U % 6][:, :, :], clipped[U % 2][:, :, :], ACT.Exp,
                                         scale=keep[:, 2 * b + kt:2 * b + kt + 1],
                                         bias=drop[:, 2 * b + kt:2 * b + kt + 1]).then_inc(probs, 1)
                    if u == 4 and b + 1 < B:
                        queries_out(b + 1)
                    if u == 6 and b + 1 < B:
                        keys_out(b + 1)
                for qt in range(2):
                    r = U - X0_U - 8 - qt
                    if r >= 0 and r % X0_U == 0:
                        j = 2 * (r // X0_U) + qt
                        act.wait_ge(turnedO, j + 1)
                        nc.scalar.copy(OT[qt][:, :, :].rearrange("p c q -> p (c q)"), pOT[:, 0:2 * P])\
                            .then_inc(OT_ready, 1)

        @block.vector
        def _(dve):
            on_vector(dve)
            dve.wait_ge(loaded, 16 * LOADS)
            nc.vector.tensor_scalar(rs[:, :], rs[:, :], 0.0, 0.3, ALU.max, ALU.min).then_inc(consts, 1)
            nc.vector.tensor_scalar(keep[:, :], mask[:, :], 0.5, None, ALU.is_gt).then_inc(consts, 1)
            dve.wait_ge(consts, 4)
            nc.vector.tensor_scalar(drop[:, :], keep[:, :], 1.0, X0_CLIP, ALU.subtract, ALU.mult).then_inc(consts, 1)
            dve.wait_ge(xn_ready, NT)
            for t in range(NT):
                nc.vector.tensor_tensor(k.x[:, t, :], k.x[:, t, :], rows[:, 3, :], ALU.add).then_inc(shaped, 1)

            def values_out(b):
                dve.wait_ge(proj, 3 * b + 3)
                if b >= 2:
                    dve.wait_ge(weighed, X0_H // 2 * (b - 1))
                bv = rows[:, 0, :].rearrange("p (h n) -> p h n", h=X0_H)
                for kt in range(2):
                    out = nc.vector.tensor_tensor(v[b % 2][:, kt, :, 0:X0_D],
                                                  pp[:, kt * D:(kt + 1) * D].rearrange("p (h n) -> p h n", h=X0_H),
                                                  bv, ALU.add)
                out.then_inc(v_out, 1)

            def normalise(b, qt):
                j = 2 * b + qt
                dve.wait_ge(weighed, X0_H // 2 * (b + 1))
                o = pO[qt][:, 0:X0_H * (X0_D + 1)].rearrange("p (h n) -> p h n", h=X0_H)
                nc.vector.reciprocal(rec[:, qt, :], o[:, :, X0_D]).then_inc(rec_ready, 1)
                dve.wait_ge(rec_ready, j + 1)
                if b >= 1:
                    dve.wait_ge(turnedO, j - 1)
                nc.vector.tensor_tensor(O[qt][:, :, :], o[:, :, 0:X0_D],
                                        rec[:, qt, :].rearrange("p (h o) -> p h o", o=1).to_broadcast([P, X0_H, X0_D]),
                                        ALU.mult).then_inc(O_ready, 1)

            def scale_delta(b, qt):
                j = 2 * b + qt
                dve.wait_ge(projected, j + 1)
                nc.vector.tensor_tensor(delta[:, j, :], pY[qt][:, 0:D], rows[:, 1, :],
                                        ALU.add).then_inc(scaled, 1)
                dve.wait_ge(scaled, 2 * j + 1)
                nc.vector.tensor_scalar(delta[:, j, :], delta[:, j, :], rs[:, 0:1], None, ALU.mult)\
                    .then_inc(scaled, 1)

            values_out(0)
            for U in range(B * X0_U + 12):
                b, u = U // X0_U, U % X0_U
                if U < B * X0_U:
                    dve.wait_ge(scored, U + 1)
                    if U >= 2:
                        dve.wait_ge(probs, U - 1)
                    nc.vector.tensor_scalar(clipped[U % 2][:, :, :].rearrange("p h s -> p (h s)"), pS[U % 2][:, :],
                                            X0_CLIP, -X0_CLIP, ALU.min, ALU.max).then_inc(clip_done, 1)
                    if u == 8 and b + 1 < B:
                        values_out(b + 1)
                for qt in range(2):
                    r = U - X0_U - 3
                    if r >= 0 and r % X0_U == 0:
                        normalise(r // X0_U, qt)
                    r = U - X0_U - 10 - qt
                    if r >= 0 and r % X0_U == 0:
                        scale_delta(r // X0_U, qt)
            dve.wait_ge(scaled, 2 * NT)
            norm_rows(nc, dve, k, delta, k.xn, ln, rstd_ready, 1, dn)
            dve.wait_ge(dn, NT)
            for t in range(NT):
                nc.vector.tensor_tensor(k.xn[:, t, :], k.xn[:, t, :], rows[:, 2, :], ALU.mult).then_inc(summed, 1)
            dve.wait_ge(shaped, NT)
            for t in range(NT):
                dve.wait_ge(summed, t + 1)
                nc.vector.tensor_tensor(k.x[:, t, :], k.x[:, t, :], k.xn[:, t, :], ALU.add).then_inc(dn, 1)
            dve.wait_ge(dn, 2 * NT)

        @block.tensor
        def _(pe):
            if not k.ident_loaded:
                pe.wait_ge(loaded, 16 * LOADS)
            on_tensor(pe)
            pe.wait_ge(loaded, 16 * LOADS)

            def project_queries(b):
                if b >= 1:
                    pe.wait_ge(v_out, b)
                for m in range(KD):
                    for d in range(KD):
                        out = nc.tensor.matmul(pp[:, m * S:(m + 1) * S], w[:, 0, d, m * P:(m + 1) * P],
                                               k.xT[:, d, b * S:(b + 1) * S], start=(d == 0), stop=(d == KD - 1))
                out.then_inc(proj, 1)

            def project_keys(b):
                pe.wait_ge(qk_out, 4 * b + 2)
                for m in range(KD):
                    for d in range(KD):
                        out = nc.tensor.matmul(pp[:, m * S:(m + 1) * S], w[:, 1, d, m * P:(m + 1) * P],
                                               cT[:, d, b * S:(b + 1) * S], start=(d == 0), stop=(d == KD - 1))
                out.then_inc(proj, 1)

            def project_values(b):
                pe.wait_ge(qk_out, 4 * b + 4)
                for kt in range(2):
                    for d in range(KD):
                        out = nc.tensor.matmul(pp[:, kt * D:(kt + 1) * D], cT[:, d, (2 * b + kt) * P:(2 * b + kt + 1) * P],
                                               w[:, 2, d, :], start=(d == 0), stop=(d == KD - 1))
                out.then_inc(proj, 1)

            def scores(U):
                b, u = U // X0_U, U % X0_U
                h, kt = 2 * (u // 2), u % 2
                if u == 0:
                    pe.wait_ge(qz_ready, 2 * b + 2)
                    pe.wait_ge(qk_out, 4 * b + 4)
                if U >= 2:
                    pe.wait_ge(clip_done, U - 1)
                nc.tensor.matmul(pS[U % 2][:, :], kT[b % 2][:, h // X0_HM, kt * P:(kt + 1) * P],
                                 qz[b % 2][:, h:h + 2, :].rearrange("p h s -> p (h s)"),
                                 start=True, stop=True).then_inc(scored, 1)

            def weigh(n):
                b, pair = n // (X0_H // 2), n % (X0_H // 2)
                pe.wait_ge(probs, 2 * n + 2)
                if pair == 0:
                    pe.wait_ge(v_out, b + 1)
                    pe.wait_ge(consts, 2)
                    if b >= 1:
                        pe.wait_ge(O_ready, 2 * b)
                for h in range(2):
                    c0 = (2 * pair + h) * (X0_D + 1)
                    for qt in range(2):
                        for kt in range(2):
                            out = nc.tensor.matmul(pO[qt][:, c0:c0 + X0_D + 1],
                                                   PT[(2 * n + kt) % 6][:, h, qt * P:(qt + 1) * P],
                                                   v[b % 2][:, kt, 2 * pair + h, :], start=(kt == 0), stop=(kt == 1))
                out.then_inc(weighed, 1)

            def turn_O(b, qt):
                j = 2 * b + qt
                pe.wait_ge(O_ready, j + 1)
                if j >= 1:
                    pe.wait_ge(OT_ready, j)
                for c in range(KD):
                    out = nc.tensor.transpose(pOT[:, c * P:(c + 1) * P],
                                              O[qt][:, c * X0_HM:(c + 1) * X0_HM, :].rearrange("p h n -> p (h n)"),
                                              k.ident[:, :])
                out.then_inc(turnedO, 1)

            def project_out(b, qt):
                j = 2 * b + qt
                pe.wait_ge(OT_ready, j + 1)
                if b >= 1:
                    pe.wait_ge(scaled, 2 * (j - 2) + 1)
                for c in range(KD):
                    out = nc.tensor.matmul(pY[qt][:, 0:D], OT[qt][:, c, :], w[:, 3, c, :],
                                           start=(c == 0), stop=(c == KD - 1))
                out.then_inc(projected, 1)

            project_queries(0)
            project_keys(0)
            project_values(0)
            for U in range(B * X0_U + 12):
                b, u = U // X0_U, U % X0_U
                if U < B * X0_U:
                    scores(U)
                    for at_u, step in ((4, project_queries), (6, project_keys), (8, project_values)):
                        if u == at_u and b + 1 < B:
                            step(b + 1)
                if U % 2 == 0 and 0 <= (U - 4) // 2 < B * X0_H // 2 and U >= 4:
                    weigh((U - 4) // 2)
                for qt in range(2):
                    r = U - X0_U - 8 - qt
                    if r >= 0 and r % X0_U == 0:
                        turn_O(r // X0_U, qt)
                    r = U - X0_U - 9 - qt
                    if r >= 0 and r % X0_U == 0:
                        project_out(r // X0_U, qt)
    k.ident_loaded = True


M0_E, M0_I, M0_SH = 8, 176, 704
M0_GRAN = 16
M0_PER = M0_I // M0_GRAN
M0_TILES = -(-(M0_E * M0_I + M0_SH) // P)
M0_COLS = -(-M0_TILES * P // M0_I)
WT = 3 * D
FB = 2


def experts_0(nc, k, src):
    with ExitStack() as ctx:
        sb = lambda name, shape, dt=F32: k.sb(ctx, "m0_" + name, shape, dt)
        rw = sb("rw", [P, KD, M0_E + 1])
        iota = sb("iota", [P, M0_E])
        lg = sb("lg", [P, NT, M0_E + 1])
        top = sb("top", [P, NT, 8])
        at = sb("at", [P, NT, 8], U32)
        atf = sb("atf", [P, NT, 2])
        gap = sb("gap", [P, NT, 2])
        eg = sb("eg", [P, NT, 2])
        share = sb("share", [P, NT, 3])
        hot = sb("hot", [P, NT, 2, M0_E])
        comb = sb("comb", [P, NT, M0_COLS])
        combT = sb("combT", [M0_COLS, T])
        zeros = sb("zeros", [P, NC], BF16)
        w = [sb(f"w{i}", [P, WT]) for i in range(3)]
        cw = [sb(f"cw{i}", [P, T]) for i in range(2)]
        sg = [sb(f"sg{i}", [P, NC]) for i in range(2)]
        hu = [sb(f"hu{i}", [P, NC]) for i in range(2)]
        hT = [sb(f"hT{i}", [P, T]) for i in range(2)]
        pg = [k.ps(ctx, f"m0_pg{i}") for i in range(2)]
        pu = [k.ps(ctx, f"m0_pu{i}") for i in range(2)]
        acc = [k.ps(ctx, f"m0_acc{i}") for i in range(4)]
        table = nc.dram_tensor("m0_table", (M0_COLS, M0_PER, T), F32, kind="Internal").ap()

        sem = lambda name: k.sem("m0_" + name)
        on_vector, on_gpsimd, on_tensor, on_scalar, _ = norm_and_turn(nc, k, ctx, "m0", [pg[0], pg[1], pu[0], pu[1]])
        loaded, zero_set = sem("loaded"), sem("zero_set")
        w_in = [sem(f"w_in{i}") for i in range(3)]
        cw_in = [sem(f"cw_in{i}") for i in range(2)]
        logits, lg_ready, routed, gates, comb_ready = (sem("logits"), sem("lg_ready"), sem("routed"),
                                                       sem("gates"), sem("comb_ready"))
        turnedC, combT_ready, table_out = sem("turnedC"), sem("combT_ready"), sem("table_out")
        gated, silu_done, up_done, h_ready, down_done, added = (sem("gated"), sem("silu_done"), sem("up_done"),
                                                                sem("h_ready"), sem("down_done"), sem("added"))
        block = ctx.enter_context(nc.Block())
        LAST = M0_TILES - 1
        PAIRS = (M0_TILES - 3) // 2
        assert M0_TILES == 3 + 2 * PAIRS

        def tiles(eng, step):
            step(0, 0)
            step(1, 1)
            with eng.Fori(0, PAIRS) as i:
                for s in range(2):
                    step(i * 2 + (2 + s), s)
            step(LAST, LAST % 2)

        def early(n, k_):
            return isinstance(n, int) and n < k_

        def w_count(n, par):
            return 16 * (n // 2 + 1) if isinstance(n, int) else n * 8 + (16 - 8 * par)

        @block.sync
        def _(sp):
            sp.dma_start(rw[:, :, :], src["m0_rw"]).then_inc(loaded, 16)
            sp.dma_start(iota[:, :], src["m0_iota"]).then_inc(loaded, 16)
            if not k.ident_loaded:
                sp.dma_start(k.ident[:, :], src["ident"]).then_inc(loaded, 16)
            else:
                sp.sem_inc(loaded, 16)
            for n in range(2):
                sp.dma_start(w[n][:, :], src["m0_w"][n]).then_inc(w_in[n], 16)
            sp.wait_ge(combT_ready, 2)
            spread_rows = combT[:, :].rearrange("e (o t) -> e o t", o=1).to_broadcast([M0_COLS, M0_PER, T])
            sp.dma_start(table, spread_rows).then_inc(table_out, 16)
            sp.wait_ge(table_out, 16)
            rows = table.rearrange("e g t -> (e g) t")

            def weights_of(n, par):
                sp.dma_start(cw[par][:, :], per_granule(rows, n)).then_inc(cw_in[par], 16)

            def step(n, par):
                sp.wait_ge(h_ready, 2 * n + 2)
                weights_of(n + 2, par)
                sp.wait_ge(down_done, n + 1)
                sp.dma_start(w[par][:, :], src["m0_w"][bass.ds(n + 2, 1)].rearrange("g p n -> p (g n)"))\
                    .then_inc(w_in[par], 16)

            def per_granule(rows, n):
                g = rows[bass.ds(n * (P // M0_GRAN), P // M0_GRAN)]
                return g.rearrange("(g o) t -> g o t", o=1).to_broadcast([P // M0_GRAN, M0_GRAN, T])

            weights_of(0, 0)
            weights_of(1, 1)
            with sp.Fori(0, PAIRS) as i:
                for s in range(2):
                    step(i * 2 + s, s)
            step(LAST - 2, LAST % 2)

        @block.gpsimd
        def _(pool):
            nc.gpsimd.memset(zeros[:, :], 0.0).then_inc(zero_set, 1)
            on_gpsimd(pool)

        @block.scalar
        def _(act):
            on_scalar(act)
            act.wait_ge(gates, 1)
            nc.scalar.activation(eg[:, :, :], gap[:, :, :], ACT.Exp).then_inc(gates, 1)
            for h in range(2):
                act.wait_ge(turnedC, 1)
                nc.scalar.copy(combT[:, h * NC:(h + 1) * NC], acc[1 + h][0:M0_COLS, :]).then_inc(combT_ready, 1)

            def step(n, par):
                for h in range(2):
                    act.wait_ge(gated, 2 * n + h + 1)
                    if not early(n, 1):
                        act.wait_ge(up_done, 2 * n + h - 1)
                    nc.scalar.activation(sg[h][:, :], pg[h][:, :], ACT.Silu).then_inc(silu_done, 1)

            tiles(act, step)

        @block.vector
        def _(dve):
            on_vector(dve)
            dve.wait_ge(loaded, 48)
            dve.wait_ge(logits, 1)
            nc.vector.tensor_copy(lg[:, :, :], acc[0][:, 0:NT * (M0_E + 1)].rearrange("p (t e) -> p t e", t=NT))\
                .then_inc(lg_ready, 1)
            dve.wait_ge(lg_ready, 1)
            for t in range(NT):
                nc.vector.max(top[:, t, :], lg[:, t, 0:M0_E]).then_inc(routed, 1)
            for t in range(NT):
                dve.wait_ge(routed, t + 1)
                nc.vector.max_index(at[:, t, :], top[:, t, :], lg[:, t, 0:M0_E]).then_inc(lg_ready, 1)
            dve.wait_ge(lg_ready, 1 + NT)
            nc.vector.tensor_tensor(gap[:, :, 0:1], top[:, :, 1:2], top[:, :, 0:1], ALU.subtract)
            nc.vector.tensor_scalar(gap[:, :, 1:2], lg[:, :, M0_E:M0_E + 1], -1.0, None, ALU.mult).then_inc(gates, 1)
            nc.vector.tensor_copy(atf[:, :, :], at[:, :, 0:2]).then_inc(comb_ready, 1)
            dve.wait_ge(comb_ready, 1)
            for c in range(2):
                nc.vector.tensor_tensor(hot[:, :, c, :], iota[:, :].rearrange("p (o e) -> p o e", o=1).to_broadcast([P, NT, M0_E]),
                                        atf[:, :, c:c + 1].to_broadcast([P, NT, M0_E]), ALU.is_equal)\
                    .then_inc(comb_ready, 1)
            dve.wait_ge(gates, 2)
            nc.vector.tensor_scalar(eg[:, :, :], eg[:, :, :], 1.0, None, ALU.add).then_inc(comb_ready, 1)
            dve.wait_ge(comb_ready, 4)
            nc.vector.reciprocal(share[:, :, 0:2], eg[:, :, :]).then_inc(comb_ready, 1)
            dve.wait_ge(comb_ready, 5)
            nc.vector.tensor_scalar(eg[:, :, 0:1], eg[:, :, 0:1], 1.0, None, ALU.subtract).then_inc(comb_ready, 1)
            dve.wait_ge(comb_ready, 6)
            nc.vector.tensor_tensor(share[:, :, 2:3], eg[:, :, 0:1], share[:, :, 0:1], ALU.mult).then_inc(comb_ready, 1)
            dve.wait_ge(comb_ready, 7)
            for c, s in ((0, 0), (1, 2)):
                nc.vector.tensor_tensor(hot[:, :, c, :], hot[:, :, c, :],
                                        share[:, :, s:s + 1].to_broadcast([P, NT, M0_E]), ALU.mult)\
                    .then_inc(comb_ready, 1)
            nc.vector.tensor_copy(comb[:, :, M0_E:M0_COLS], share[:, :, 1:2].to_broadcast([P, NT, M0_COLS - M0_E]))\
                .then_inc(comb_ready, 1)
            dve.wait_ge(comb_ready, 10)
            nc.vector.tensor_tensor(comb[:, :, 0:M0_E], hot[:, :, 0, :], hot[:, :, 1, :], ALU.add).then_inc(comb_ready, 1)

            def step(n, par):
                for h in range(2):
                    dve.wait_ge(silu_done, 2 * n + h + 1)
                    nc.vector.tensor_tensor(hu[h][:, :], sg[h][:, :], pu[h][:, :], ALU.mult).then_inc(up_done, 1)
                    if h == 0:
                        dve.wait_ge(cw_in[par], w_count(n, par))
                    dve.wait_ge(up_done, 2 * n + h + 1)
                    if not early(n, 2):
                        dve.wait_ge(down_done, n - 1)
                    nc.vector.tensor_tensor(hT[par][:, h * NC:(h + 1) * NC], hu[h][:, :],
                                            cw[par][:, h * NC:(h + 1) * NC], ALU.mult).then_inc(h_ready, 1)

            tiles(dve, step)
            dve.wait_ge(down_done, M0_TILES)
            for a in range(4):
                nc.vector.tensor_tensor(k.x[:, 2 * a:2 * a + 2, :], acc[a][:, :].rearrange("p (t n) -> p t n", t=2),
                                        k.x[:, 2 * a:2 * a + 2, :], ALU.add).then_inc(added, 1)
            dve.wait_ge(added, 4)

        @block.tensor
        def _(pe):
            pe.wait_ge(loaded, 48)
            on_tensor(pe)
            for t in range(NT):
                for d in range(KD):
                    out = nc.tensor.matmul(acc[0][:, t * (M0_E + 1):(t + 1) * (M0_E + 1)], k.xT[:, d, t * P:(t + 1) * P],
                                           rw[:, d, :], start=(d == 0), stop=(d == KD - 1))
            out.then_inc(logits, 1)

            def gate_up(n, par):
                pe.wait_ge(w_in[par], w_count(n, par))
                for h in range(2):
                    if not early(n, 1):
                        pe.wait_ge(up_done, 2 * n + h - 1)
                    for bank, off in ((pg[h], 0), (pu[h], D)):
                        for d in range(KD):
                            out = nc.tensor.matmul(bank[:, :], w[par][:, off + d * P:off + (d + 1) * P],
                                                   k.xT[:, d, h * NC:(h + 1) * NC],
                                                   start=(d == 0), stop=(d == KD - 1))
                    out.then_inc(gated, 1)

            def down(n, par, last=False):
                for h in range(2):
                    pe.wait_ge(h_ready, 2 * n + h + 1)
                    for t in range(h * NT // 2, (h + 1) * NT // 2):
                        out = nc.tensor.matmul(acc[t // 2][:, (t % 2) * D:(t % 2 + 1) * D], hT[par][:, t * P:(t + 1) * P],
                                               w[par][:, 2 * D:3 * D], start=False, stop=last, skip_group_check=True)
                out.then_inc(down_done, 1)

            gate_up(0, 0)
            pe.wait_ge(comb_ready, 11)
            for t in range(NT):
                out = nc.tensor.transpose(acc[1 + t // 4][0:M0_COLS, (t % 4) * P:(t % 4 + 1) * P], comb[:, t, :], k.ident[:, :])
            out.then_inc(turnedC, 1)
            pe.wait_ge(combT_ready, 2)
            pe.wait_ge(lg_ready, 1)
            pe.wait_ge(zero_set, 1)
            for a in range(4):
                nc.tensor.matmul(acc[a][:, :], zeros[:, 0:P], zeros[:, :], start=True, stop=False, skip_group_check=True)
            gate_up(1, 1)
            down(0, 0)
            with pe.Fori(0, PAIRS) as i:
                for s in range(2):
                    gate_up(i * 2 + (2 + s), s)
                    down(i * 2 + (1 + s), 1 - s)
            gate_up(LAST, LAST % 2)
            down(LAST - 1, 1 - LAST % 2)
            down(LAST, LAST % 2, last=True)
    k.ident_loaded = True


def store_x(nc, k, out):
    with ExitStack() as ctx:
        stored = k.sem("stored")
        block = ctx.enter_context(nc.Block())

        @block.sync
        def _(sp):
            for t in range(NT):
                sp.dma_start(out.rearrange("(t p) d -> p t d", p=P)[:, t, :], k.x[:, t, :]).then_inc(stored, 16)
            sp.wait_ge(stored, 16 * NT)

def attention_1(nc, k, src):
    with ExitStack() as ctx:
        sb = lambda name, shape, dt=F32: k.sb(ctx, "a1_" + name, shape, dt)
        w = [sb(f"w{i}", [P, A1_W]) for i in range(2)]
        wo = [sb(f"wo{i}", [P, D + P]) for i in range(2)]
        cs = sb("cs", [P, 4, S])
        cmask = sb("cmask", [P, 3 * P])
        rows = sb("rows", [P, 3, D])
        qT = [sb(f"qT{i}", [P, T]) for i in range(2)]
        kT = [sb(f"kT{i}", [P, T]) for i in range(2)]
        v = [sb(f"v{i}", [P, NT, P + 1]) for i in range(2)]
        t1 = [sb(f"t1{i}", [P, 2, S]) for i in range(2)]
        t2 = [sb(f"t2{i}", [P, 2, S]) for i in range(2)]
        hn = sb("hn", [P, NT, D])
        nS = [sb(f"nS{i}", [P, 3 * P]) for i in range(2)]
        nm = [sb(f"nm{i}", [P, 2]) for i in range(2)]
        Pm = [sb(f"Pm{i}", [P, 3 * P]) for i in range(2)]
        PT = [sb(f"PT{i}", [P, 3, P]) for i in range(2)]
        rec = sb("rec", [P, 2])
        O = [sb(f"O{i}", [P, 2, P]) for i in range(2)]
        OT = [sb(f"OT{i}", [P, 2, P]) for i in range(2)]
        pp = [k.ps(ctx, f"a1_pp{i}") for i in range(2)]
        pS = [k.ps(ctx, f"a1_pS{i}") for i in range(2)]
        pT = k.ps(ctx, "a1_pT")
        pO = k.ps(ctx, "a1_pO")
        pOT = k.ps(ctx, "a1_pOT")
        pY = k.ps(ctx, "a1_pY")
        turn_banks = [pS[0], pS[1], pT, pO]

        sem = lambda name: k.sem("a1_" + name)
        loaded, ones_set, gate, sp_gate = sem("loaded"), sem("ones_set"), sem("gate"), sem("sp_gate")
        w_in, wo_in = [sem("w_in0"), sem("w_in1")], [sem("wo_in0"), sem("wo_in1")]
        ln, rstd_ready, h_ready, n_ready, xn_ready = (sem("ln"), sem("rstd_ready"), sem("h_ready"),
                                                      sem("n_ready"), sem("xn_ready"))
        turned, xT_ready, based = sem("turned"), sem("xT_ready"), sem("based")
        proj, roped, chunk, v_ready = sem("proj"), sem("roped"), sem("chunk"), sem("v_ready")
        scored, maxed, probs, turnedP, PT_ready = (sem("scored"), sem("maxed"), sem("probs"),
                                                   sem("turnedP"), sem("PT_ready"))
        weighed, rec_ready, O_ready = sem("weighed"), sem("rec_ready"), sem("O_ready")
        turnedO, OT_ready, projected, added = sem("turnedO"), sem("OT_ready"), sem("projected"), sem("added")
        LOADS = 4

        def heads(eng, step):
            step(0, 0, first=True)
            with eng.Fori(0, (A1_H - 2) // 2) as i:
                for s in range(2):
                    step(i * 2 + (1 + s), (1 + s) % 2)
            step(A1_H - 1, 1, last=True)
            step(A1_H, 0, drain=True)

        def after(H, b, lag):
            if b >= lag:
                return H, b - lag, 0
            return H - 1, b - lag + A1_U, 1

        def exists(H, b, lag, first, drain):
            return not ((first and b < lag) or (drain and b >= lag))

        def before(H, c, n):
            return isinstance(H, int) and A1_U * H + c < n

        def arrivals(H, par):
            return 16 * (H // 2 + 1) if isinstance(H, int) else H * 8 + (16 - 8 * par)

        CHUNKS = {0: (0, 1), 1: (2, 3), 2: (4,), 3: (5,)}
        block = ctx.enter_context(nc.Block())

        @block.sync
        def _(sp):
            for dst, name in ((rows, "a1_rows"), (cs, "a1_cs"), (cmask, "a1_mask")):
                sp.dma_start(dst[tuple([slice(None)] * len(dst.shape))], src[name]).then_inc(loaded, 16)
            if not k.ident_loaded:
                sp.dma_start(k.ident[:, :], src["ident"]).then_inc(loaded, 16)
            else:
                sp.sem_inc(loaded, 16)
            for h in range(2):
                sp.dma_start(w[h][:, :], src["a1_w"][h]).then_inc(w_in[h], 16)
                sp.dma_start(wo[h][:, :], src["a1_wo"][h]).then_inc(wo_in[h], 16)
            with sp.Fori(0, (A1_H - 2) // 2) as i:
                for s in range(2):
                    h = i * 2 + (2 + s)
                    sp.wait_ge(chunk, (h - 1) * 4)
                    sp.sem_inc(sp_gate, 1)
                    sp.wait_ge(v_ready, (h - 1) * 2)
                    sp.dma_start(w[s][:, :], src["a1_w"][bass.ds(h, 1)].rearrange("g p n -> p (g n)"))\
                        .then_inc(w_in[s], 16)
                    sp.wait_ge(added, (h - 1) * A1_U)
                    sp.dma_start(wo[s][:, :], src["a1_wo"][bass.ds(h, 1)].rearrange("g p n -> p (g n)"))\
                        .then_inc(wo_in[s], 16)

        @block.gpsimd
        def _(pool):
            for i in range(2):
                nc.gpsimd.memset(v[i][:, :, P:P + 1], 1.0).then_inc(ones_set, 1)
            inverse_root(nc, pool, k, ln, rstd_ready, 0)
            inverse_root(nc, pool, k, ln, rstd_ready, 1)

            def project(H, par):
                for c in range(4):
                    pool.wait_ge(roped, H * 4 + (c + 1))
                    dst, half = (qT, kT)[c // 2][par], c % 2
                    nc.gpsimd.tensor_tensor(dst[:, half * NC:(half + 1) * NC],
                                            t1[c % 2][:, :, :].rearrange("p b s -> p (b s)"),
                                            t2[c % 2][:, :, :].rearrange("p b s -> p (b s)"),
                                            ALU.add).then_inc(chunk, 1)

            project(0, 0)
            project(1, 1)
            with pool.Fori(0, (A1_H - 2) // 2) as i:
                for s in range(2):
                    project(i * 2 + (2 + s), s)

        @block.scalar
        def _(act):
            for j in range(4):
                act.wait_ge(turned, (j % NH2) + 1)
                nc.scalar.copy(k.xT[:, j // NH2, (j % NH2) * NC:(j % NH2 + 1) * NC],
                               turn_banks[j][:, :]).then_inc(xT_ready, 1)

            def values(H, par, c):
                act.wait_ge(proj, H * 6 + (c + 1))
                n = c - 4
                nc.scalar.copy(v[par][:, 4 * n:4 * n + 4, 0:P],
                               pp[c % 2][:, :].rearrange("p (t n) -> p t n", t=4)).then_inc(v_ready, 1)

            def step(H, par, first=False, last=False, drain=False):
                for b in range(A1_U if not drain else 2):
                    if exists(H, b, 2, first, drain):
                        h, u, _ = after(H, b, 2)
                        act.wait_ge(turnedO, h * A1_U + (u + 1))
                        nc.scalar.copy(OT[u % 2][:, :, :].rearrange("p c q -> p (c q)"), pOT[:, 0:2 * P])\
                            .then_inc(OT_ready, 1)
                    if exists(H, b, 1, first, drain):
                        h, u, _ = after(H, b, 1)
                        act.wait_ge(turnedP, h * A1_U + (u + 1))
                        nc.scalar.copy(PT[u % 2][:, :, :].rearrange("p c q -> p (c q)"), pT[:, 0:3 * P])\
                            .then_inc(PT_ready, 1)
                    if not drain:
                        act.wait_ge(maxed, H * A1_U + (b + 1))
                        nc.scalar.activation(Pm[b % 2][:, 0:P], nS[b % 2][:, 0:P], ACT.Exp,
                                             bias=nm[b % 2][:, 0:1], scale=-1.0)
                        nc.scalar.activation(Pm[b % 2][:, P:3 * P], nS[b % 2][:, P:3 * P], ACT.Exp,
                                             bias=nm[b % 2][:, 1:2], scale=-1.0).then_inc(probs, 1)
                    if not (last or drain):
                        for c in CHUNKS[b]:
                            if c >= 4:
                                values(H + 1, 1 - par, c)

            for c in (4, 5):
                values(0, 0, c)
            heads(act, step)

        @block.vector
        def _(dve):
            norm_rows(nc, dve, k, k.x, hn, ln, rstd_ready, 0, h_ready)
            dve.wait_ge(h_ready, NT)
            norm_rows(nc, dve, k, hn, k.xn, ln, rstd_ready, 1, n_ready)
            dve.wait_ge(loaded, 16 * LOADS)
            for t in range(NT):
                dve.wait_ge(n_ready, t + 1)
                nc.vector.tensor_tensor(k.xn[:, t, :], k.xn[:, t, :], rows[:, 0, :], ALU.mult).then_inc(based, 1)
            for t in range(NT):
                dve.wait_ge(based, t + 1)
                nc.vector.tensor_tensor(k.xn[:, t, :], k.xn[:, t, :], rows[:, 1, :], ALU.add).then_inc(xn_ready, 1)
            for t in range(NT):
                nc.vector.tensor_tensor(k.x[:, t, :], k.x[:, t, :], rows[:, 2, :], ALU.add).then_inc(based, 1)
            for t in range(NT):
                dve.wait_ge(based, NT + t + 1)
                nc.vector.tensor_tensor(k.x[:, t, :], k.x[:, t, :], hn[:, t, :], ALU.add).then_inc(based, 1)
            dve.wait_ge(based, 3 * NT)

            def rope(H, par, c):
                n, kind = c % 2, c // 2
                bias = w[par][:, A1_W - 2 + kind:A1_W - 1 + kind]
                dve.wait_ge(w_in[par], arrivals(H, par))
                dve.wait_ge(proj, H * 6 + (c + 1))
                if not before(H, c, 2):
                    dve.wait_ge(chunk, H * 4 + (c - 1))
                a = pp[n][:, :].rearrange("p (b s) -> p b s", b=2)
                lo, hi = slice(0, 64), slice(64, 128)
                tab = lambda i, r: cs[r, 2 * kind + i:2 * kind + i + 1, :].to_broadcast([r.stop - r.start, 2, S])
                nc.vector.scalar_tensor_tensor(out=t1[n][:, :, :], in0=a, scalar=bias, in1=tab(0, slice(0, P)),
                                               op0=ALU.add, op1=ALU.mult)
                nc.vector.scalar_tensor_tensor(out=t2[n][lo, :, :], in0=a[hi], scalar=bias[hi], in1=tab(1, hi),
                                               op0=ALU.add, op1=ALU.mult)
                nc.vector.scalar_tensor_tensor(out=t2[n][hi, :, :], in0=a[lo], scalar=bias[lo], in1=tab(1, lo),
                                               op0=ALU.add, op1=ALU.mult).then_inc(roped, 1)

            def maxima(H, b):
                dve.wait_ge(scored, H * A1_U + (b + 1))
                if not before(H, b, 2):
                    dve.wait_ge(probs, H * A1_U + (b - 1))
                dve.sem_inc(gate, 1)
                nc.vector.tensor_tensor_reduce(nS[b % 2][:, 0:P], pS[b % 2][:, 0:P], cmask[:, 0:P], -1.0, 3.0e38,
                                               ALU.add, ALU.min, nm[b % 2][:, 0:1])
                nc.vector.tensor_tensor_reduce(nS[b % 2][:, P:3 * P], pS[b % 2][:, P:3 * P], cmask[:, P:3 * P], -1.0,
                                               3.0e38, ALU.add, ALU.min, nm[b % 2][:, 1:2]).then_inc(maxed, 1)

            def normalise(H, u, par):
                dve.wait_ge(weighed, H * A1_U + (u + 1))
                o = pO[:, 0:2 * (P + 1)].rearrange("p (c n) -> p c n", c=2)
                nc.vector.reciprocal(rec[:, :], o[:, :, P]).then_inc(rec_ready, 1)
                if u == 0:
                    dve.wait_ge(wo_in[par], arrivals(H, par))
                dve.wait_ge(rec_ready, H * A1_U + (u + 1))
                if not before(H, u, 2):
                    dve.wait_ge(turnedO, H * A1_U + (u - 1))
                for c in range(2):
                    out = nc.vector.scalar_tensor_tensor(out=O[u % 2][:, c, :], in0=o[:, c, 0:P],
                                                         scalar=rec[:, c:c + 1], in1=wo[par][:, D:D + P],
                                                         op0=ALU.mult, op1=ALU.add)
                out.then_inc(O_ready, 1)

            def add_y(H, u):
                dve.wait_ge(projected, H * A1_U + (u + 1))
                if not before(H, u, A1_U):
                    dve.wait_ge(added, H * A1_U + u)
                nc.vector.tensor_tensor(k.x[:, 2 * u:2 * u + 2, :], pY[:, :].rearrange("p (c n) -> p c n", c=2),
                                        k.x[:, 2 * u:2 * u + 2, :], ALU.add).then_inc(added, 1)

            def step(H, par, first=False, last=False, drain=False):
                for b in range(A1_U if not drain else 2):
                    cc = CHUNKS[b] if not (last or drain) else ()
                    if not drain:
                        maxima(H, b)
                    if len(cc) and cc[0] < 4:
                        rope(H + 1, 1 - par, cc[0])
                    if exists(H, b, 1, first, drain):
                        h, u, x = after(H, b, 1)
                        normalise(h, u, par ^ x)
                    if exists(H, b, 2, first, drain):
                        h, u, _ = after(H, b, 2)
                        add_y(h, u)
                    if len(cc) > 1:
                        rope(H + 1, 1 - par, cc[1])

            for c in range(4):
                rope(0, 0, c)
            heads(dve, step)
            dve.wait_ge(added, A1_H * A1_U)

        @block.tensor
        def _(pe):
            pe.wait_ge(loaded, 16 * LOADS)
            turn_rows(nc, pe, k, turn_banks, xn_ready, 0, turned)
            pe.wait_ge(xT_ready, 4)

            def chunk_of(H, par, c):
                if c == 0:
                    pe.wait_ge(w_in[par], arrivals(H, par))
                if not (isinstance(H, int) and H == 0 and c < 2):
                    if c < 2:
                        pe.wait_ge(v_ready, H * 2 + (c - 1))
                    else:
                        pe.wait_ge(roped, H * 4 + (c - 1))
                if c < 4:
                    for d in range(KD):
                        off = ((c // 2) * KD + d) * P
                        out = nc.tensor.matmul(pp[c % 2][:, :], w[par][:, off:off + P],
                                               k.xT[:, d, (c % 2) * NC:(c % 2 + 1) * NC],
                                               start=(d == 0), stop=(d == KD - 1))
                else:
                    for t in range(4):
                        for d in range(KD):
                            off = (2 * KD + d) * P
                            tt = 4 * (c - 4) + t
                            out = nc.tensor.matmul(pp[c % 2][:, t * P:(t + 1) * P], k.xT[:, d, tt * P:(tt + 1) * P],
                                                   w[par][:, off:off + P], start=(d == 0), stop=(d == KD - 1))
                out.then_inc(proj, 1)

            def scores(H, par, b):
                if b == 0:
                    pe.wait_ge(chunk, (H + 1) * 4)
                if not before(H, b, 2):
                    pe.wait_ge(maxed, H * A1_U + (b - 1))
                c = b * S
                nc.tensor.matmul(pS[b % 2][:, 0:P], qT[par][:, c:c + P], kT[par][:, c:c + P], start=True, stop=True)
                nc.tensor.matmul(pS[b % 2][:, P:3 * P], qT[par][:, c + P:c + S], kT[par][:, c:c + S],
                                 start=True, stop=True).then_inc(scored, 1)

            def turn_P(H, u):
                pe.wait_ge(probs, H * A1_U + (u + 1))
                if not before(H, u, 1):
                    pe.wait_ge(PT_ready, H * A1_U + u)
                for c in range(3):
                    out = nc.tensor.transpose(pT[:, c * P:(c + 1) * P], Pm[u % 2][:, c * P:(c + 1) * P], k.ident[:, :])
                out.then_inc(turnedP, 1)

            def weigh(H, par, u):
                pe.wait_ge(PT_ready, H * A1_U + (u + 1))
                if u == 0:
                    pe.wait_ge(v_ready, (H + 1) * 2)
                if isinstance(H, int) and H == 0 and u == 0:
                    pe.wait_ge(ones_set, 2)
                if not before(H, u, 1):
                    pe.wait_ge(O_ready, H * A1_U + u)
                nc.tensor.matmul(pO[:, 0:P + 1], PT[u % 2][:, 0, :], v[par][:, 2 * u, :], start=True, stop=True)
                for c in range(2):
                    out = nc.tensor.matmul(pO[:, P + 1:2 * (P + 1)], PT[u % 2][:, 1 + c, :], v[par][:, 2 * u + c, :],
                                           start=(c == 0), stop=(c == 1))
                out.then_inc(weighed, 1)

            def turn_O(H, u):
                pe.wait_ge(O_ready, H * A1_U + (u + 1))
                if not before(H, u, 1):
                    pe.wait_ge(OT_ready, H * A1_U + u)
                for c in range(2):
                    out = nc.tensor.transpose(pOT[:, c * P:(c + 1) * P], O[u % 2][:, c, :], k.ident[:, :])
                out.then_inc(turnedO, 1)

            def project_out(H, par, u):
                pe.wait_ge(OT_ready, H * A1_U + (u + 1))
                if u == 0:
                    pe.wait_ge(wo_in[par], arrivals(H, par))
                if not before(H, u, 1):
                    pe.wait_ge(added, H * A1_U + u)
                for c in range(2):
                    out = nc.tensor.matmul(pY[:, c * D:(c + 1) * D], OT[u % 2][:, c, :], wo[par][:, 0:D],
                                           start=True, stop=True)
                out.then_inc(projected, 1)

            def step(H, par, first=False, last=False, drain=False):
                for b in range(A1_U if not drain else 2):
                    cc = CHUNKS[b] if not (last or drain) else ()
                    if not drain:
                        scores(H, par, b)
                    if exists(H, b, 2, first, drain):
                        h, u, _ = after(H, b, 2)
                        turn_O(h, u)
                    if exists(H, b, 1, first, drain):
                        h, u, _ = after(H, b, 1)
                        turn_P(h, u)
                    if len(cc):
                        chunk_of(H + 1, 1 - par, cc[0])
                    if exists(H, b, 1, first, drain):
                        h, u, x = after(H, b, 1)
                        weigh(h, par ^ x, u)
                    if exists(H, b, 2, first, drain):
                        h, u, x = after(H, b, 2)
                        project_out(h, par ^ x, u)
                    if len(cc) > 1:
                        chunk_of(H + 1, 1 - par, cc[1])

            for c in range(6):
                chunk_of(0, 0, c)
            heads(pe, step)
    k.ident_loaded = True

X1_H = 2
X1_EPS = 1e-3


def retention_1(nc, k, src):
    with ExitStack() as ctx:
        sb = lambda name, shape, dt=F32: k.sb(ctx, "x1_" + name, shape, dt)
        wh = sb("wh", [P, X1_H, P])
        wg = sb("wg", [P, KD, D])
        wo = sb("wo", [P, KD, D])
        cT = sb("cT", [P, KD, T])
        decay = sb("decay", [P, X1_H, 3 * P])
        rows = sb("rows", [P, 2, D])
        QT = sb("QT", [P, X1_H, T])
        KT = sb("KT", [P, X1_H, T])
        V = sb("V", [P, 2, X1_H, B, P])
        W = sb("W", [P, NT, D])
        A = sb("A", [P, X1_H, 4 * P])
        raw = sb("raw", [P, X1_H, 3 * P])
        O = sb("O", [P, NT, D])
        ba = [k.ps(ctx, f"x1_ba{i}") for i in range(4)]
        bb = [k.ps(ctx, f"x1_bb{i}") for i in range(4)]

        sem = lambda name: k.sem("x1_" + name)
        on_vector, on_gpsimd, on_tensor, on_scalar, (ln, rstd_ready, xn_ready, xT_ready) = \
            norm_and_turn(nc, k, ctx, "x1", bb)
        loaded, filled, moved, ones_set = sem("loaded"), sem("filled"), sem("moved"), sem("ones_set")
        scored, raw_ready, A_ready, weighed, O_ready = (sem("scored"), sem("raw_ready"), sem("A_ready"),
                                                        sem("weighed"), sem("O_ready"))
        normed, shaped, mixed, turned, mT_ready = (sem("normed"), sem("shaped"), sem("mixed"), sem("turnedM"),
                                                   sem("mT_ready"))
        projected, added = sem("projected"), sem("added")
        LOADS = 7
        block = ctx.enter_context(nc.Block())

        @block.sync
        def _(sp):
            for dst, name in ((wh, "x1_wh"), (cT, "ctxT"), (wg, "x1_wg"), (decay, "x1_decay"), (rows, "x1_rows"),
                              (wo, "x1_wo")):
                sp.dma_start(dst[tuple([slice(None)] * len(dst.shape))], src[name]).then_inc(loaded, 16)
            if not k.ident_loaded:
                sp.dma_start(k.ident[:, :], src["ident"]).then_inc(loaded, 16)
            else:
                sp.sem_inc(loaded, 16)

        @block.gpsimd
        def _(pool):
            nc.gpsimd.memset(A[:, :, 3 * P:4 * P], 1.0).then_inc(ones_set, 1)
            on_gpsimd(pool)
            inverse_root(nc, pool, k, ln, rstd_ready, 1, X1_EPS)

        @block.scalar
        def _(act):
            def move(j, out, func=ACT.Copy):
                act.wait_ge(filled, j + 1)
                bank = ba[j % 4][:, :]
                if len(out.shape) == 3:
                    bank = bank.rearrange("p (t n) -> p t n", t=out.shape[1])
                nc.scalar.activation(out, bank, func).then_inc(moved, 1)

            for h in range(X1_H):
                for half in range(NH2):
                    move(2 * h + half, KT[:, h, half * NC:(half + 1) * NC])
            for h in range(X1_H):
                for kt in range(2):
                    move(4 + 2 * h + kt, V[:, kt, h, :, :])
            on_scalar(act)
            for h in range(X1_H):
                for half in range(NH2):
                    move(8 + 2 * h + half, QT[:, h, half * NC:(half + 1) * NC])
            for g in range(4):
                move(12 + g, W[:, 2 * g:2 * g + 2, :], ACT.Relu)
            for h in range(X1_H):
                for st in range(2):
                    act.wait_ge(weighed, 2 * h + st + 1)
                    nc.scalar.copy(O[:, st:NT:2, h * P:(h + 1) * P],
                                   ba[2 * h + st][:, :].rearrange("p (b n) -> p b n", b=B)).then_inc(O_ready, 1)
            for j in range(4):
                act.wait_ge(turned, (j % NH2) + 1)
                nc.scalar.copy(k.xT[:, j // NH2, (j % NH2) * NC:(j % NH2 + 1) * NC], bb[j][:, :]).then_inc(mT_ready, 1)

        @block.vector
        def _(dve):
            on_vector(dve)
            dve.wait_ge(loaded, 16 * LOADS)
            for h in range(X1_H):
                dve.wait_ge(scored, h + 1)
                nc.vector.tensor_tensor(raw[:, h, :], bb[h][:, 0:3 * P], decay[:, h, :], ALU.mult).then_inc(raw_ready, 1)
                dve.wait_ge(raw_ready, 2 * h + 1)
                nc.vector.scalar_tensor_tensor(out=A[:, h, 0:3 * P], in0=raw[:, h, :], scalar=-1.0, in1=raw[:, h, :],
                                               op0=ALU.mult, op1=ALU.max).then_inc(raw_ready, 1)
                dve.wait_ge(raw_ready, 2 * h + 2)
                nc.vector.tensor_scalar(A[:, h, 0:3 * P], A[:, h, 0:3 * P], 1.0, None, ALU.max).then_inc(A_ready, 1)
            dve.wait_ge(O_ready, 4)
            norm_rows(nc, dve, k, O, k.xn, ln, rstd_ready, 1, normed)
            for t in range(NT):
                dve.wait_ge(normed, t + 1)
                nc.vector.tensor_tensor(k.xn[:, t, :], k.xn[:, t, :], rows[:, 0, :], ALU.mult).then_inc(shaped, 1)
            for t in range(NT):
                dve.wait_ge(shaped, t + 1)
                nc.vector.tensor_tensor(k.xn[:, t, :], k.xn[:, t, :], rows[:, 1, :], ALU.add).then_inc(shaped, 1)
            dve.wait_ge(moved, 16)
            for t in range(NT):
                dve.wait_ge(shaped, NT + t + 1)
                nc.vector.tensor_tensor(k.xn[:, t, :], k.xn[:, t, :], W[:, t, :], ALU.mult).then_inc(mixed, 1)
            for g in range(4):
                dve.wait_ge(projected, g + 1)
                nc.vector.tensor_tensor(k.x[:, 2 * g:2 * g + 2, :], ba[g][:, :].rearrange("p (t n) -> p t n", t=2),
                                        k.x[:, 2 * g:2 * g + 2, :], ALU.add).then_inc(added, 1)
            dve.wait_ge(added, 4)

        @block.tensor
        def _(pe):
            pe.wait_ge(loaded, 16 * LOADS)

            def free(j):
                if j >= 4:
                    pe.wait_ge(moved, j - 3)

            for h in range(X1_H):
                for half in range(NH2):
                    j = 2 * h + half
                    free(j)
                    nc.tensor.matmul(ba[j % 4][:, :], wh[:, h, :], cT[:, h, half * NC:(half + 1) * NC],
                                     start=True, stop=True).then_inc(filled, 1)
            for h in range(X1_H):
                for kt in range(2):
                    j = 4 + 2 * h + kt
                    free(j)
                    for b in range(B):
                        out = nc.tensor.matmul(ba[j % 4][:, b * P:(b + 1) * P], cT[:, h, (2 * b + kt) * P:(2 * b + kt + 1) * P],
                                               wh[:, h, :], start=True, stop=True)
                    out.then_inc(filled, 1)
            on_tensor(pe)
            for h in range(X1_H):
                for half in range(NH2):
                    j = 8 + 2 * h + half
                    free(j)
                    nc.tensor.matmul(ba[j % 4][:, :], wh[:, h, :], k.xT[:, h, half * NC:(half + 1) * NC],
                                     start=True, stop=True).then_inc(filled, 1)
            for g in range(4):
                free(12 + g)
                for t in range(2):
                    for d in range(KD):
                        tt = 2 * g + t
                        out = nc.tensor.matmul(ba[g][:, t * D:(t + 1) * D], k.xT[:, d, tt * P:(tt + 1) * P], wg[:, d, :],
                                               start=(d == 0), stop=(d == KD - 1))
                out.then_inc(filled, 1)
            pe.wait_ge(moved, 12)
            for h in range(X1_H):
                for b in range(B):
                    nc.tensor.matmul(bb[h][:, 0:2 * P], KT[:, h, b * S:b * S + P], QT[:, h, b * S:(b + 1) * S],
                                     start=(b == 0), stop=(b == B - 1))
                for b in range(B):
                    out = nc.tensor.matmul(bb[h][:, 2 * P:3 * P], KT[:, h, b * S + P:(b + 1) * S],
                                           QT[:, h, b * S + P:(b + 1) * S], start=(b == 0), stop=(b == B - 1))
                out.then_inc(scored, 1)
            pe.wait_ge(moved, 16)
            pe.wait_ge(ones_set, 1)
            for h in range(X1_H):
                pe.wait_ge(A_ready, h + 1)
                for st in range(2):
                    for kt in range(2):
                        block_at = st if kt == 0 else (3 if st == 0 else 2)
                        out = nc.tensor.matmul(ba[2 * h + st][:, :], A[:, h, block_at * P:(block_at + 1) * P],
                                               V[:, kt, h, :, :].rearrange("p b n -> p (b n)"),
                                               start=(kt == 0), stop=(kt == 1))
                    out.then_inc(weighed, 1)
            pe.wait_ge(A_ready, 2)
            turn_rows(nc, pe, k, bb, mixed, 0, turned)
            pe.wait_ge(mT_ready, 4)
            pe.wait_ge(O_ready, 4)
            for g in range(4):
                for t in range(2):
                    for d in range(KD):
                        tt = 2 * g + t
                        out = nc.tensor.matmul(ba[g][:, t * D:(t + 1) * D], k.xT[:, d, tt * P:(tt + 1) * P], wo[:, d, :],
                                               start=(d == 0), stop=(d == KD - 1))
                out.then_inc(projected, 1)
    k.ident_loaded = True


F1_GT, F1_ET = 1024 // P, 512 // P
F1_KEYS, F1_TOP, F1_E, F1_R = 64, 8, 512, 64


def memory_1(nc, k, src):
    with ExitStack() as ctx:
        sb = lambda name, shape, dt=F32: k.sb(ctx, "f1_" + name, shape, dt)
        wq = sb("wq", [P, KD, P])
        keys = sb("keys", [F1_R, 2, F1_KEYS])
        iota = sb("iota", [P, F1_E])
        QI = sb("QI", [F1_R, T, 2])
        R = sb("R", [P, 2, NT, F1_KEYS])
        top = sb("top", [P, 2, NT, F1_TOP])
        at = sb("at", [P, 2, NT, F1_TOP], U32)
        atf = sb("atf", [P, 2, NT, F1_TOP])
        sums = sb("sums", [P, F1_TOP, F1_TOP])
        which = sb("which", [P, F1_TOP, F1_TOP])
        best = sb("best", [P, NT, F1_TOP])
        bat = sb("bat", [P, F1_TOP], U32)
        batf = sb("batf", [P, F1_TOP])
        sel = sb("sel", [P, F1_TOP, F1_KEYS])
        expert = sb("expert", [P, NT, F1_TOP])
        ex = sb("ex", [P, NT, F1_TOP])
        tot = sb("tot", [P, NT, 2])
        PW = sb("PW", [P, NT, F1_E])
        hotv = [sb(f"hotv{i}", [P, F1_E]) for i in range(2)]
        hotp = [sb(f"hotp{i}", [P, F1_E]) for i in range(2)]
        zeros = sb("zeros", [P, NC], BF16)
        w = [sb(f"w{i}", [P, WT]) for i in range(3)]
        sg = [sb(f"sg{i}", [P, NC]) for i in range(2)]
        hT = [sb(f"hT{i}", [P, T]) for i in range(2)]
        pg = [k.ps(ctx, f"f1_pg{i}") for i in range(2)]
        pu = [k.ps(ctx, f"f1_pu{i}") for i in range(2)]
        acc = [k.ps(ctx, f"f1_acc{i}") for i in range(4)]

        sem = lambda name: k.sem("f1_" + name)
        on_vector, on_gpsimd, on_tensor, on_scalar, _ = norm_and_turn(nc, k, ctx, "f1", [pg[0], pg[1], pu[0], pu[1]])
        loaded, zero_set = sem("loaded"), sem("zero_set")
        w_in = [sem(f"w_in{i}") for i in range(3)]
        queried, QI_ready, routed, R_ready = sem("queried"), sem("QI_ready"), sem("routed"), sem("R_ready")
        step_done, best_ready, ex_ready, mix_ready = sem("step_done"), sem("best_ready"), sem("ex_ready"), sem("mix_ready")
        built, pool_step, pool_built = sem("built"), sem("pool_step"), sem("pool_built")
        gated, silu_done, h_ready, down_done, added = (sem("gated"), sem("silu_done"), sem("h_ready"),
                                                       sem("down_done"), sem("added"))
        TILES = F1_GT + F1_ET
        POOL_TILES = (6, 7)
        DVE_TILES = [j for j in range(NT) if j not in POOL_TILES]
        block = ctx.enter_context(nc.Block())

        @block.sync
        def _(sp):
            sp.dma_start(wq[:, :, :], src["f1_wq"]).then_inc(loaded, 16)
            sp.dma_start(keys[:, :, :], src["f1_keys"]).then_inc(loaded, 16)
            sp.dma_start(iota[:, :], src["f1_iota"]).then_inc(loaded, 16)
            if not k.ident_loaded:
                sp.dma_start(k.ident[:, :], src["ident"]).then_inc(loaded, 16)
            else:
                sp.sem_inc(loaded, 16)
            for n in range(TILES):
                if n >= 3:
                    sp.wait_ge(down_done, n - 2)
                sp.dma_start(w[n % 3][:, :], src["f1_w"][n]).then_inc(w_in[n % 3], 16)

        @block.gpsimd
        def _(pool):
            nc.gpsimd.memset(zeros[:, :], 0.0).then_inc(zero_set, 1)
            on_gpsimd(pool)
            pool.wait_ge(mix_ready, 1)
            n = 0
            for j in POOL_TILES:
                for c in range(F1_TOP):
                    out = PW[:, j, :] if c == 0 else hotp[c % 2][:, :]
                    nc.gpsimd.tensor_scalar(out, iota[:, :], expert[:, j, c:c + 1], ex[:, j, c:c + 1],
                                            ALU.is_equal, ALU.mult).then_inc(pool_step, 1)
                    n += 1
                    if c:
                        pool.wait_ge(pool_step, n)
                        nc.gpsimd.tensor_tensor(PW[:, j, :], PW[:, j, :], hotp[c % 2][:, :], ALU.add)\
                            .then_inc(pool_step, 1)
                        n += 1
                        pool.wait_ge(pool_step, n)
                pool.sem_inc(pool_built, 1)

        @block.scalar
        def _(act):
            on_scalar(act)
            for s in range(2):
                for half in range(NH2):
                    act.wait_ge(queried, 2 * s + half + 1)
                    nc.scalar.copy(QI[:, half * NC:(half + 1) * NC, s], acc[2 * s + half][0:F1_R, :]).then_inc(QI_ready, 1)
            for n in range(TILES):
                for h in range(2):
                    i = 2 * n + h
                    act.wait_ge(gated, i + 1)
                    if i >= 2:
                        act.wait_ge(h_ready, i - 1)
                    nc.scalar.activation(sg[h][:, :], pg[h][:, :], ACT.Silu).then_inc(silu_done, 1)
                if n == 3:
                    act.wait_ge(best_ready, 1)
                    nc.scalar.activation(ex[:, :, :], ex[:, :, :], ACT.Exp).then_inc(ex_ready, 1)

        @block.vector
        def _(dve):
            on_vector(dve)
            dve.wait_ge(loaded, 64)
            done = [0]

            def link(ins):
                done[0] += 1
                ins.then_inc(step_done, 1)
                dve.wait_ge(step_done, done[0])

            def gate_times_up(n):
                for h in range(2):
                    i = 2 * n + h
                    dve.wait_ge(silu_done, i + 1)
                    if n >= 2:
                        dve.wait_ge(down_done, n - 1)
                    nc.vector.tensor_tensor(hT[n % 2][:, h * NC:(h + 1) * NC], sg[h][:, :], pu[h][:, :], ALU.mult)\
                        .then_inc(h_ready, 1)

            def best_of(j):
                for a in range(2):
                    out = nc.vector.max(top[:, a, j, :], R[:, a, j, :])
                link(out)
                for a in range(2):
                    out = nc.vector.max_index(at[:, a, j, :], top[:, a, j, :], R[:, a, j, :])
                link(out)
                link(nc.vector.tensor_copy(atf[:, :, j, :], at[:, :, j, :]))
                first = lambda x: x[:, 0, j, :].rearrange("p (a o) -> p a o", o=1).to_broadcast([P, F1_TOP, F1_TOP])
                second = lambda x: x[:, 1, j, :].rearrange("p (o b) -> p o b", o=1).to_broadcast([P, F1_TOP, F1_TOP])
                nc.vector.tensor_tensor(sums[:, :, :], first(top), second(top), ALU.add)
                link(nc.vector.scalar_tensor_tensor(out=which[:, :, :], in0=first(atf), scalar=float(F1_KEYS),
                                                    in1=second(atf), op0=ALU.mult, op1=ALU.add))
                flat = lambda x: x[:, :, :].rearrange("p a b -> p (a b)")
                nc.vector.max(best[:, j, :], flat(sums))
                link(nc.vector.tensor_scalar(flat(which), flat(which), float(F1_E - 1), None, ALU.min))
                link(nc.vector.max_index(bat[:, :], best[:, j, :], flat(sums)))
                link(nc.vector.tensor_copy(batf[:, :], bat[:, :]))
                link(nc.vector.tensor_tensor(sel[:, :, :],
                                             iota[:, 0:F1_KEYS].rearrange("p (o n) -> p o n", o=1).to_broadcast([P, F1_TOP, F1_KEYS]),
                                             batf[:, :].rearrange("p (c o) -> p c o", o=1).to_broadcast([P, F1_TOP, F1_KEYS]),
                                             ALU.is_equal))
                link(nc.vector.tensor_tensor(sel[:, :, :], sel[:, :, :],
                                             flat(which).rearrange("p (o n) -> p o n", o=1).to_broadcast([P, F1_TOP, F1_KEYS]),
                                             ALU.mult))
                link(nc.vector.tensor_reduce(expert[:, j, :], sel[:, :, :], AX.X, ALU.add))

            def spread_weights(j):
                for c in range(F1_TOP):
                    out = PW[:, j, :] if c == 0 else hotv[c % 2][:, :]
                    link(nc.vector.tensor_scalar(out, iota[:, :], expert[:, j, c:c + 1], ex[:, j, c:c + 1],
                                                 ALU.is_equal, ALU.mult))
                    if c:
                        link(nc.vector.tensor_tensor(PW[:, j, :], PW[:, j, :], hotv[c % 2][:, :], ALU.add))
                dve.sem_inc(built, 1)

            dve.wait_ge(routed, 1)
            for a in range(2):
                out = nc.vector.tensor_copy(R[:, a, :, :], acc[a][:, :].rearrange("p (t n) -> p t n", t=NT))
            out.then_inc(R_ready, 1)
            dve.wait_ge(R_ready, 1)
            for j in range(NT):
                best_of(j)
                if j % 2 == 1:
                    gate_times_up(j // 2)
            nc.vector.tensor_tensor(ex[:, :, :], best[:, :, :], best[:, :, 0:1].to_broadcast([P, NT, F1_TOP]),
                                    ALU.subtract).then_inc(best_ready, 1)
            dve.wait_ge(ex_ready, 1)
            link(nc.vector.tensor_reduce(tot[:, :, 0], ex[:, :, :], AX.X, ALU.add))
            link(nc.vector.reciprocal(tot[:, :, 1], tot[:, :, 0]))
            nc.vector.tensor_tensor(ex[:, :, :], ex[:, :, :], tot[:, :, 1:2].to_broadcast([P, NT, F1_TOP]),
                                    ALU.mult).then_inc(mix_ready, 1)
            dve.wait_ge(mix_ready, 1)
            for n in range(4, F1_GT):
                gate_times_up(n)
                for j in DVE_TILES[(n - 4) * len(DVE_TILES) // 4:(n - 3) * len(DVE_TILES) // 4]:
                    spread_weights(j)
            for n in range(F1_GT, TILES):
                gate_times_up(n)
            dve.wait_ge(down_done, TILES)
            for a in range(4):
                nc.vector.tensor_tensor(k.x[:, 2 * a:2 * a + 2, :], acc[a][:, :].rearrange("p (t n) -> p t n", t=2),
                                        k.x[:, 2 * a:2 * a + 2, :], ALU.add).then_inc(added, 1)
            dve.wait_ge(added, 4)

        @block.tensor
        def _(pe):
            pe.wait_ge(loaded, 64)
            on_tensor(pe)
            for s in range(2):
                for half in range(NH2):
                    for d in range(KD):
                        out = nc.tensor.matmul(acc[2 * s + half][0:F1_R, :], wq[:, d, s * F1_R:(s + 1) * F1_R],
                                               k.xT[:, d, half * NC:(half + 1) * NC], start=(d == 0), stop=(d == KD - 1))
                    out.then_inc(queried, 1)

            def gate_up(n):
                pe.wait_ge(w_in[n % 3], 16 * (n // 3 + 1))
                if n == F1_GT:
                    pe.wait_ge(built, len(DVE_TILES))
                    pe.wait_ge(pool_built, len(POOL_TILES))
                for h in range(2):
                    if n >= 1:
                        pe.wait_ge(h_ready, 2 * n + h - 1)
                    for d in range(KD):
                        out = nc.tensor.matmul(pg[h][:, :], w[n % 3][:, d * P:(d + 1) * P],
                                               k.xT[:, d, h * NC:(h + 1) * NC], start=(d == 0), stop=(d == KD - 1))
                    if n < F1_GT:
                        for d in range(KD):
                            out = nc.tensor.matmul(pu[h][:, :], w[n % 3][:, D + d * P:D + (d + 1) * P],
                                                   k.xT[:, d, h * NC:(h + 1) * NC], start=(d == 0), stop=(d == KD - 1))
                    else:
                        e = n - F1_GT
                        for t in range(4):
                            out = nc.tensor.transpose(pu[h][:, t * P:(t + 1) * P],
                                                      PW[:, 4 * h + t, e * P:(e + 1) * P], k.ident[:, :])
                    out.then_inc(gated, 1)

            def down(n):
                for h in range(2):
                    pe.wait_ge(h_ready, 2 * n + h + 1)
                    for t in range(h * NT // 2, (h + 1) * NT // 2):
                        out = nc.tensor.matmul(acc[t // 2][:, (t % 2) * D:(t % 2 + 1) * D],
                                               hT[n % 2][:, t * P:(t + 1) * P], w[n % 3][:, 2 * D:3 * D],
                                               start=False, stop=(n == TILES - 1), skip_group_check=True)
                out.then_inc(down_done, 1)

            pe.wait_ge(QI_ready, 4)
            for a in range(2):
                for j in range(NT):
                    rows_n = QI[:, a * NC + j * (P // 2):a * NC + (j + 1) * (P // 2), :].rearrange("r t s -> r (t s)")
                    out = nc.tensor.matmul(acc[a][:, j * F1_KEYS:(j + 1) * F1_KEYS], rows_n, keys[:, a, :],
                                           start=True, stop=True)
            out.then_inc(routed, 1)
            gate_up(0)
            pe.wait_ge(R_ready, 1)
            pe.wait_ge(zero_set, 1)
            for a in range(4):
                nc.tensor.matmul(acc[a][:, :], zeros[:, 0:P], zeros[:, :], start=True, stop=False, skip_group_check=True)
            for n in range(1, TILES):
                gate_up(n)
                down(n - 1)
            down(TILES - 1)
    k.ident_loaded = True


def load_x(nc, k, src):
    with ExitStack() as ctx:
        block = ctx.enter_context(nc.Block())

        @block.sync
        def _(sp):
            xr = src["x"].rearrange("(t p) d -> p t d", p=P)
            for t in range(NT):
                sp.dma_start(k.x[:, t, :], xr[:, t, :]).then_inc(k.x_in, 16)
            sp.wait_ge(k.x_in, 16 * NT)


def program(nc, src, out, start=0, stages=6):
    with ExitStack() as ctx:
        k = Kernel(nc, ctx)
        k.x_in = k.sem("x_in")
        k.ident_loaded = False
        subs = [lambda: attention_0(nc, k, src, None), lambda: cross_attention_0(nc, k, src),
                lambda: experts_0(nc, k, src), lambda: attention_1(nc, k, src),
                lambda: retention_1(nc, k, src), lambda: memory_1(nc, k, src)]
        if start:
            load_x(nc, k, src)
        for n, sub in enumerate(subs[start:stages]):
            if n == 3:
                k.clear_semaphores()
            sub()
        store_x(nc, k, out)



def layouts(a):
    f = np.float32
    out = {"x": a["x"].reshape(T, D)}
    out["ident"] = np.eye(P, dtype=f)
    half = A0_D // 2
    inv = 1.0 / 150000.0 ** (np.arange(half, dtype=np.float64) * 2.0 / A0_D)
    ang = (np.arange(S, dtype=f)[:, None] * inv.astype(f)[None, :]).astype(np.float64)
    scale = A0_D ** -0.25
    c, s = (np.cos(ang) * scale).T, (np.sin(ang) * scale).T
    out["a0_cos"] = np.concatenate([c] * 4).astype(f)
    out["a0_sin"] = np.concatenate([s, s, -s, -s]).astype(f)
    i = np.arange(S)
    far = np.abs(i[:, None] - i[None, :]) > A0_WIN
    out["a0_mask"] = np.where(far, MASKED, 0.0).astype(f).reshape(2, P, S).transpose(1, 0, 2).copy()
    slot = (np.arange(P) // 32) % 2
    out["a0_slot"] = np.stack([slot == 0, slot == 1], 1).astype(f)
    out["a0_bo"] = np.broadcast_to(a["L0_attn_bo"], (P, D))

    def pairs(w):
        lead = w.shape[:-2]
        w = w.reshape(*lead, w.shape[-2] // 2, 2, half, 2)
        n = len(lead)
        return w.transpose(*range(n), n, n + 3, n + 1, n + 2).reshape(*lead, -1, P)

    G = A0_G
    wq = pairs(a["L0_attn_Wq"]).reshape(KD, P, G, A0_PAIRS, P).transpose(2, 1, 0, 3, 4).reshape(G, P, A0_NQ)
    wk = pairs(np.repeat(a["L0_attn_Wk"], 2, axis=1)).reshape(KD, P, G, P).transpose(2, 1, 0, 3).reshape(G, P, A0_NK)
    wv = a["L0_attn_Wv"].reshape(KD, P, G, A0_D).transpose(2, 1, 0, 3).reshape(G, P, A0_NV)
    bq = pairs(a["L0_attn_bq"]).reshape(G, A0_PAIRS, P).transpose(0, 2, 1)
    bk = pairs(np.repeat(a["L0_attn_bk"], 2, axis=0)).reshape(G, 1, P).transpose(0, 2, 1)
    sk = np.broadcast_to(a["L0_attn_sinks"].reshape(G, 1, A0_R), (G, P, A0_R))
    bv = np.broadcast_to(a["L0_attn_bv"].reshape(G, 1, A0_D), (G, P, A0_D))
    out["a0_w"] = np.concatenate([wq, wk, wv, bq, bk, sk, bv], axis=2)
    out["a0_wo"] = a["L0_attn_Wo"].reshape(G, 2, P, D).transpose(0, 2, 1, 3)
    both = lambda v: np.broadcast_to(np.asarray(v), (P, v.shape[-1]))
    fm = lambda wt: wt.T.reshape(KD, P, -1).transpose(1, 0, 2)
    out["x0_w"] = np.stack([fm(a["L0_xattn_" + n]) for n in ("Wq", "Wk", "Wv", "Wo")], axis=1)
    out["ctxT"] = a["ctx_2048"].reshape(T, KD, P).transpose(2, 1, 0)
    out["x0_rows"] = np.stack([both(a["L0_xattn_" + n]) for n in ("bv", "bo", "ln_gamma", "ln_beta")], axis=1)
    out["x0_cols"] = np.concatenate([a["L0_xattn_bq"].reshape(KD, P).T, a["L0_xattn_bk"].reshape(KD, P).T], axis=1)
    out["x0_hmask"] = (np.arange(P)[:, None] // X0_D == np.arange(X0_HM)[None, :]).astype(f) * f(X0_D ** -0.5)
    out["x0_rs"] = np.broadcast_to(a["L0_xattn_residual_scale"].reshape(1, 1), (P, 1))
    out["x0_mask"] = a["mask_BxS2_ik0"].reshape(B, 2, P).transpose(2, 0, 1).reshape(P, NT)
    gate = np.concatenate([a["L0_ffn_gate_up_proj"][:, :M0_I].reshape(-1, D), a["L0_ffn_sh_gate_w"]])
    up = np.concatenate([a["L0_ffn_gate_up_proj"][:, M0_I:].reshape(-1, D), a["L0_ffn_sh_up_w"]])
    down = np.concatenate([a["L0_ffn_down_proj"].transpose(0, 2, 1).reshape(-1, D), a["L0_ffn_sh_down_w"].T])
    fill = np.zeros((M0_TILES * P - gate.shape[0], D), f)
    tiled = lambda wt: np.concatenate([wt, fill]).reshape(M0_TILES, P, KD, P).transpose(0, 3, 2, 1).reshape(M0_TILES, P, D)
    out["m0_w"] = np.concatenate([tiled(gate), tiled(up), np.concatenate([down, fill]).reshape(M0_TILES, P, D)], axis=2)
    out["m0_rw"] = fm(np.concatenate([a["L0_ffn_router_weight"], a["L0_ffn_shared_gate_w"]]))
    out["m0_iota"] = np.broadcast_to(np.arange(M0_E, dtype=f), (P, M0_E))
    half = P // 2
    inv = (1.0 / 10000.0 ** (np.arange(0, P, 2, dtype=f) / P)).astype(f)
    ang = (np.arange(S, dtype=f)[:, None] * inv[None, :]).astype(np.float64)
    c, s = np.cos(ang).T, np.sin(ang).T
    tabs = []
    for scale in (P ** -0.5, 1.0):
        tabs += [np.concatenate([c, c]) * scale, np.concatenate([s, -s]) * scale]
    out["a1_cs"] = np.stack(tabs, axis=1).astype(f)
    above = np.where(np.arange(P)[None, :] > np.arange(P)[:, None], -1.0e30, 0.0).astype(f)
    out["a1_mask"] = np.concatenate([above, np.zeros((P, P), f), above], axis=1)
    out["a1_rows"] = np.stack([both(a["L1_attn_" + n]) for n in ("ln_g", "ln_b", "bo")], axis=1)
    hw = lambda wt: wt.reshape(A1_H, P, KD, P).transpose(0, 3, 2, 1).reshape(A1_H, P, KD * P)
    hb = lambda bb: bb.reshape(A1_H, P, 1)
    out["a1_w"] = np.concatenate([hw(a["L1_attn_" + n]) for n in ("wq", "wk", "wv")]
                                 + [hb(a["L1_attn_" + n]) for n in ("bq", "bk")], axis=2)
    bv = np.broadcast_to(a["L1_attn_bv"].reshape(A1_H, 1, P), (A1_H, P, P))
    out["a1_wo"] = np.concatenate([a["L1_attn_wo"].T.reshape(A1_H, P, D), bv], axis=2)
    out["x1_wh"] = a["L1_xattn_Wh"].transpose(1, 0, 2)
    rowm = lambda wt: wt.reshape(-1, P, wt.shape[1]).transpose(1, 0, 2)
    out["x1_wg"], out["x1_wo"] = rowm(a["L1_xattn_wg_w"]), rowm(a["L1_xattn_wo_w"])
    out["x1_rows"] = np.stack([both(a["L1_xattn_" + n]) for n in ("gn_gamma", "gn_beta")], axis=1)
    gam = (1.0 - 2.0 ** (-5.0 - np.arange(X1_H, dtype=f))).astype(f).astype(np.float64)
    ex = np.arange(S)[None, :] - np.arange(S)[:, None]
    dec = np.where(ex[None] <= 0, gam[:, None, None] ** ex[None], 0.0)
    dec = dec / np.sqrt(dec.sum(-1))[:, None, :] / np.sqrt(P)
    dT = dec.transpose(2, 0, 1).reshape(2, P, X1_H, S)
    out["x1_decay"] = np.concatenate([dT[0], dT[1][:, :, P:]], axis=2).astype(f)
    out["f1_wq"] = rowm(a["L1_ffn_W_q"])
    out["f1_keys"] = a["L1_ffn_keys"].transpose(1, 0, 2)
    out["f1_iota"] = np.broadcast_to(np.arange(F1_E, dtype=f), (P, F1_E))
    tl = lambda wt: wt.reshape(-1, P, KD, P).transpose(0, 3, 2, 1).reshape(-1, P, D)
    de, ue = a["L1_ffn_down_embed"], a["L1_ffn_up_embed"]
    up = np.concatenate([tl(a["L1_ffn_up_w"].T), np.zeros((F1_ET, P, D), f)])
    out["f1_w"] = np.concatenate([tl(np.concatenate([a["L1_ffn_gate_w"].T, de])), up,
                                  np.concatenate([a["L1_ffn_down_w"], ue]).reshape(-1, P, D)], axis=2)
    return {n: np.ascontiguousarray(v) for n, v in out.items()}


def kernel(**inputs):
    import concourse.bacc as bacc
    from concourse.bass_utils import run_bass_kernel_spmd

    arrays = layouts({n: np.asarray(v) for n, v in inputs.items()})
    nc = bacc.Bacc("TRN2", target_bir_lowering=False, num_devices=1)
    src = {n: nc.dram_tensor(n, v.shape, mybir.dt.from_np(v.dtype), kind="ExternalInput").ap()
           for n, v in arrays.items()}
    out = nc.dram_tensor("out", (T, D), F32, kind="ExternalOutput").ap()
    program(nc, src, out)
    got = run_bass_kernel_spmd(nc, [arrays], core_ids=[0])
    return got.results[0]["out"].reshape(B, S, D)
```

```python
from contextlib import ExitStack

import numpy as np

import concourse.bass as bass
import concourse.mybir as mybir
from concourse.alu_op_type import AluOpType as ALU

F32 = mybir.dt.float32
BF16 = mybir.dt.bfloat16
U32 = mybir.dt.uint32
ACT = mybir.ActivationFunctionType
AX = mybir.AxisListType

P = 128
B, S, D = 4, 256, 256
T = B * S
NT = T // P
KD = D // P
NC = 512
NH2 = T // NC
LN_EPS = 1e-5

A0_G, A0_R, A0_D, A0_WIN = 8, 4, 64, 128
A0_PAIRS = A0_R // 2
A0_NQ = KD * A0_PAIRS * P
A0_NK = KD * P
A0_NB = A0_PAIRS + 1 + A0_R
A0_W = A0_NQ + A0_NK + A0_NB
A0_U = B * 2 * A0_PAIRS
MASKED = -1.0e9

A1_H = 16
A1_W = 3 * KD * P + 2
A1_U = B


AHEAD = {
    "a0": [("ident", [P, P], F32), ("a0_cos", [P, S], F32), ("a0_sin", [P, S], F32), ("a0_mask", [P, 2, S], F32),
           ("a0_slot", [P, 2], F32), ("a0_bo", [P, D], F32)],
    "x0": [("ctxT", [P, KD, T], F32), ("x0_w", [P, 4, KD, D], F32), ("x0_rows", [P, 4, D], F32),
           ("x0_cols", [P, 4], F32), ("x0_hmask", [P, 8], F32), ("x0_rs", [P, 1], F32),
           ("x0_mask", [P, NT], mybir.dt.int32)],
    "m0": [("m0_rw", [P, KD, 9], F32), ("m0_iota", [P, 8], F32)]
          + [(f"m0_gu{i}", [P, 2 * D], F32) for i in range(2)] + [(f"m0_dn{i}", [P, D], F32) for i in range(2)],
    "a1": [("a1_rows", [P, 3, D], F32), ("a1_cs", [P, 4, S], F32), ("a1_mask", [P, 3 * P], F32)]
          + [(f"a1_w{i}", [P, A1_W], F32) for i in range(2)] + [(f"a1_wo{i}", [P, D + P], F32) for i in range(2)],
    "x1": [("x1_wh", [P, 2, P], F32), ("x1_wg", [P, KD, D], F32), ("x1_wo", [P, KD, D], F32),
           ("x1_decay", [P, 2, 3 * P], F32), ("x1_rows", [P, 2, D], F32)],
    "f1": [("f1_wq", [P, KD, P], F32), ("f1_keys", [64, 2, 64], F32), ("f1_iota", [P, 512], F32)]
          + [(f"f1_w{i}", [P, 3 * D], F32) for i in range(3)],
}


class Kernel:

    def __init__(self, nc, ctx):
        self.nc, self.sems = nc, []
        self.x = self.sb(ctx, "x", [P, NT, D])
        self.xn = self.sb(ctx, "xn", [P, NT, D])
        self.xT = self.sb(ctx, "xT", [P, KD, T])
        self.stats = self.sb(ctx, "stats", [P, NT, 6])
        self.mv = self.sb(ctx, "mv", [P, NT, 2])
        self.rstd = self.sb(ctx, "rstd", [P, NT])
        self.ve = self.sb(ctx, "ve", [P, NT])
        self.minus_half = self.sb(ctx, "minus_half", [P, NT])

        self.tile, self.arrived = {}, {}
        for group, tiles in AHEAD.items():
            self.arrived[group] = nc.alloc_semaphore(name=group + "_arrived")
            for name, shape, dt in tiles:
                self.tile[name] = self.sb(ctx, name, shape, dt)

    def fetch(self, eng, src, *groups):
        for group in groups:
            for name, shape, _ in AHEAD[group]:
                tile = self.tile[name]
                where = src[name] if name in src else src[name[:-1]][int(name[-1])]
                eng.dma_start(tile[tuple([slice(None)] * len(shape))], where).then_inc(self.arrived[group], 16)

    def wait(self, eng, group):
        eng.wait_ge(self.arrived[group], 16 * len(AHEAD[group]))

    def sb(self, ctx, name, shape, dt=F32):
        return ctx.enter_context(self.nc.sbuf_tensor("sb_" + name, shape, dt))

    def ps(self, ctx, name, n=NC):
        return ctx.enter_context(self.nc.psum_tensor(name, [P, n], F32))

    def sem(self, name):
        s = self.nc.alloc_semaphore(name=name)
        self.sems.append(s)
        return s

    def clear_semaphores(self):
        self.nc.clear_and_free_semaphores(self.sems)
        self.nc.all_engine_barrier()
        self.sems = []


def spread(column, *dims):
    p = column.shape[0]
    if len(dims) == 1:
        return column.to_broadcast([p, dims[0]])
    return column.rearrange("p (o n) -> p o n", o=1).to_broadcast([p, *dims])


def norm_rows(nc, dve, k, src, dst, done, rstd_ready, turn, out_sem):
    base = turn * 2 * NT
    for t in range(NT):
        nc.vector.bn_stats(k.stats[:, t, :], src[:, t, :]).then_inc(done, 1)
    dve.wait_ge(done, base + NT)
    for t in range(NT):
        nc.vector.bn_aggr(k.mv[:, t, :], k.stats[:, t, :]).then_inc(done, 1)
    dve.wait_ge(rstd_ready, 3 * turn + 3)
    for t in range(NT):
        nc.vector.tensor_scalar(dst[:, t, :], src[:, t, :], k.mv[:, t, 0:1], k.rstd[:, t:t + 1],
                                ALU.subtract, ALU.mult).then_inc(out_sem, 1)


def inverse_root(nc, pool, k, done, rstd_ready, turn, eps=LN_EPS):
    pool.wait_ge(done, (turn + 1) * 2 * NT)
    nc.gpsimd.tensor_scalar(k.ve[:, :], k.mv[:, :, 1], eps, None, ALU.add).then_inc(rstd_ready, 1)
    pool.wait_ge(rstd_ready, 3 * turn + 1)
    nc.gpsimd.memset(k.minus_half[:, :], -0.5).then_inc(rstd_ready, 1)
    pool.wait_ge(rstd_ready, 3 * turn + 2)
    nc.gpsimd.tensor_tensor(k.rstd[:, :], k.ve[:, :], k.minus_half[:, :], ALU.pow).then_inc(rstd_ready, 1)


def turn_rows(nc, pe, k, banks, xn_ready, base, turned):
    per = NC // P
    for h in range(NH2):
        for t in range(per):
            pe.wait_ge(xn_ready, base + h * per + t + 1)
            for d in range(KD):
                last = nc.tensor.transpose(banks[d * NH2 + h][:, t * P:(t + 1) * P],
                                           k.xn[:, h * per + t, d * P:(d + 1) * P], k.tile["ident"][:, :])
        last.then_inc(turned, 1)


def attention_0(nc, k, src):
    with ExitStack() as ctx:
        sb = lambda name, shape, dt=F32: k.sb(ctx, "a0_" + name, shape, dt)
        w = [sb(f"w{i}", [P, A0_W]) for i in range(2)]
        wo = [sb(f"wo{i}", [P, KD, D]) for i in range(2)]
        wv = sb("wv", [P, KD, A0_G * A0_D])
        bv = sb("bv", [P, A0_G * A0_D])
        cosq, sinq, wmask, slotm, bo = (k.tile["a0_" + n] for n in ("cos", "sin", "mask", "slot", "bo"))
        qT = [[sb(f"qT{i}{j}", [P, T]) for j in range(A0_PAIRS)] for i in range(2)]
        kz = [sb(f"kz{i}", [P, B, 2, S]) for i in range(2)]
        kr = sb("kr", [P, 2, S])
        v = sb("v", [P, A0_G, NT, A0_D + 1])
        t1 = [sb(f"t1{i}", [P, 2, S]) for i in range(2)]
        t2 = [sb(f"t2{i}", [P, 2, S]) for i in range(2)]
        nsink = [sb(f"nsink{i}", [P, A0_R]) for i in range(2)]
        nS = [sb(f"nS{i}", [P, 2, S]) for i in range(2)]
        nm = [sb(f"nm{i}", [P, A0_R]) for i in range(4)]
        Pm = [sb(f"Pm{i}", [P, 2, S]) for i in range(4)]
        PT = [sb(f"PT{i}", [P, 2, 2, P]) for i in range(2)]
        ds = sb("ds", [P, 2, A0_R])
        es = [sb(f"es{i}", [P, A0_R]) for i in range(4)]
        den = sb("den", [P, 2, A0_R])
        O = [sb(f"O{i}", [P, A0_R, A0_D]) for i in range(2)]
        OT = [sb(f"OT{i}", [P, 2, P]) for i in range(2)]
        pp = k.ps(ctx, "a0_pp")
        pS = [k.ps(ctx, f"a0_pS{i}") for i in range(2)]
        pT = k.ps(ctx, "a0_pT")
        pO = [k.ps(ctx, f"a0_pO{i}") for i in range(2)]
        pOT = k.ps(ctx, "a0_pOT")
        pY = k.ps(ctx, "a0_pY")
        turn_banks = [pS[0], pS[1], pT, pOT]
        v_banks = [pS[0], pS[1], pO[0], pO[1]]

        sem = lambda name: k.sem("a0_" + name)
        wv_in, w_in, wo_in = sem("wv_in"), [sem("w_in0"), sem("w_in1")], [sem("wo_in0"), sem("wo_in1")]
        ln, xn_ready, turned, xT_ready = sem("ln"), sem("xn_ready"), sem("turned"), sem("xT_ready")
        proj, proj_used, roped, chunk = sem("proj"), sem("proj_used"), sem("roped"), sem("chunk")
        kr_done, valued, v_ready, ns_ready = sem("kr_done"), sem("valued"), sem("v_ready"), sem("ns_ready")
        scored, maxed, probs, turnedP, PT_ready = (sem("scored"), sem("maxed"), sem("probs"),
                                                   sem("turnedP"), sem("PT_ready"))
        pvd, shifted, es_ready, den_ready, O_ready = (sem("pvd"), sem("shifted"), sem("es_ready"),
                                                      sem("den_ready"), sem("O_ready"))
        turnedO, OT_ready, projected, added = sem("turnedO"), sem("OT_ready"), sem("projected"), sem("added")
        bo_in, ones_set, rstd_ready, gate = sem("bo_in"), sem("ones_set"), sem("rstd_ready"), sem("gate")

        NCH = 6
        CH_AT = {0: 0, 2: 1, 4: 2, 6: 3, 8: 4, 10: 5}

        def groups(eng, first, step, last):
            first()
            with eng.Fori(0, (A0_G - 2) // 2) as i:
                for s in range(2):
                    step(i * 2 + (1 + s), (1 + s) % 2)
            last()

        def halves(G, par):
            if isinstance(G, int):
                return 16 * (G // 2 + 1)
            return G * 8 + (16 - 8 * par)

        block = ctx.enter_context(nc.Block())

        @block.sync
        def _(sp):
            xr = src["x"].rearrange("(t p) d -> p t d", p=P)
            for t in range(NT):
                sp.dma_start(k.x[:, t, :], xr[:, t, :]).then_inc(k.x_in, 16)
            k.fetch(sp, src, "a0")
            sp.dma_start(w[0][:, :], src["a0_w"][0]).then_inc(w_in[0], 16)
            sp.dma_start(wv[:, :, :], src["a0_wv"]).then_inc(wv_in, 16)
            sp.dma_start(bv[:, :], src["a0_bv"]).then_inc(wv_in, 16)
            sp.dma_start(wo[0][:, :, :], src["a0_wo"][0]).then_inc(wo_in[0], 16)
            sp.dma_start(w[1][:, :], src["a0_w"][1]).then_inc(w_in[1], 16)
            sp.dma_start(wo[1][:, :, :], src["a0_wo"][1]).then_inc(wo_in[1], 16)
            k.fetch(sp, src, "x0", "m0")
            with sp.Fori(0, (A0_G - 2) // 2) as i:
                for s in range(2):
                    g = i * 2 + (2 + s)
                    sp.wait_ge(ns_ready, g - 1)
                    sp.dma_start(w[s][:, :], src["a0_w"][bass.ds(g, 1)].rearrange("g p n -> p (g n)"))\
                        .then_inc(w_in[s], 16)
                    sp.wait_ge(added, (g - 1) * NT)
                    sp.dma_start(wo[s][:, :, :], src["a0_wo"][bass.ds(g, 1)].rearrange("g p c n -> p (g c) n"))\
                        .then_inc(wo_in[s], 16)

        @block.gpsimd
        def _(pool):
            nc.gpsimd.memset(v[:, :, :, A0_D:A0_D + 1], 1.0).then_inc(ones_set, 1)
            inverse_root(nc, pool, k, ln, rstd_ready, 0)

            def project(G, par, c):
                pool.wait_ge(roped, G * 6 + c + 1)
                if c < 4:
                    half = c % 2
                    nc.gpsimd.tensor_tensor(qT[par][c // 2][:, half * NC:(half + 1) * NC],
                                            t1[c % 2][:, :, :].rearrange("p b s -> p (b s)"),
                                            t2[c % 2][:, :, :].rearrange("p b s -> p (b s)"),
                                            ALU.add).then_inc(chunk, 1)
                else:
                    half = c - 4
                    pool.wait_ge(chunk, G * NCH + c)
                    nc.gpsimd.tensor_tensor(kr[:, :, :], t1[c % 2][:, :, :], t2[c % 2][:, :, :],
                                            ALU.add).then_inc(kr_done, 1)
                    k.wait(pool, "a0")
                    pool.wait_ge(kr_done, G * 2 + half + 1)
                    for slot in range(2):
                        out = nc.gpsimd.tensor_tensor(kz[par][:, 2 * half:2 * half + 2, slot, :], kr[:, :, :],
                                                      spread(slotm[:, slot:slot + 1], 2, S), ALU.mult)
                    out.then_inc(chunk, 1)

            def next_chunks(G, par):
                for c in range(NCH):
                    project(G, par, c)

            next_chunks(0, 0)
            next_chunks(1, 1)
            with pool.Fori(0, (A0_G - 2) // 2) as i:
                for s in range(2):
                    next_chunks(i * 2 + (2 + s), s)

        @block.scalar
        def _(act):
            for j in range(4):
                act.wait_ge(turned, (j % NH2) + 1)
                nc.scalar.copy(k.xT[:, j // NH2, (j % NH2) * NC:(j % NH2 + 1) * NC],
                               turn_banks[j][:, :]).then_inc(xT_ready, 1)

            def exps(G, par, u):
                U = G * A0_U + u
                act.wait_ge(maxed, U + 1)
                if not (isinstance(G, int) and G == 0 and u < 4):
                    act.wait_ge(turnedP, U - 3)
                for h in range(2):
                    out = nc.scalar.activation(Pm[u % 4][:, h, :], nS[u % 2][:, h, :], ACT.Exp,
                                               bias=nm[(u // 2) % 4][:, 2 * (u % 2) + h:2 * (u % 2) + h + 1],
                                               scale=-1.0)
                out.then_inc(probs, 1)

            def evac_PT(G, u):
                U = G * A0_U + u
                act.wait_ge(turnedP, U + 1)
                nc.scalar.copy(PT[u % 2][:, :, :, :].rearrange("p h c q -> p (h c q)"), pT[:, :])\
                    .then_inc(PT_ready, 1)

            def sink_exps(G, j):
                act.wait_ge(shifted, G * NT + j + 1)
                nc.scalar.activation(es[j % 4][:, :], ds[:, j % 2, :], ACT.Exp).then_inc(es_ready, 1)

            def evac_OT(G, j):
                act.wait_ge(turnedO, G * NT + j + 1)
                nc.scalar.copy(OT[j % 2][:, :, :].rearrange("p c q -> p (c q)"), pOT[:, 0:2 * P])\
                    .then_inc(OT_ready, 1)

            def body(G, par, first=False):
                for u in range(A0_U):
                    exps(G, par, u)
                    lag(G, u, first)

            def lag(G, u, first):
                v2, g2 = (u - 2) % A0_U, G if u >= 2 else G - 1
                if u >= 2 or not first:
                    evac_PT(g2, v2)
                if u % 2 == 1:
                    sink_exps(G, u // 2)
                if u % 2 == 0 and (u >= 6 or not first):
                    evac_OT(G if u >= 6 else G - 1, (u // 2 - 3) % NT)

            groups(act, lambda: body(0, 0, True), body, lambda: body(A0_G - 1, 1))
            for u in range(A0_U, A0_U + 6):
                if u < A0_U + 2:
                    evac_PT(A0_G - 1, u - 2)
                if u % 2 == 0:
                    evac_OT(A0_G - 1, u // 2 - 3)

        @block.vector
        def _(dve):
            dve.wait_ge(k.x_in, 16 * NT)
            norm_rows(nc, dve, k, k.x, k.xn, ln, rstd_ready, 0, xn_ready)
            k.wait(dve, "a0")
            dve.wait_ge(xn_ready, NT)
            for t in range(NT):
                nc.vector.tensor_tensor(k.x[:, t, :], k.x[:, t, :], bo[:, :], ALU.add).then_inc(bo_in, 1)
            dve.wait_ge(bo_in, NT)

            def rope(G, par, c):
                n = c % 2
                bias = w[par][:, A0_W - A0_NB + c // 2:A0_W - A0_NB + c // 2 + 1]
                dve.wait_ge(w_in[par], halves(G, par))
                dve.wait_ge(proj, G * NCH + c + 1)
                if not (isinstance(G, int) and G == 0 and c < 2):
                    dve.wait_ge(chunk, G * NCH + (c - 1))
                a = pp[:, :].rearrange("p (b s) -> p b s", b=2)
                lo, hi = slice(0, 64), slice(64, 128)
                cs = lambda tab, rows: tab[rows, :].rearrange("p (o s) -> p o s", o=1).to_broadcast([rows.stop - rows.start, 2, S])
                nc.vector.scalar_tensor_tensor(out=t1[n][:, :, :], in0=a, scalar=bias,
                                               in1=cs(cosq, slice(0, 128)), op0=ALU.add, op1=ALU.mult)
                nc.vector.scalar_tensor_tensor(out=t2[n][lo, :, :], in0=a[hi], scalar=bias[hi],
                                               in1=cs(sinq, hi), op0=ALU.add, op1=ALU.mult)
                nc.vector.scalar_tensor_tensor(out=t2[n][hi, :, :], in0=a[lo], scalar=bias[lo],
                                               in1=cs(sinq, lo), op0=ALU.add, op1=ALU.mult).then_inc(roped, 1)

            def values(t):
                dve.wait_ge(valued, t + 1)
                nc.vector.tensor_tensor(v[:, :, t, 0:A0_D], v_banks[t % 4][:, :].rearrange("p (g n) -> p g n", g=A0_G),
                                        bv[:, :].rearrange("p (g n) -> p g n", g=A0_G), ALU.add).then_inc(v_ready, 1)

            def sinks(G, par):
                if not (isinstance(G, int) and G < 2):
                    dve.wait_ge(ns_ready, G)
                sink = A0_W - A0_R
                nc.vector.tensor_scalar(nsink[par][:, :], w[par][:, sink:sink + A0_R], -1.0, None,
                                        ALU.mult).then_inc(ns_ready, 1)

            def maxima(G, par, u):
                U, j = G * A0_U + u, u // 2
                k.wait(dve, "a0")
                dve.wait_ge(scored, U + 1)
                if u == 0:
                    dve.wait_ge(ns_ready, G + 1)
                if not (isinstance(G, int) and G == 0 and u < 2):
                    dve.wait_ge(probs, U - 1)
                dve.sem_inc(gate, 1)
                for h in range(2):
                    c = 2 * (u % 2) + h
                    out = nc.vector.tensor_tensor_reduce(
                        nS[u % 2][:, h, :], pS[u % 2][:, h * S:(h + 1) * S], wmask[:, j % 2, :], -1.0,
                        nsink[par][:, c:c + 1], ALU.add, ALU.min, nm[j % 4][:, c:c + 1])
                out.then_inc(maxed, 1)

            def shift(G, par, j):
                dve.wait_ge(maxed, G * A0_U + 2 * j + 2)
                if not (isinstance(G, int) and G == 0 and j < 2):
                    dve.wait_ge(es_ready, G * NT + j - 1)
                nc.vector.tensor_tensor(ds[:, j % 2, :], nm[j % 4][:, :], nsink[par][:, :], ALU.subtract)\
                    .then_inc(shifted, 1)

            def outputs(G, j):
                dve.wait_ge(pvd, G * A0_U + 2 * j + 2)
                dve.wait_ge(es_ready, G * NT + j + 1)
                o = pO[j % 2][:, 0:A0_R * (A0_D + 1)].rearrange("p (h n) -> p h n", h=A0_R)
                nc.vector.tensor_tensor(den[:, 0, :], o[:, :, A0_D], es[j % 4][:, :], ALU.add).then_inc(den_ready, 1)
                dve.wait_ge(den_ready, (G * NT + j) * 2 + 1)
                nc.vector.reciprocal(den[:, 1, :], den[:, 0, :]).then_inc(den_ready, 1)
                dve.wait_ge(den_ready, (G * NT + j) * 2 + 2)
                if not (isinstance(G, int) and G == 0 and j < 2):
                    dve.wait_ge(turnedO, G * NT + j - 1)
                nc.vector.tensor_tensor(O[j % 2][:, :, :], o[:, :, 0:A0_D],
                                        den[:, 1, :].rearrange("p (h o) -> p h o", o=1).to_broadcast([P, A0_R, A0_D]),
                                        ALU.mult).then_inc(O_ready, 1)

            def add_y(G, j):
                dve.wait_ge(projected, G * NT + j + 1)
                if not (isinstance(G, int) and G == 0):
                    dve.wait_ge(added, G * NT + j)
                nc.vector.tensor_tensor(k.x[:, j, :], pY[:, 0:D], k.x[:, j, :], ALU.add).then_inc(added, 1)

            def body(G, par, first=False, last=False):
                for u in range(A0_U):
                    maxima(G, par, u)
                    if u % 2 == 1:
                        shift(G, par, u // 2)
                    if u % 2 == 0 and (u >= 4 or not first):
                        outputs(G if u >= 4 else G - 1, (u // 2 - 2) % NT)
                    if u % 2 == 1 and (u >= 7 or not first):
                        add_y(G if u >= 7 else G - 1, ((u - 1) // 2 - 3) % NT)
                    if u in CH_AT and not last:
                        rope(G + 1, 1 - par, CH_AT[u])
                    if u == 13 and not last:
                        sinks(G + 1, 1 - par)

            dve.wait_ge(wv_in, 32)
            for t in range(NT):
                if t < NCH:
                    rope(0, 0, t)
                values(t)
            sinks(0, 0)
            groups(dve, lambda: body(0, 0, True), body, lambda: body(A0_G - 1, 1, last=True))
            for u in range(A0_U, A0_U + 8):
                if u % 2 == 0 and u // 2 - 2 < NT:
                    outputs(A0_G - 1, u // 2 - 2)
                if u % 2 == 1 and (u - 1) // 2 - 3 < NT:
                    add_y(A0_G - 1, (u - 1) // 2 - 3)
            dve.wait_ge(added, A0_G * NT)

        @block.tensor
        def _(pe):
            k.wait(pe, "a0")
            turn_rows(nc, pe, k, turn_banks, xn_ready, 0, turned)
            pe.wait_ge(xT_ready, 4)

            def chunk_of(G, par, c):
                if c == 0:
                    pe.wait_ge(w_in[par], halves(G, par))
                if not (isinstance(G, int) and G == 0 and c == 0):
                    pe.wait_ge(roped, G * NCH + c)
                col = (c // 2) * P if c < 4 else 0
                half = c % 2
                for d in range(KD):
                    off = (d * A0_PAIRS * P + col) if c < 4 else (A0_NQ + d * P)
                    out = nc.tensor.matmul(pp[:, :], w[par][:, off:off + P],
                                           k.xT[:, d, half * NC:(half + 1) * NC],
                                           start=(d == 0), stop=(d == KD - 1))
                out.then_inc(proj, 1)

            def values_of(t):
                if t >= 4:
                    pe.wait_ge(v_ready, t - 3)
                for d in range(KD):
                    out = nc.tensor.matmul(v_banks[t % 4][:, :], k.xT[:, d, t * P:(t + 1) * P], wv[:, d, :],
                                           start=(d == 0), stop=(d == KD - 1))
                out.then_inc(valued, 1)

            def scores(G, par, u):
                U, b, qt, pair = G * A0_U + u, u // 4, (u // 2) % 2, u % 2
                if u == 0:
                    pe.wait_ge(chunk, (G + 1) * NCH)
                if not (isinstance(G, int) and G == 0 and u < 2):
                    pe.wait_ge(maxed, U - 1)
                c = b * S + qt * P
                nc.tensor.matmul(pS[u % 2][:, :], qT[par][pair][:, c:c + P],
                                 kz[par][:, b, :, :].rearrange("p h s -> p (h s)"),
                                 start=True, stop=True).then_inc(scored, 1)

            def values_at(G, t):
                return v[:, G, t, :] if isinstance(G, int) else v[:, bass.ds(G, 1), t, :].rearrange("p g n -> p (g n)")

            def turn_P(G, u):
                U = G * A0_U + u
                pe.wait_ge(probs, U + 1)
                if not (isinstance(G, int) and G == 0 and u < 1):
                    pe.wait_ge(PT_ready, U)
                for h in range(2):
                    for c in range(2):
                        out = nc.tensor.transpose(pT[:, (2 * h + c) * P:(2 * h + c + 1) * P],
                                                  Pm[u % 4][:, h, c * P:(c + 1) * P], k.tile["ident"][:, :])
                out.then_inc(turnedP, 1)

            def weigh(G, par, u):
                U, b, j, pair = G * A0_U + u, u // 4, u // 2, u % 2
                pe.wait_ge(PT_ready, U + 1)
                if pair == 0 and not (isinstance(G, int) and G == 0 and j < 2):
                    pe.wait_ge(O_ready, G * NT + j - 1)
                for h in range(2):
                    c0 = (2 * pair + h) * (A0_D + 1)
                    for c in range(2):
                        out = nc.tensor.matmul(pO[j % 2][:, c0:c0 + A0_D + 1], PT[u % 2][:, h, c, :],
                                               values_at(G, 2 * b + c), start=(c == 0), stop=(c == 1))
                out.then_inc(pvd, 1)

            def turn_O(G, j):
                pe.wait_ge(O_ready, G * NT + j + 1)
                if not (isinstance(G, int) and G == 0 and j < 1):
                    pe.wait_ge(OT_ready, G * NT + j)
                for c in range(2):
                    out = nc.tensor.transpose(pOT[:, c * P:(c + 1) * P],
                                              O[j % 2][:, 2 * c:2 * c + 2, :].rearrange("p h n -> p (h n)"),
                                              k.tile["ident"][:, :])
                out.then_inc(turnedO, 1)

            def project_out(G, par, j):
                if j == 0:
                    pe.wait_ge(wo_in[par], halves(G, par))
                pe.wait_ge(OT_ready, G * NT + j + 1)
                if not (isinstance(G, int) and G == 0 and j < 1):
                    pe.wait_ge(added, G * NT + j)
                for c in range(2):
                    out = nc.tensor.matmul(pY[:, 0:D], OT[j % 2][:, c, :], wo[par][:, c, :],
                                           start=(c == 0), stop=(c == 1))
                out.then_inc(projected, 1)

            def lag(G, par, u, first=False):
                if u >= 2 or not first:
                    turn_P(G if u >= 2 else G - 1, (u - 2) % A0_U)
                if u >= 3 or not first:
                    weigh(G if u >= 3 else G - 1, par if u >= 3 else 1 - par, (u - 3) % A0_U)
                if u % 2 == 0 and (u >= 6 or not first):
                    turn_O(G if u >= 6 else G - 1, (u // 2 - 3) % NT)
                if u % 2 == 1 and (u >= 7 or not first):
                    project_out(G if u >= 7 else G - 1, par if u >= 7 else 1 - par, ((u - 1) // 2 - 3) % NT)

            def body(G, par, first=False, last=False):
                for u in range(A0_U):
                    scores(G, par, u)
                    if u in CH_AT and not last:
                        chunk_of(G + 1, 1 - par, CH_AT[u])
                    lag(G, par, u, first)

            pe.wait_ge(wv_in, 32)
            for t in range(NT):
                if t < NCH:
                    chunk_of(0, 0, t)
                values_of(t)
            pe.wait_ge(ones_set, 1)
            pe.wait_ge(v_ready, NT)
            groups(pe, lambda: body(0, 0, True), body, lambda: body(A0_G - 1, 1, last=True))
            for u in range(A0_U, A0_U + 8):
                if u < A0_U + 2:
                    turn_P(A0_G - 1, u - 2)
                if u < A0_U + 3:
                    weigh(A0_G - 1, 1, u - 3)
                if u % 2 == 0 and u < A0_U + 6:
                    turn_O(A0_G - 1, u // 2 - 3)
                if u % 2 == 1 and u < A0_U + 7:
                    project_out(A0_G - 1, 1, (u - 1) // 2 - 3)


def norm_and_turn(nc, k, ctx, tag, banks, eps=LN_EPS):
    sem = lambda name: k.sem(f"{tag}_{name}")
    ln, rstd_ready, xn_ready, turned, xT_ready = (sem("ln"), sem("rstd_ready"), sem("xn_ready"),
                                                  sem("turned"), sem("xT_ready"))

    def on_vector(dve):
        norm_rows(nc, dve, k, k.x, k.xn, ln, rstd_ready, 0, xn_ready)

    def on_gpsimd(pool):
        inverse_root(nc, pool, k, ln, rstd_ready, 0, eps)

    def on_tensor(pe):
        turn_rows(nc, pe, k, banks, xn_ready, 0, turned)
        pe.wait_ge(xT_ready, 4)

    def on_scalar(act):
        for j in range(4):
            act.wait_ge(turned, (j % NH2) + 1)
            nc.scalar.copy(k.xT[:, j // NH2, (j % NH2) * NC:(j % NH2 + 1) * NC],
                           banks[j][:, :]).then_inc(xT_ready, 1)

    return on_vector, on_gpsimd, on_tensor, on_scalar, (ln, rstd_ready, xn_ready, xT_ready)


X0_H, X0_D = 16, 16
X0_HM = P // X0_D
X0_U = 2 * X0_H // 2
X0_CLIP = 50.0


def cross_attention_0(nc, k, src):
    with ExitStack() as ctx:
        sb = lambda name, shape, dt=F32: k.sb(ctx, "x0_" + name, shape, dt)
        w = k.tile["x0_w"]
        cT = k.tile["ctxT"]
        cols = k.tile["x0_cols"]
        rows = k.tile["x0_rows"]
        hmask, rs, mask = k.tile["x0_hmask"], k.tile["x0_rs"], k.tile["x0_mask"]
        keep = sb("keep", [P, NT])
        drop = sb("drop", [P, NT])
        qT = sb("qT", [P, KD, S])
        qz = [sb(f"qz{i}", [P, X0_H, S]) for i in range(2)]
        kT = sb("kT", [P, KD, T])
        v = sb("v", [P, NT, X0_H, X0_D + 1])
        clipped = [sb(f"clipped{i}", [P, 2, S]) for i in range(2)]
        PT = [sb(f"PT{i}", [P, 2, S]) for i in range(6)]
        rec = sb("rec", [P, 2, X0_H])
        O = [sb(f"O{i}", [P, X0_H, X0_D]) for i in range(2)]
        OT = [sb(f"OT{i}", [P, KD, P]) for i in range(2)]
        delta = sb("delta", [P, NT, D])
        pp = k.ps(ctx, "x0_pp")
        pS = [k.ps(ctx, f"x0_pS{i}") for i in range(2)]
        pO = [k.ps(ctx, f"x0_pO{i}") for i in range(2)]
        pOT = k.ps(ctx, "x0_pOT")
        pY = [k.ps(ctx, f"x0_pY{i}") for i in range(2)]

        sem = lambda name: k.sem("x0_" + name)
        on_vector, on_gpsimd, on_tensor, on_scalar, (ln, rstd_ready, xn_ready, xT_ready) = \
            norm_and_turn(nc, k, ctx, "x0", [pS[0], pS[1], pO[0], pO[1]])
        front, back = [pS[0], pS[1], pO[0], pO[1]], [pp, pOT, pY[0], pY[1]]
        ones_set = sem("ones_set")
        consts, keyed, k_out, valued, v_out = sem("consts"), sem("keyed"), sem("k_out"), sem("valued"), sem("v_out")
        proj, q_out, qz_ready = sem("proj"), sem("q_out"), sem("qz_ready")
        scored, clip_done, probs, weighed = sem("scored"), sem("clip_done"), sem("probs"), sem("weighed")
        rec_ready, O_ready, turnedO, OT_ready = sem("rec_ready"), sem("O_ready"), sem("turnedO"), sem("OT_ready")
        projected, shaped, scaled, dn, summed = (sem("projected"), sem("shaped"), sem("scaled"), sem("dn"),
                                                 sem("summed"))
        block = ctx.enter_context(nc.Block())

        @block.sync
        def _(sp):
            k.fetch(sp, src, "a1", "x1", "f1")

        @block.gpsimd
        def _(pool):
            nc.gpsimd.memset(v[:, :, :, X0_D:X0_D + 1], 1.0).then_inc(ones_set, 1)
            on_gpsimd(pool)
            k.wait(pool, "x0")
            for b in range(B):
                pool.wait_ge(q_out, 2 * b + 2)
                if b >= 2:
                    pool.wait_ge(scored, X0_U * (b - 1))
                for m in range(KD):
                    nc.gpsimd.tensor_tensor(
                        qz[b % 2][:, m * X0_HM:(m + 1) * X0_HM, :],
                        qT[:, m:m + 1, :].to_broadcast([P, X0_HM, S]),
                        hmask[:, :].rearrange("p (h o) -> p h o", o=1).to_broadcast([P, X0_HM, S]),
                        ALU.mult).then_inc(qz_ready, 1)
            inverse_root(nc, pool, k, ln, rstd_ready, 1)

        @block.scalar
        def _(act):
            k.wait(act, "x0")
            for m in range(KD):
                for half in range(NH2):
                    act.wait_ge(keyed, 2 * m + half + 1)
                    nc.scalar.activation(kT[:, m, half * NC:(half + 1) * NC], front[2 * m + half][:, :], ACT.Identity,
                                         bias=cols[:, 2 + m:3 + m]).then_inc(k_out, 1)
            on_scalar(act)

            def queries_out(b):
                act.wait_ge(proj, b + 1)
                if b >= 1:
                    act.wait_ge(qz_ready, 2 * b)
                for m in range(KD):
                    nc.scalar.activation(qT[:, m, :], pp[:, m * S:(m + 1) * S], ACT.Identity,
                                         bias=cols[:, m:m + 1]).then_inc(q_out, 1)

            queries_out(0)
            for U in range(B * X0_U + 10):
                b, u = U // X0_U, U % X0_U
                if U < B * X0_U:
                    kt = u % 2
                    act.wait_ge(clip_done, U + 1)
                    if U == 0:
                        act.wait_ge(consts, 3)
                    if U >= 6:
                        act.wait_ge(weighed, (U - 6) // 2 + 1)
                    nc.scalar.activation(PT[U % 6][:, :, :], clipped[U % 2][:, :, :], ACT.Exp,
                                         scale=keep[:, 2 * b + kt:2 * b + kt + 1],
                                         bias=drop[:, 2 * b + kt:2 * b + kt + 1]).then_inc(probs, 1)
                    if u == 4 and b + 1 < B:
                        queries_out(b + 1)
                for qt in range(2):
                    r = U - X0_U - 8 - qt
                    if r >= 0 and r % X0_U == 0:
                        j = 2 * (r // X0_U) + qt
                        act.wait_ge(turnedO, j + 1)
                        nc.scalar.copy(OT[qt][:, :, :].rearrange("p c q -> p (c q)"), pOT[:, 0:2 * P])\
                            .then_inc(OT_ready, 1)

        @block.vector
        def _(dve):
            on_vector(dve)
            k.wait(dve, "x0")
            nc.vector.tensor_scalar(rs[:, :], rs[:, :], 0.0, 0.3, ALU.max, ALU.min).then_inc(consts, 1)
            nc.vector.tensor_scalar(keep[:, :], mask[:, :], 0.5, None, ALU.is_gt).then_inc(consts, 1)
            dve.wait_ge(consts, 2)
            nc.vector.tensor_scalar(drop[:, :], keep[:, :], 1.0, X0_CLIP, ALU.subtract, ALU.mult).then_inc(consts, 1)
            dve.wait_ge(xn_ready, NT)
            for t in range(NT):
                nc.vector.tensor_tensor(k.x[:, t, :], k.x[:, t, :], rows[:, 3, :], ALU.add).then_inc(shaped, 1)

            def normalise(b, qt):
                j = 2 * b + qt
                dve.wait_ge(weighed, X0_H // 2 * (b + 1))
                o = pO[qt][:, 0:X0_H * (X0_D + 1)].rearrange("p (h n) -> p h n", h=X0_H)
                nc.vector.reciprocal(rec[:, qt, :], o[:, :, X0_D]).then_inc(rec_ready, 1)
                dve.wait_ge(rec_ready, j + 1)
                if b >= 1:
                    dve.wait_ge(turnedO, j - 1)
                nc.vector.tensor_tensor(O[qt][:, :, :], o[:, :, 0:X0_D],
                                        rec[:, qt, :].rearrange("p (h o) -> p h o", o=1).to_broadcast([P, X0_H, X0_D]),
                                        ALU.mult).then_inc(O_ready, 1)

            def scale_delta(b, qt):
                j = 2 * b + qt
                dve.wait_ge(projected, j + 1)
                nc.vector.tensor_tensor(delta[:, j, :], pY[qt][:, 0:D], rows[:, 1, :],
                                        ALU.add).then_inc(scaled, 1)
                dve.wait_ge(scaled, 2 * j + 1)
                nc.vector.tensor_scalar(delta[:, j, :], delta[:, j, :], rs[:, 0:1], None, ALU.mult)\
                    .then_inc(scaled, 1)

            bv = rows[:, 0, :].rearrange("p (h n) -> p h n", h=X0_H)
            for t in range(NT):
                dve.wait_ge(valued, t // 2 + 1)
                nc.vector.tensor_tensor(v[:, t, :, 0:X0_D],
                                        back[t // 2][:, (t % 2) * D:(t % 2 + 1) * D].rearrange("p (h n) -> p h n", h=X0_H),
                                        bv, ALU.add).then_inc(v_out, 1)
            for U in range(B * X0_U + 12):
                b, u = U // X0_U, U % X0_U
                if U < B * X0_U:
                    dve.wait_ge(scored, U + 1)
                    if U >= 2:
                        dve.wait_ge(probs, U - 1)
                    nc.vector.tensor_scalar(clipped[U % 2][:, :, :].rearrange("p h s -> p (h s)"), pS[U % 2][:, :],
                                            X0_CLIP, -X0_CLIP, ALU.min, ALU.max).then_inc(clip_done, 1)
                for qt in range(2):
                    r = U - X0_U - 3
                    if r >= 0 and r % X0_U == 0:
                        normalise(r // X0_U, qt)
                    r = U - X0_U - 10 - qt
                    if r >= 0 and r % X0_U == 0:
                        scale_delta(r // X0_U, qt)
            dve.wait_ge(scaled, 2 * NT)
            norm_rows(nc, dve, k, delta, k.xn, ln, rstd_ready, 1, dn)
            dve.wait_ge(dn, NT)
            for t in range(NT):
                nc.vector.tensor_tensor(k.xn[:, t, :], k.xn[:, t, :], rows[:, 2, :], ALU.mult).then_inc(summed, 1)
            dve.wait_ge(shaped, NT)
            for t in range(NT):
                dve.wait_ge(summed, t + 1)
                nc.vector.tensor_tensor(k.x[:, t, :], k.x[:, t, :], k.xn[:, t, :], ALU.add).then_inc(dn, 1)
            dve.wait_ge(dn, 2 * NT)

        @block.tensor
        def _(pe):
            k.wait(pe, "x0")
            for m in range(KD):
                for half in range(NH2):
                    for d in range(KD):
                        out = nc.tensor.matmul(front[2 * m + half][:, :], w[:, 1, d, m * P:(m + 1) * P],
                                               cT[:, d, half * NC:(half + 1) * NC], start=(d == 0), stop=(d == KD - 1))
                    out.then_inc(keyed, 1)
            for t in range(NT):
                for d in range(KD):
                    out = nc.tensor.matmul(back[t // 2][:, (t % 2) * D:(t % 2 + 1) * D], cT[:, d, t * P:(t + 1) * P],
                                           w[:, 2, d, :], start=(d == 0), stop=(d == KD - 1))
                if t % 2 == 1:
                    out.then_inc(valued, 1)
            pe.wait_ge(k_out, 4)
            on_tensor(pe)

            def project_queries(b):
                if b == 0:
                    pe.wait_ge(v_out, 2)
                else:
                    pe.wait_ge(q_out, 2 * b)
                for m in range(KD):
                    for d in range(KD):
                        out = nc.tensor.matmul(pp[:, m * S:(m + 1) * S], w[:, 0, d, m * P:(m + 1) * P],
                                               k.xT[:, d, b * S:(b + 1) * S], start=(d == 0), stop=(d == KD - 1))
                out.then_inc(proj, 1)

            def scores(U):
                b, u = U // X0_U, U % X0_U
                h, kt = 2 * (u // 2), u % 2
                if u == 0:
                    pe.wait_ge(qz_ready, 2 * b + 2)
                if U >= 2:
                    pe.wait_ge(clip_done, U - 1)
                nc.tensor.matmul(pS[U % 2][:, :], kT[:, h // X0_HM, b * S + kt * P:b * S + (kt + 1) * P],
                                 qz[b % 2][:, h:h + 2, :].rearrange("p h s -> p (h s)"),
                                 start=True, stop=True).then_inc(scored, 1)

            def weigh(n):
                b, pair = n // (X0_H // 2), n % (X0_H // 2)
                pe.wait_ge(probs, 2 * n + 2)
                if n == 0:
                    pe.wait_ge(v_out, NT)
                    pe.wait_ge(ones_set, 1)
                if pair == 0:
                    if b >= 1:
                        pe.wait_ge(O_ready, 2 * b)
                for h in range(2):
                    c0 = (2 * pair + h) * (X0_D + 1)
                    for qt in range(2):
                        for kt in range(2):
                            out = nc.tensor.matmul(pO[qt][:, c0:c0 + X0_D + 1],
                                                   PT[(2 * n + kt) % 6][:, h, qt * P:(qt + 1) * P],
                                                   v[:, 2 * b + kt, 2 * pair + h, :], start=(kt == 0), stop=(kt == 1))
                out.then_inc(weighed, 1)

            def turn_O(b, qt):
                j = 2 * b + qt
                pe.wait_ge(O_ready, j + 1)
                if j >= 1:
                    pe.wait_ge(OT_ready, j)
                for c in range(KD):
                    out = nc.tensor.transpose(pOT[:, c * P:(c + 1) * P],
                                              O[qt][:, c * X0_HM:(c + 1) * X0_HM, :].rearrange("p h n -> p (h n)"),
                                              k.tile["ident"][:, :])
                out.then_inc(turnedO, 1)

            def project_out(b, qt):
                j = 2 * b + qt
                pe.wait_ge(OT_ready, j + 1)
                if b >= 1:
                    pe.wait_ge(scaled, 2 * (j - 2) + 1)
                for c in range(KD):
                    out = nc.tensor.matmul(pY[qt][:, 0:D], OT[qt][:, c, :], w[:, 3, c, :],
                                           start=(c == 0), stop=(c == KD - 1))
                out.then_inc(projected, 1)

            project_queries(0)
            for U in range(B * X0_U + 12):
                b, u = U // X0_U, U % X0_U
                if U < B * X0_U:
                    scores(U)
                    if u == 4 and b + 1 < B:
                        project_queries(b + 1)
                if U % 2 == 0 and 0 <= (U - 4) // 2 < B * X0_H // 2 and U >= 4:
                    weigh((U - 4) // 2)
                for qt in range(2):
                    r = U - X0_U - 8 - qt
                    if r >= 0 and r % X0_U == 0:
                        turn_O(r // X0_U, qt)
                    r = U - X0_U - 9 - qt
                    if r >= 0 and r % X0_U == 0:
                        project_out(r // X0_U, qt)


M0_E, M0_I, M0_SH = 8, 176, 704
M0_GRAN = 16
M0_PER = M0_I // M0_GRAN
M0_TILES = -(-(M0_E * M0_I + M0_SH) // P)
M0_COLS = -(-M0_TILES * P // M0_I)
WT = 3 * D
FB = 2


def experts_0(nc, k, src):
    with ExitStack() as ctx:
        sb = lambda name, shape, dt=F32: k.sb(ctx, "m0_" + name, shape, dt)
        rw, iota = k.tile["m0_rw"], k.tile["m0_iota"]
        lg = sb("lg", [P, NT, M0_E + 1])
        top = sb("top", [P, NT, 8])
        at = sb("at", [P, NT, 8], U32)
        atf = sb("atf", [P, NT, 2])
        gap = sb("gap", [P, NT, 2])
        eg = sb("eg", [P, NT, 2])
        share = sb("share", [P, NT, 3])
        hot = sb("hot", [P, NT, 2, M0_E])
        comb = sb("comb", [P, NT, M0_COLS])
        combT = sb("combT", [M0_COLS, T])
        zeros = sb("zeros", [P, NC], BF16)
        gu = [k.tile[f"m0_gu{i}"] for i in range(2)]
        dn = [k.tile[f"m0_dn{i}"] for i in range(2)]
        cw = [sb(f"cw{i}", [P, T]) for i in range(2)]
        sg = [sb(f"sg{i}", [P, NC]) for i in range(2)]
        hu = [[sb(f"hu{i}{h}", [P, NC]) for h in range(2)] for i in range(2)]
        hT = [sb(f"hT{i}", [P, T]) for i in range(2)]
        pg = [k.ps(ctx, f"m0_pg{i}") for i in range(2)]
        pu = [k.ps(ctx, f"m0_pu{i}") for i in range(2)]
        acc = [k.ps(ctx, f"m0_acc{i}") for i in range(4)]
        table = nc.dram_tensor("m0_table", (M0_COLS, M0_PER, T), F32, kind="Internal").ap()

        sem = lambda name: k.sem("m0_" + name)
        on_vector, on_gpsimd, on_tensor, on_scalar, _ = norm_and_turn(nc, k, ctx, "m0", [pg[0], pg[1], pu[0], pu[1]])
        zero_set = sem("zero_set")
        gu_in, dn_in = [sem(f"gu_in{i}") for i in range(2)], [sem(f"dn_in{i}") for i in range(2)]
        cw_in = [sem(f"cw_in{i}") for i in range(2)]
        logits, lg_ready, routed, gates, comb_ready = (sem("logits"), sem("lg_ready"), sem("routed"),
                                                       sem("gates"), sem("comb_ready"))
        turnedC, combT_ready, table_out = sem("turnedC"), sem("combT_ready"), sem("table_out")
        gated, silu_done, up_done, h_ready, down_done, added = (sem("gated"), sem("silu_done"), sem("up_done"),
                                                                sem("h_ready"), sem("down_done"), sem("added"))
        block = ctx.enter_context(nc.Block())
        LAST = M0_TILES - 1
        PAIRS = (M0_TILES - 3) // 2
        assert M0_TILES == 3 + 2 * PAIRS

        def tiles(eng, step):
            step(0, 0)
            step(1, 1)
            with eng.Fori(0, PAIRS) as i:
                for s in range(2):
                    step(i * 2 + (2 + s), s)
            step(LAST, LAST % 2)

        def early(n, count):
            return isinstance(n, int) and n < count

        def arrivals(n, par, ahead=1):
            return 16 * (n // 2 + 1 - ahead) if isinstance(n, int) else n * 8 + (16 - 16 * ahead - 8 * par)

        @block.sync
        def _(sp):
            sp.wait_ge(combT_ready, 2)
            spread_rows = combT[:, :].rearrange("e (o t) -> e o t", o=1).to_broadcast([M0_COLS, M0_PER, T])
            sp.dma_start(table, spread_rows).then_inc(table_out, 16)
            sp.wait_ge(table_out, 16)
            rows = table.rearrange("e g t -> (e g) t")

            def weights_of(n, par):
                sp.dma_start(cw[par][:, :], per_granule(rows, n)).then_inc(cw_in[par], 16)

            def step(n, par):
                sp.wait_ge(gated, 2 * n + 2)
                sp.dma_start(gu[par][:, :], src["m0_gu"][bass.ds(n + 2, 1)].rearrange("g p n -> p (g n)"))\
                    .then_inc(gu_in[par], 16)
                sp.wait_ge(h_ready, 2 * n + 2)
                weights_of(n + 2, par)
                sp.wait_ge(down_done, n + 1)
                sp.dma_start(dn[par][:, :], src["m0_dn"][bass.ds(n + 2, 1)].rearrange("g p n -> p (g n)"))\
                    .then_inc(dn_in[par], 16)

            def per_granule(rows, n):
                g = rows[bass.ds(n * (P // M0_GRAN), P // M0_GRAN)]
                return g.rearrange("(g o) t -> g o t", o=1).to_broadcast([P // M0_GRAN, M0_GRAN, T])

            weights_of(0, 0)
            weights_of(1, 1)
            with sp.Fori(0, PAIRS) as i:
                for s in range(2):
                    step(i * 2 + s, s)
            step(LAST - 2, LAST % 2)

        @block.gpsimd
        def _(pool):
            nc.gpsimd.memset(zeros[:, :], 0.0).then_inc(zero_set, 1)
            on_gpsimd(pool)

        @block.scalar
        def _(act):
            on_scalar(act)
            act.wait_ge(gates, 1)
            nc.scalar.activation(eg[:, :, :], gap[:, :, :], ACT.Exp).then_inc(gates, 1)
            for h in range(2):
                act.wait_ge(turnedC, 1)
                nc.scalar.copy(combT[:, h * NC:(h + 1) * NC], acc[1 + h][0:M0_COLS, :]).then_inc(combT_ready, 1)

            def step(n, par):
                for h in range(2):
                    act.wait_ge(gated, 2 * n + h + 1)
                    if not early(n, 1):
                        act.wait_ge(up_done, 2 * n + h - 1)
                    nc.scalar.activation(sg[h][:, :], pg[h][:, :], ACT.Silu).then_inc(silu_done, 1)

            tiles(act, step)

        @block.vector
        def _(dve):
            on_vector(dve)
            k.wait(dve, "m0")
            dve.wait_ge(logits, 1)
            nc.vector.tensor_copy(lg[:, :, :], acc[0][:, 0:NT * (M0_E + 1)].rearrange("p (t e) -> p t e", t=NT))\
                .then_inc(lg_ready, 1)
            dve.wait_ge(lg_ready, 1)
            for t in range(NT):
                nc.vector.max(top[:, t, :], lg[:, t, 0:M0_E]).then_inc(routed, 1)
            for t in range(NT):
                dve.wait_ge(routed, t + 1)
                nc.vector.max_index(at[:, t, :], top[:, t, :], lg[:, t, 0:M0_E]).then_inc(lg_ready, 1)
            dve.wait_ge(lg_ready, 1 + NT)
            nc.vector.tensor_tensor(gap[:, :, 0:1], top[:, :, 1:2], top[:, :, 0:1], ALU.subtract)
            nc.vector.tensor_scalar(gap[:, :, 1:2], lg[:, :, M0_E:M0_E + 1], -1.0, None, ALU.mult).then_inc(gates, 1)
            nc.vector.tensor_copy(atf[:, :, :], at[:, :, 0:2]).then_inc(comb_ready, 1)
            dve.wait_ge(comb_ready, 1)
            for c in range(2):
                nc.vector.tensor_tensor(hot[:, :, c, :], iota[:, :].rearrange("p (o e) -> p o e", o=1).to_broadcast([P, NT, M0_E]),
                                        atf[:, :, c:c + 1].to_broadcast([P, NT, M0_E]), ALU.is_equal)\
                    .then_inc(comb_ready, 1)
            dve.wait_ge(gates, 2)
            nc.vector.tensor_scalar(eg[:, :, :], eg[:, :, :], 1.0, None, ALU.add).then_inc(comb_ready, 1)
            dve.wait_ge(comb_ready, 4)
            nc.vector.reciprocal(share[:, :, 0:2], eg[:, :, :]).then_inc(comb_ready, 1)
            dve.wait_ge(comb_ready, 5)
            nc.vector.tensor_scalar(eg[:, :, 0:1], eg[:, :, 0:1], 1.0, None, ALU.subtract).then_inc(comb_ready, 1)
            dve.wait_ge(comb_ready, 6)
            nc.vector.tensor_tensor(share[:, :, 2:3], eg[:, :, 0:1], share[:, :, 0:1], ALU.mult).then_inc(comb_ready, 1)
            dve.wait_ge(comb_ready, 7)
            for c, s in ((0, 0), (1, 2)):
                nc.vector.tensor_tensor(hot[:, :, c, :], hot[:, :, c, :],
                                        share[:, :, s:s + 1].to_broadcast([P, NT, M0_E]), ALU.mult)\
                    .then_inc(comb_ready, 1)
            nc.vector.tensor_copy(comb[:, :, M0_E:M0_COLS], share[:, :, 1:2].to_broadcast([P, NT, M0_COLS - M0_E]))\
                .then_inc(comb_ready, 1)
            dve.wait_ge(comb_ready, 10)
            nc.vector.tensor_tensor(comb[:, :, 0:M0_E], hot[:, :, 0, :], hot[:, :, 1, :], ALU.add).then_inc(comb_ready, 1)

            def times_up(n, par):
                for h in range(2):
                    dve.wait_ge(silu_done, 2 * n + h + 1)
                    nc.vector.tensor_tensor(hu[par][h][:, :], sg[h][:, :], pu[h][:, :], ALU.mult).then_inc(up_done, 1)

            def times_combine(n, par):
                dve.wait_ge(cw_in[par], arrivals(n, par, 0))
                for h in range(2):
                    dve.wait_ge(up_done, 2 * n + h + 1)
                    if not early(n, 2):
                        dve.wait_ge(down_done, n - 1)
                    nc.vector.tensor_tensor(hT[par][:, h * NC:(h + 1) * NC], hu[par][h][:, :],
                                            cw[par][:, h * NC:(h + 1) * NC], ALU.mult).then_inc(h_ready, 1)

            def step(n, par):
                times_up(n, par)
                times_combine(n, par)

            times_up(0, 0)
            times_up(1, 1)
            times_combine(0, 0)
            times_combine(1, 1)
            with dve.Fori(0, PAIRS) as i:
                for s in range(2):
                    step(i * 2 + (2 + s), s)
            step(LAST, LAST % 2)
            dve.wait_ge(down_done, M0_TILES)
            for a in range(4):
                nc.vector.tensor_tensor(k.x[:, 2 * a:2 * a + 2, :], acc[a][:, :].rearrange("p (t n) -> p t n", t=2),
                                        k.x[:, 2 * a:2 * a + 2, :], ALU.add).then_inc(added, 1)
            dve.wait_ge(added, 4)

        @block.tensor
        def _(pe):
            k.wait(pe, "m0")
            on_tensor(pe)
            for t in range(NT):
                for d in range(KD):
                    out = nc.tensor.matmul(acc[0][:, t * (M0_E + 1):(t + 1) * (M0_E + 1)], k.xT[:, d, t * P:(t + 1) * P],
                                           rw[:, d, :], start=(d == 0), stop=(d == KD - 1))
            out.then_inc(logits, 1)

            def gate_up(n, par):
                if not early(n, 2):
                    pe.wait_ge(gu_in[par], arrivals(n, par))
                for h in range(2):
                    if not early(n, 1):
                        pe.wait_ge(up_done, 2 * n + h - 1)
                    for bank, off in ((pg[h], 0), (pu[h], D)):
                        for d in range(KD):
                            out = nc.tensor.matmul(bank[:, :], gu[par][:, off + d * P:off + (d + 1) * P],
                                                   k.xT[:, d, h * NC:(h + 1) * NC],
                                                   start=(d == 0), stop=(d == KD - 1))
                    out.then_inc(gated, 1)

            def down(n, par, last=False):
                if not early(n, 2):
                    pe.wait_ge(dn_in[par], arrivals(n, par))
                for h in range(2):
                    pe.wait_ge(h_ready, 2 * n + h + 1)
                    for t in range(h * NT // 2, (h + 1) * NT // 2):
                        out = nc.tensor.matmul(acc[t // 2][:, (t % 2) * D:(t % 2 + 1) * D], hT[par][:, t * P:(t + 1) * P],
                                               dn[par][:, :], start=False, stop=last, skip_group_check=True)
                out.then_inc(down_done, 1)

            gate_up(0, 0)
            pe.wait_ge(comb_ready, 11)
            for t in range(NT):
                out = nc.tensor.transpose(acc[1 + t // 4][0:M0_COLS, (t % 4) * P:(t % 4 + 1) * P], comb[:, t, :], k.tile["ident"][:, :])
            out.then_inc(turnedC, 1)
            pe.wait_ge(combT_ready, 2)
            pe.wait_ge(lg_ready, 1)
            pe.wait_ge(zero_set, 1)
            for a in range(4):
                nc.tensor.matmul(acc[a][:, :], zeros[:, 0:P], zeros[:, :], start=True, stop=False, skip_group_check=True)
            gate_up(1, 1)
            down(0, 0)
            with pe.Fori(0, PAIRS) as i:
                for s in range(2):
                    gate_up(i * 2 + (2 + s), s)
                    down(i * 2 + (1 + s), 1 - s)
            gate_up(LAST, LAST % 2)
            down(LAST - 1, 1 - LAST % 2)
            down(LAST, LAST % 2, last=True)


def store_x(nc, k, out):
    with ExitStack() as ctx:
        stored = k.sem("stored")
        block = ctx.enter_context(nc.Block())

        @block.sync
        def _(sp):
            for t in range(NT):
                sp.dma_start(out.rearrange("(t p) d -> p t d", p=P)[:, t, :], k.x[:, t, :]).then_inc(stored, 16)
            sp.wait_ge(stored, 16 * NT)

def attention_1(nc, k, src):
    with ExitStack() as ctx:
        sb = lambda name, shape, dt=F32: k.sb(ctx, "a1_" + name, shape, dt)
        w = [k.tile[f"a1_w{i}"] for i in range(2)]
        wo = [k.tile[f"a1_wo{i}"] for i in range(2)]
        cs = k.tile["a1_cs"]
        cmask = k.tile["a1_mask"]
        rows = k.tile["a1_rows"]
        qT = [sb(f"qT{i}", [P, T]) for i in range(2)]
        kT = [sb(f"kT{i}", [P, T]) for i in range(2)]
        v = [sb(f"v{i}", [P, NT, P + 1]) for i in range(2)]
        t1 = [sb(f"t1{i}", [P, 2, S]) for i in range(2)]
        t2 = [sb(f"t2{i}", [P, 2, S]) for i in range(2)]
        hn = sb("hn", [P, NT, D])
        nS = [sb(f"nS{i}", [P, 3 * P]) for i in range(2)]
        nm = [sb(f"nm{i}", [P, 2]) for i in range(2)]
        Pm = [sb(f"Pm{i}", [P, 3 * P]) for i in range(2)]
        PT = [sb(f"PT{i}", [P, 3, P]) for i in range(2)]
        rec = sb("rec", [P, 2])
        O = [sb(f"O{i}", [P, 2, P]) for i in range(2)]
        OT = [sb(f"OT{i}", [P, 2, P]) for i in range(2)]
        pp = [k.ps(ctx, f"a1_pp{i}") for i in range(2)]
        pS = [k.ps(ctx, f"a1_pS{i}") for i in range(2)]
        pT = k.ps(ctx, "a1_pT")
        pO = k.ps(ctx, "a1_pO")
        pOT = k.ps(ctx, "a1_pOT")
        pY = k.ps(ctx, "a1_pY")
        turn_banks = [pS[0], pS[1], pT, pO]

        sem = lambda name: k.sem("a1_" + name)
        ones_set, gate, sp_gate = sem("ones_set"), sem("gate"), sem("sp_gate")
        w_in, wo_in = [sem("w_in0"), sem("w_in1")], [sem("wo_in0"), sem("wo_in1")]
        ln, rstd_ready, h_ready, n_ready, xn_ready = (sem("ln"), sem("rstd_ready"), sem("h_ready"),
                                                      sem("n_ready"), sem("xn_ready"))
        turned, xT_ready, based = sem("turned"), sem("xT_ready"), sem("based")
        proj, roped, chunk, v_ready = sem("proj"), sem("roped"), sem("chunk"), sem("v_ready")
        scored, maxed, probs, turnedP, PT_ready = (sem("scored"), sem("maxed"), sem("probs"),
                                                   sem("turnedP"), sem("PT_ready"))
        weighed, rec_ready, O_ready = sem("weighed"), sem("rec_ready"), sem("O_ready")
        turnedO, OT_ready, projected, added = sem("turnedO"), sem("OT_ready"), sem("projected"), sem("added")

        def heads(eng, step):
            step(0, 0, first=True)
            with eng.Fori(0, (A1_H - 2) // 2) as i:
                for s in range(2):
                    step(i * 2 + (1 + s), (1 + s) % 2)
            step(A1_H - 1, 1, last=True)
            step(A1_H, 0, drain=True)

        def after(H, b, lag):
            if b >= lag:
                return H, b - lag, 0
            return H - 1, b - lag + A1_U, 1

        def exists(H, b, lag, first, drain):
            return not ((first and b < lag) or (drain and b >= lag))

        def before(H, c, n):
            return isinstance(H, int) and A1_U * H + c < n

        def arrived(eng, H, par, sems):
            if not isinstance(H, int):
                eng.wait_ge(sems[par], (H + (2 - par)) * 8 - 16)
            elif H >= 2:
                eng.wait_ge(sems[par], 16 * (H // 2))

        CHUNKS = {0: (0, 1), 1: (2, 3), 2: (4,), 3: (5,)}
        block = ctx.enter_context(nc.Block())

        @block.sync
        def _(sp):
            with sp.Fori(0, (A1_H - 2) // 2) as i:
                for s in range(2):
                    h = i * 2 + (2 + s)
                    sp.wait_ge(chunk, (h - 1) * 4)
                    sp.sem_inc(sp_gate, 1)
                    sp.wait_ge(v_ready, (h - 1) * 2)
                    sp.dma_start(w[s][:, :], src["a1_w"][bass.ds(h, 1)].rearrange("g p n -> p (g n)"))\
                        .then_inc(w_in[s], 16)
                    sp.wait_ge(added, (h - 1) * A1_U)
                    sp.dma_start(wo[s][:, :], src["a1_wo"][bass.ds(h, 1)].rearrange("g p n -> p (g n)"))\
                        .then_inc(wo_in[s], 16)

        @block.gpsimd
        def _(pool):
            for i in range(2):
                nc.gpsimd.memset(v[i][:, :, P:P + 1], 1.0).then_inc(ones_set, 1)
            inverse_root(nc, pool, k, ln, rstd_ready, 0)
            inverse_root(nc, pool, k, ln, rstd_ready, 1)

            def project(H, par):
                for c in range(4):
                    pool.wait_ge(roped, H * 4 + (c + 1))
                    dst, half = (qT, kT)[c // 2][par], c % 2
                    nc.gpsimd.tensor_tensor(dst[:, half * NC:(half + 1) * NC],
                                            t1[c % 2][:, :, :].rearrange("p b s -> p (b s)"),
                                            t2[c % 2][:, :, :].rearrange("p b s -> p (b s)"),
                                            ALU.add).then_inc(chunk, 1)

            project(0, 0)
            project(1, 1)
            with pool.Fori(0, (A1_H - 2) // 2) as i:
                for s in range(2):
                    project(i * 2 + (2 + s), s)

        @block.scalar
        def _(act):
            for j in range(4):
                act.wait_ge(turned, (j % NH2) + 1)
                nc.scalar.copy(k.xT[:, j // NH2, (j % NH2) * NC:(j % NH2 + 1) * NC],
                               turn_banks[j][:, :]).then_inc(xT_ready, 1)

            def values(H, par, c):
                act.wait_ge(proj, H * 6 + (c + 1))
                n = c - 4
                nc.scalar.copy(v[par][:, 4 * n:4 * n + 4, 0:P],
                               pp[c % 2][:, :].rearrange("p (t n) -> p t n", t=4)).then_inc(v_ready, 1)

            def step(H, par, first=False, last=False, drain=False):
                for b in range(A1_U if not drain else 2):
                    if exists(H, b, 2, first, drain):
                        h, u, _ = after(H, b, 2)
                        act.wait_ge(turnedO, h * A1_U + (u + 1))
                        nc.scalar.copy(OT[u % 2][:, :, :].rearrange("p c q -> p (c q)"), pOT[:, 0:2 * P])\
                            .then_inc(OT_ready, 1)
                    if exists(H, b, 1, first, drain):
                        h, u, _ = after(H, b, 1)
                        act.wait_ge(turnedP, h * A1_U + (u + 1))
                        nc.scalar.copy(PT[u % 2][:, :, :].rearrange("p c q -> p (c q)"), pT[:, 0:3 * P])\
                            .then_inc(PT_ready, 1)
                    if not drain:
                        act.wait_ge(maxed, H * A1_U + (b + 1))
                        nc.scalar.activation(Pm[b % 2][:, 0:P], nS[b % 2][:, 0:P], ACT.Exp,
                                             bias=nm[b % 2][:, 0:1], scale=-1.0)
                        nc.scalar.activation(Pm[b % 2][:, P:3 * P], nS[b % 2][:, P:3 * P], ACT.Exp,
                                             bias=nm[b % 2][:, 1:2], scale=-1.0).then_inc(probs, 1)
                    if not (last or drain):
                        for c in CHUNKS[b]:
                            if c >= 4:
                                values(H + 1, 1 - par, c)

            for c in (4, 5):
                values(0, 0, c)
            heads(act, step)

        @block.vector
        def _(dve):
            norm_rows(nc, dve, k, k.x, hn, ln, rstd_ready, 0, h_ready)
            dve.wait_ge(h_ready, NT)
            norm_rows(nc, dve, k, hn, k.xn, ln, rstd_ready, 1, n_ready)
            k.wait(dve, "a1")
            for t in range(NT):
                dve.wait_ge(n_ready, t + 1)
                nc.vector.tensor_tensor(k.xn[:, t, :], k.xn[:, t, :], rows[:, 0, :], ALU.mult).then_inc(based, 1)
            for t in range(NT):
                dve.wait_ge(based, t + 1)
                nc.vector.tensor_tensor(k.xn[:, t, :], k.xn[:, t, :], rows[:, 1, :], ALU.add).then_inc(xn_ready, 1)
            for t in range(NT):
                nc.vector.tensor_tensor(k.x[:, t, :], k.x[:, t, :], rows[:, 2, :], ALU.add).then_inc(based, 1)
            for t in range(NT):
                dve.wait_ge(based, NT + t + 1)
                nc.vector.tensor_tensor(k.x[:, t, :], k.x[:, t, :], hn[:, t, :], ALU.add).then_inc(based, 1)
            dve.wait_ge(based, 3 * NT)

            def rope(H, par, c):
                n, kind = c % 2, c // 2
                bias = w[par][:, A1_W - 2 + kind:A1_W - 1 + kind]
                arrived(dve, H, par, w_in)
                dve.wait_ge(proj, H * 6 + (c + 1))
                if not before(H, c, 2):
                    dve.wait_ge(chunk, H * 4 + (c - 1))
                a = pp[n][:, :].rearrange("p (b s) -> p b s", b=2)
                lo, hi = slice(0, 64), slice(64, 128)
                tab = lambda i, r: cs[r, 2 * kind + i:2 * kind + i + 1, :].to_broadcast([r.stop - r.start, 2, S])
                nc.vector.scalar_tensor_tensor(out=t1[n][:, :, :], in0=a, scalar=bias, in1=tab(0, slice(0, P)),
                                               op0=ALU.add, op1=ALU.mult)
                nc.vector.scalar_tensor_tensor(out=t2[n][lo, :, :], in0=a[hi], scalar=bias[hi], in1=tab(1, hi),
                                               op0=ALU.add, op1=ALU.mult)
                nc.vector.scalar_tensor_tensor(out=t2[n][hi, :, :], in0=a[lo], scalar=bias[lo], in1=tab(1, lo),
                                               op0=ALU.add, op1=ALU.mult).then_inc(roped, 1)

            def maxima(H, b):
                dve.wait_ge(scored, H * A1_U + (b + 1))
                if not before(H, b, 2):
                    dve.wait_ge(probs, H * A1_U + (b - 1))
                dve.sem_inc(gate, 1)
                nc.vector.tensor_tensor_reduce(nS[b % 2][:, 0:P], pS[b % 2][:, 0:P], cmask[:, 0:P], -1.0, 3.0e38,
                                               ALU.add, ALU.min, nm[b % 2][:, 0:1])
                nc.vector.tensor_tensor_reduce(nS[b % 2][:, P:3 * P], pS[b % 2][:, P:3 * P], cmask[:, P:3 * P], -1.0,
                                               3.0e38, ALU.add, ALU.min, nm[b % 2][:, 1:2]).then_inc(maxed, 1)

            def normalise(H, u, par):
                dve.wait_ge(weighed, H * A1_U + (u + 1))
                o = pO[:, 0:2 * (P + 1)].rearrange("p (c n) -> p c n", c=2)
                nc.vector.reciprocal(rec[:, :], o[:, :, P]).then_inc(rec_ready, 1)
                if u == 0:
                    arrived(dve, H, par, wo_in)
                dve.wait_ge(rec_ready, H * A1_U + (u + 1))
                if not before(H, u, 2):
                    dve.wait_ge(turnedO, H * A1_U + (u - 1))
                for c in range(2):
                    out = nc.vector.scalar_tensor_tensor(out=O[u % 2][:, c, :], in0=o[:, c, 0:P],
                                                         scalar=rec[:, c:c + 1], in1=wo[par][:, D:D + P],
                                                         op0=ALU.mult, op1=ALU.add)
                out.then_inc(O_ready, 1)

            def add_y(H, u):
                dve.wait_ge(projected, H * A1_U + (u + 1))
                if not before(H, u, A1_U):
                    dve.wait_ge(added, H * A1_U + u)
                nc.vector.tensor_tensor(k.x[:, 2 * u:2 * u + 2, :], pY[:, :].rearrange("p (c n) -> p c n", c=2),
                                        k.x[:, 2 * u:2 * u + 2, :], ALU.add).then_inc(added, 1)

            def step(H, par, first=False, last=False, drain=False):
                for b in range(A1_U if not drain else 2):
                    cc = CHUNKS[b] if not (last or drain) else ()
                    if not drain:
                        maxima(H, b)
                    if len(cc) and cc[0] < 4:
                        rope(H + 1, 1 - par, cc[0])
                    if exists(H, b, 1, first, drain):
                        h, u, x = after(H, b, 1)
                        normalise(h, u, par ^ x)
                    if exists(H, b, 2, first, drain):
                        h, u, _ = after(H, b, 2)
                        add_y(h, u)
                    if len(cc) > 1:
                        rope(H + 1, 1 - par, cc[1])

            for c in range(4):
                rope(0, 0, c)
            heads(dve, step)
            dve.wait_ge(added, A1_H * A1_U)

        @block.tensor
        def _(pe):
            k.wait(pe, "a1")
            turn_rows(nc, pe, k, turn_banks, xn_ready, 0, turned)
            pe.wait_ge(xT_ready, 4)

            def chunk_of(H, par, c):
                if c == 0:
                    arrived(pe, H, par, w_in)
                if not (isinstance(H, int) and H == 0 and c < 2):
                    if c < 2:
                        pe.wait_ge(v_ready, H * 2 + (c - 1))
                    else:
                        pe.wait_ge(roped, H * 4 + (c - 1))
                if c < 4:
                    for d in range(KD):
                        off = ((c // 2) * KD + d) * P
                        out = nc.tensor.matmul(pp[c % 2][:, :], w[par][:, off:off + P],
                                               k.xT[:, d, (c % 2) * NC:(c % 2 + 1) * NC],
                                               start=(d == 0), stop=(d == KD - 1))
                else:
                    for t in range(4):
                        for d in range(KD):
                            off = (2 * KD + d) * P
                            tt = 4 * (c - 4) + t
                            out = nc.tensor.matmul(pp[c % 2][:, t * P:(t + 1) * P], k.xT[:, d, tt * P:(tt + 1) * P],
                                                   w[par][:, off:off + P], start=(d == 0), stop=(d == KD - 1))
                out.then_inc(proj, 1)

            def scores(H, par, b):
                if b == 0:
                    pe.wait_ge(chunk, (H + 1) * 4)
                if not before(H, b, 2):
                    pe.wait_ge(maxed, H * A1_U + (b - 1))
                c = b * S
                nc.tensor.matmul(pS[b % 2][:, 0:P], qT[par][:, c:c + P], kT[par][:, c:c + P], start=True, stop=True)
                nc.tensor.matmul(pS[b % 2][:, P:3 * P], qT[par][:, c + P:c + S], kT[par][:, c:c + S],
                                 start=True, stop=True).then_inc(scored, 1)

            def turn_P(H, u):
                pe.wait_ge(probs, H * A1_U + (u + 1))
                if not before(H, u, 1):
                    pe.wait_ge(PT_ready, H * A1_U + u)
                for c in range(3):
                    out = nc.tensor.transpose(pT[:, c * P:(c + 1) * P], Pm[u % 2][:, c * P:(c + 1) * P], k.tile["ident"][:, :])
                out.then_inc(turnedP, 1)

            def weigh(H, par, u):
                pe.wait_ge(PT_ready, H * A1_U + (u + 1))
                if u == 0:
                    pe.wait_ge(v_ready, (H + 1) * 2)
                if isinstance(H, int) and H == 0 and u == 0:
                    pe.wait_ge(ones_set, 2)
                if not before(H, u, 1):
                    pe.wait_ge(O_ready, H * A1_U + u)
                nc.tensor.matmul(pO[:, 0:P + 1], PT[u % 2][:, 0, :], v[par][:, 2 * u, :], start=True, stop=True)
                for c in range(2):
                    out = nc.tensor.matmul(pO[:, P + 1:2 * (P + 1)], PT[u % 2][:, 1 + c, :], v[par][:, 2 * u + c, :],
                                           start=(c == 0), stop=(c == 1))
                out.then_inc(weighed, 1)

            def turn_O(H, u):
                pe.wait_ge(O_ready, H * A1_U + (u + 1))
                if not before(H, u, 1):
                    pe.wait_ge(OT_ready, H * A1_U + u)
                for c in range(2):
                    out = nc.tensor.transpose(pOT[:, c * P:(c + 1) * P], O[u % 2][:, c, :], k.tile["ident"][:, :])
                out.then_inc(turnedO, 1)

            def project_out(H, par, u):
                pe.wait_ge(OT_ready, H * A1_U + (u + 1))
                if u == 0:
                    arrived(pe, H, par, wo_in)
                if not before(H, u, 1):
                    pe.wait_ge(added, H * A1_U + u)
                for c in range(2):
                    out = nc.tensor.matmul(pY[:, c * D:(c + 1) * D], OT[u % 2][:, c, :], wo[par][:, 0:D],
                                           start=True, stop=True)
                out.then_inc(projected, 1)

            def step(H, par, first=False, last=False, drain=False):
                for b in range(A1_U if not drain else 2):
                    cc = CHUNKS[b] if not (last or drain) else ()
                    if not drain:
                        scores(H, par, b)
                    if exists(H, b, 2, first, drain):
                        h, u, _ = after(H, b, 2)
                        turn_O(h, u)
                    if exists(H, b, 1, first, drain):
                        h, u, _ = after(H, b, 1)
                        turn_P(h, u)
                    if len(cc):
                        chunk_of(H + 1, 1 - par, cc[0])
                    if exists(H, b, 1, first, drain):
                        h, u, x = after(H, b, 1)
                        weigh(h, par ^ x, u)
                    if exists(H, b, 2, first, drain):
                        h, u, x = after(H, b, 2)
                        project_out(h, par ^ x, u)
                    if len(cc) > 1:
                        chunk_of(H + 1, 1 - par, cc[1])

            for c in range(6):
                chunk_of(0, 0, c)
            heads(pe, step)

X1_H = 2
X1_EPS = 1e-3


def retention_1(nc, k, src):
    with ExitStack() as ctx:
        sb = lambda name, shape, dt=F32: k.sb(ctx, "x1_" + name, shape, dt)
        wh, wg, wo, cT = k.tile["x1_wh"], k.tile["x1_wg"], k.tile["x1_wo"], k.tile["ctxT"]
        decay = k.tile["x1_decay"]
        rows = k.tile["x1_rows"]
        QT = sb("QT", [P, X1_H, T])
        KT = sb("KT", [P, X1_H, T])
        V = sb("V", [P, 2, X1_H, B, P])
        W = sb("W", [P, NT, D])
        A = sb("A", [P, X1_H, 4 * P])
        raw = sb("raw", [P, X1_H, 3 * P])
        O = sb("O", [P, NT, D])
        ba = [k.ps(ctx, f"x1_ba{i}") for i in range(4)]
        bb = [k.ps(ctx, f"x1_bb{i}") for i in range(4)]

        sem = lambda name: k.sem("x1_" + name)
        on_vector, on_gpsimd, on_tensor, on_scalar, (ln, rstd_ready, xn_ready, xT_ready) = \
            norm_and_turn(nc, k, ctx, "x1", bb)
        filled, moved, ones_set = sem("filled"), sem("moved"), sem("ones_set")
        scored, raw_ready, A_ready, weighed, O_ready = (sem("scored"), sem("raw_ready"), sem("A_ready"),
                                                        sem("weighed"), sem("O_ready"))
        normed, shaped, mixed, turned, mT_ready = (sem("normed"), sem("shaped"), sem("mixed"), sem("turnedM"),
                                                   sem("mT_ready"))
        projected, added = sem("projected"), sem("added")
        block = ctx.enter_context(nc.Block())

        @block.gpsimd
        def _(pool):
            nc.gpsimd.memset(A[:, :, 3 * P:4 * P], 1.0).then_inc(ones_set, 1)
            on_gpsimd(pool)
            inverse_root(nc, pool, k, ln, rstd_ready, 1, X1_EPS)

        @block.scalar
        def _(act):
            def move(j, out, func=ACT.Copy):
                act.wait_ge(filled, j + 1)
                bank = ba[j % 4][:, :]
                if len(out.shape) == 3:
                    bank = bank.rearrange("p (t n) -> p t n", t=out.shape[1])
                nc.scalar.activation(out, bank, func).then_inc(moved, 1)

            for h in range(X1_H):
                for half in range(NH2):
                    move(2 * h + half, KT[:, h, half * NC:(half + 1) * NC])
            for h in range(X1_H):
                for kt in range(2):
                    move(4 + 2 * h + kt, V[:, kt, h, :, :])
            on_scalar(act)
            for h in range(X1_H):
                for half in range(NH2):
                    move(8 + 2 * h + half, QT[:, h, half * NC:(half + 1) * NC])
            for g in range(4):
                move(12 + g, W[:, 2 * g:2 * g + 2, :], ACT.Relu)
            for h in range(X1_H):
                for st in range(2):
                    act.wait_ge(weighed, 2 * h + st + 1)
                    nc.scalar.copy(O[:, st:NT:2, h * P:(h + 1) * P],
                                   ba[2 * h + st][:, :].rearrange("p (b n) -> p b n", b=B)).then_inc(O_ready, 1)
            for j in range(4):
                act.wait_ge(turned, (j % NH2) + 1)
                nc.scalar.copy(k.xT[:, j // NH2, (j % NH2) * NC:(j % NH2 + 1) * NC], bb[j][:, :]).then_inc(mT_ready, 1)

        @block.vector
        def _(dve):
            on_vector(dve)
            k.wait(dve, "x1")
            for h in range(X1_H):
                dve.wait_ge(scored, h + 1)
                nc.vector.tensor_tensor(raw[:, h, :], bb[h][:, 0:3 * P], decay[:, h, :], ALU.mult).then_inc(raw_ready, 1)
                dve.wait_ge(raw_ready, 2 * h + 1)
                nc.vector.scalar_tensor_tensor(out=A[:, h, 0:3 * P], in0=raw[:, h, :], scalar=-1.0, in1=raw[:, h, :],
                                               op0=ALU.mult, op1=ALU.max).then_inc(raw_ready, 1)
                dve.wait_ge(raw_ready, 2 * h + 2)
                nc.vector.tensor_scalar(A[:, h, 0:3 * P], A[:, h, 0:3 * P], 1.0, None, ALU.max).then_inc(A_ready, 1)
            dve.wait_ge(O_ready, 4)
            norm_rows(nc, dve, k, O, k.xn, ln, rstd_ready, 1, normed)
            for t in range(NT):
                dve.wait_ge(normed, t + 1)
                nc.vector.tensor_tensor(k.xn[:, t, :], k.xn[:, t, :], rows[:, 0, :], ALU.mult).then_inc(shaped, 1)
            for t in range(NT):
                dve.wait_ge(shaped, t + 1)
                nc.vector.tensor_tensor(k.xn[:, t, :], k.xn[:, t, :], rows[:, 1, :], ALU.add).then_inc(shaped, 1)
            dve.wait_ge(moved, 16)
            for t in range(NT):
                dve.wait_ge(shaped, NT + t + 1)
                nc.vector.tensor_tensor(k.xn[:, t, :], k.xn[:, t, :], W[:, t, :], ALU.mult).then_inc(mixed, 1)
            for g in range(4):
                dve.wait_ge(projected, g + 1)
                nc.vector.tensor_tensor(k.x[:, 2 * g:2 * g + 2, :], ba[g][:, :].rearrange("p (t n) -> p t n", t=2),
                                        k.x[:, 2 * g:2 * g + 2, :], ALU.add).then_inc(added, 1)
            dve.wait_ge(added, 4)

        @block.tensor
        def _(pe):
            k.wait(pe, "x1")

            def free(j):
                if j >= 4:
                    pe.wait_ge(moved, j - 3)

            for h in range(X1_H):
                for half in range(NH2):
                    j = 2 * h + half
                    free(j)
                    nc.tensor.matmul(ba[j % 4][:, :], wh[:, h, :], cT[:, h, half * NC:(half + 1) * NC],
                                     start=True, stop=True).then_inc(filled, 1)
            for h in range(X1_H):
                for kt in range(2):
                    j = 4 + 2 * h + kt
                    free(j)
                    for b in range(B):
                        out = nc.tensor.matmul(ba[j % 4][:, b * P:(b + 1) * P], cT[:, h, (2 * b + kt) * P:(2 * b + kt + 1) * P],
                                               wh[:, h, :], start=True, stop=True)
                    out.then_inc(filled, 1)
            on_tensor(pe)
            for h in range(X1_H):
                for half in range(NH2):
                    j = 8 + 2 * h + half
                    free(j)
                    nc.tensor.matmul(ba[j % 4][:, :], wh[:, h, :], k.xT[:, h, half * NC:(half + 1) * NC],
                                     start=True, stop=True).then_inc(filled, 1)
            for g in range(4):
                free(12 + g)
                for t in range(2):
                    for d in range(KD):
                        tt = 2 * g + t
                        out = nc.tensor.matmul(ba[g][:, t * D:(t + 1) * D], k.xT[:, d, tt * P:(tt + 1) * P], wg[:, d, :],
                                               start=(d == 0), stop=(d == KD - 1))
                out.then_inc(filled, 1)
            pe.wait_ge(moved, 12)
            for h in range(X1_H):
                for b in range(B):
                    nc.tensor.matmul(bb[h][:, 0:2 * P], KT[:, h, b * S:b * S + P], QT[:, h, b * S:(b + 1) * S],
                                     start=(b == 0), stop=(b == B - 1))
                for b in range(B):
                    out = nc.tensor.matmul(bb[h][:, 2 * P:3 * P], KT[:, h, b * S + P:(b + 1) * S],
                                           QT[:, h, b * S + P:(b + 1) * S], start=(b == 0), stop=(b == B - 1))
                out.then_inc(scored, 1)
            pe.wait_ge(moved, 16)
            pe.wait_ge(ones_set, 1)
            for h in range(X1_H):
                pe.wait_ge(A_ready, h + 1)
                for st in range(2):
                    for kt in range(2):
                        block_at = st if kt == 0 else (3 if st == 0 else 2)
                        out = nc.tensor.matmul(ba[2 * h + st][:, :], A[:, h, block_at * P:(block_at + 1) * P],
                                               V[:, kt, h, :, :].rearrange("p b n -> p (b n)"),
                                               start=(kt == 0), stop=(kt == 1))
                    out.then_inc(weighed, 1)
            pe.wait_ge(A_ready, 2)
            turn_rows(nc, pe, k, bb, mixed, 0, turned)
            pe.wait_ge(mT_ready, 4)
            pe.wait_ge(O_ready, 4)
            for g in range(4):
                for t in range(2):
                    for d in range(KD):
                        tt = 2 * g + t
                        out = nc.tensor.matmul(ba[g][:, t * D:(t + 1) * D], k.xT[:, d, tt * P:(tt + 1) * P], wo[:, d, :],
                                               start=(d == 0), stop=(d == KD - 1))
                out.then_inc(projected, 1)


F1_GT, F1_ET = 1024 // P, 512 // P
F1_KEYS, F1_TOP, F1_E, F1_R = 64, 8, 512, 64


def memory_1(nc, k, src):
    with ExitStack() as ctx:
        sb = lambda name, shape, dt=F32: k.sb(ctx, "f1_" + name, shape, dt)
        wq, keys, iota = k.tile["f1_wq"], k.tile["f1_keys"], k.tile["f1_iota"]
        QI = sb("QI", [F1_R, T, 2])
        R = sb("R", [P, 2, NT, F1_KEYS])
        top = sb("top", [P, 2, NT, F1_TOP])
        at = sb("at", [P, 2, NT, F1_TOP], U32)
        atf = sb("atf", [P, 2, NT, F1_TOP])
        sums = sb("sums", [P, F1_TOP, F1_TOP])
        which = sb("which", [P, F1_TOP, F1_TOP])
        best = sb("best", [P, NT, F1_TOP])
        bat = sb("bat", [P, F1_TOP], U32)
        batf = sb("batf", [P, F1_TOP])
        sel = sb("sel", [P, F1_TOP, F1_KEYS])
        expert = sb("expert", [P, NT, F1_TOP])
        ex = sb("ex", [P, NT, F1_TOP])
        tot = sb("tot", [P, NT, 2])
        PW = sb("PW", [P, NT, F1_E])
        hotv = [sb(f"hotv{i}", [P, F1_E]) for i in range(2)]
        hotp = [sb(f"hotp{i}", [P, F1_E]) for i in range(2)]
        zeros = sb("zeros", [P, NC], BF16)
        w = [k.tile[f"f1_w{i}"] for i in range(3)]
        sg = [sb(f"sg{i}", [P, NC]) for i in range(2)]
        hT = [sb(f"hT{i}", [P, T]) for i in range(2)]
        pg = [k.ps(ctx, f"f1_pg{i}") for i in range(2)]
        pu = [k.ps(ctx, f"f1_pu{i}") for i in range(2)]
        acc = [k.ps(ctx, f"f1_acc{i}") for i in range(4)]

        sem = lambda name: k.sem("f1_" + name)
        on_vector, on_gpsimd, on_tensor, on_scalar, _ = norm_and_turn(nc, k, ctx, "f1", [pg[0], pg[1], pu[0], pu[1]])
        zero_set = sem("zero_set")
        w_in = [sem(f"w_in{i}") for i in range(3)]
        queried, QI_ready, routed, R_ready = sem("queried"), sem("QI_ready"), sem("routed"), sem("R_ready")
        step_done, best_ready, ex_ready, mix_ready = sem("step_done"), sem("best_ready"), sem("ex_ready"), sem("mix_ready")
        built, pool_step, pool_built = sem("built"), sem("pool_step"), sem("pool_built")
        gated, silu_done, h_ready, down_done, added = (sem("gated"), sem("silu_done"), sem("h_ready"),
                                                       sem("down_done"), sem("added"))
        TILES = F1_GT + F1_ET
        POOL_TILES = (6, 7)
        DVE_TILES = [j for j in range(NT) if j not in POOL_TILES]
        block = ctx.enter_context(nc.Block())

        @block.sync
        def _(sp):
            for n in range(3, TILES):
                sp.wait_ge(down_done, n - 2)
                sp.dma_start(w[n % 3][:, :], src["f1_w"][n]).then_inc(w_in[n % 3], 16)

        @block.gpsimd
        def _(pool):
            nc.gpsimd.memset(zeros[:, :], 0.0).then_inc(zero_set, 1)
            on_gpsimd(pool)
            k.wait(pool, "f1")
            pool.wait_ge(mix_ready, 1)
            n = 0
            for j in POOL_TILES:
                for c in range(F1_TOP):
                    out = PW[:, j, :] if c == 0 else hotp[c % 2][:, :]
                    nc.gpsimd.tensor_scalar(out, iota[:, :], expert[:, j, c:c + 1], ex[:, j, c:c + 1],
                                            ALU.is_equal, ALU.mult).then_inc(pool_step, 1)
                    n += 1
                    if c:
                        pool.wait_ge(pool_step, n)
                        nc.gpsimd.tensor_tensor(PW[:, j, :], PW[:, j, :], hotp[c % 2][:, :], ALU.add)\
                            .then_inc(pool_step, 1)
                        n += 1
                        pool.wait_ge(pool_step, n)
                pool.sem_inc(pool_built, 1)

        @block.scalar
        def _(act):
            on_scalar(act)
            for s in range(2):
                for half in range(NH2):
                    act.wait_ge(queried, 2 * s + half + 1)
                    nc.scalar.copy(QI[:, half * NC:(half + 1) * NC, s], acc[2 * s + half][0:F1_R, :]).then_inc(QI_ready, 1)
            for n in range(TILES):
                for h in range(2):
                    i = 2 * n + h
                    act.wait_ge(gated, i + 1)
                    if i >= 2:
                        act.wait_ge(h_ready, i - 1)
                    nc.scalar.activation(sg[h][:, :], pg[h][:, :], ACT.Silu).then_inc(silu_done, 1)
                if n == 3:
                    act.wait_ge(best_ready, 1)
                    nc.scalar.activation(ex[:, :, :], ex[:, :, :], ACT.Exp).then_inc(ex_ready, 1)

        @block.vector
        def _(dve):
            on_vector(dve)
            k.wait(dve, "f1")
            done = [0]

            def link(ins):
                done[0] += 1
                ins.then_inc(step_done, 1)
                dve.wait_ge(step_done, done[0])

            def gate_times_up(n):
                for h in range(2):
                    i = 2 * n + h
                    dve.wait_ge(silu_done, i + 1)
                    if n >= 2:
                        dve.wait_ge(down_done, n - 1)
                    nc.vector.tensor_tensor(hT[n % 2][:, h * NC:(h + 1) * NC], sg[h][:, :], pu[h][:, :], ALU.mult)\
                        .then_inc(h_ready, 1)

            def best_of(j):
                for a in range(2):
                    out = nc.vector.max(top[:, a, j, :], R[:, a, j, :])
                link(out)
                for a in range(2):
                    out = nc.vector.max_index(at[:, a, j, :], top[:, a, j, :], R[:, a, j, :])
                link(out)
                link(nc.vector.tensor_copy(atf[:, :, j, :], at[:, :, j, :]))
                first = lambda x: x[:, 0, j, :].rearrange("p (a o) -> p a o", o=1).to_broadcast([P, F1_TOP, F1_TOP])
                second = lambda x: x[:, 1, j, :].rearrange("p (o b) -> p o b", o=1).to_broadcast([P, F1_TOP, F1_TOP])
                nc.vector.tensor_tensor(sums[:, :, :], first(top), second(top), ALU.add)
                link(nc.vector.scalar_tensor_tensor(out=which[:, :, :], in0=first(atf), scalar=float(F1_KEYS),
                                                    in1=second(atf), op0=ALU.mult, op1=ALU.add))
                flat = lambda x: x[:, :, :].rearrange("p a b -> p (a b)")
                nc.vector.max(best[:, j, :], flat(sums))
                link(nc.vector.tensor_scalar(flat(which), flat(which), float(F1_E - 1), None, ALU.min))
                link(nc.vector.max_index(bat[:, :], best[:, j, :], flat(sums)))
                link(nc.vector.tensor_copy(batf[:, :], bat[:, :]))
                link(nc.vector.tensor_tensor(sel[:, :, :],
                                             iota[:, 0:F1_KEYS].rearrange("p (o n) -> p o n", o=1).to_broadcast([P, F1_TOP, F1_KEYS]),
                                             batf[:, :].rearrange("p (c o) -> p c o", o=1).to_broadcast([P, F1_TOP, F1_KEYS]),
                                             ALU.is_equal))
                link(nc.vector.tensor_tensor(sel[:, :, :], sel[:, :, :],
                                             flat(which).rearrange("p (o n) -> p o n", o=1).to_broadcast([P, F1_TOP, F1_KEYS]),
                                             ALU.mult))
                link(nc.vector.tensor_reduce(expert[:, j, :], sel[:, :, :], AX.X, ALU.add))

            def spread_weights(j):
                for c in range(F1_TOP):
                    out = PW[:, j, :] if c == 0 else hotv[c % 2][:, :]
                    link(nc.vector.tensor_scalar(out, iota[:, :], expert[:, j, c:c + 1], ex[:, j, c:c + 1],
                                                 ALU.is_equal, ALU.mult))
                    if c:
                        link(nc.vector.tensor_tensor(PW[:, j, :], PW[:, j, :], hotv[c % 2][:, :], ALU.add))
                dve.sem_inc(built, 1)

            dve.wait_ge(routed, 1)
            for a in range(2):
                out = nc.vector.tensor_copy(R[:, a, :, :], acc[a][:, :].rearrange("p (t n) -> p t n", t=NT))
            out.then_inc(R_ready, 1)
            dve.wait_ge(R_ready, 1)
            for j in range(NT):
                best_of(j)
                if j % 2 == 1:
                    gate_times_up(j // 2)
            nc.vector.tensor_tensor(ex[:, :, :], best[:, :, :], best[:, :, 0:1].to_broadcast([P, NT, F1_TOP]),
                                    ALU.subtract).then_inc(best_ready, 1)
            dve.wait_ge(ex_ready, 1)
            link(nc.vector.tensor_reduce(tot[:, :, 0], ex[:, :, :], AX.X, ALU.add))
            link(nc.vector.reciprocal(tot[:, :, 1], tot[:, :, 0]))
            nc.vector.tensor_tensor(ex[:, :, :], ex[:, :, :], tot[:, :, 1:2].to_broadcast([P, NT, F1_TOP]),
                                    ALU.mult).then_inc(mix_ready, 1)
            dve.wait_ge(mix_ready, 1)
            for n in range(4, F1_GT):
                gate_times_up(n)
                for j in DVE_TILES[(n - 4) * len(DVE_TILES) // 4:(n - 3) * len(DVE_TILES) // 4]:
                    spread_weights(j)
            for n in range(F1_GT, TILES):
                gate_times_up(n)
            dve.wait_ge(down_done, TILES)
            for a in range(4):
                nc.vector.tensor_tensor(k.x[:, 2 * a:2 * a + 2, :], acc[a][:, :].rearrange("p (t n) -> p t n", t=2),
                                        k.x[:, 2 * a:2 * a + 2, :], ALU.add).then_inc(added, 1)
            dve.wait_ge(added, 4)

        @block.tensor
        def _(pe):
            k.wait(pe, "f1")
            on_tensor(pe)
            for s in range(2):
                for half in range(NH2):
                    for d in range(KD):
                        out = nc.tensor.matmul(acc[2 * s + half][0:F1_R, :], wq[:, d, s * F1_R:(s + 1) * F1_R],
                                               k.xT[:, d, half * NC:(half + 1) * NC], start=(d == 0), stop=(d == KD - 1))
                    out.then_inc(queried, 1)

            def gate_up(n):
                if n >= 3:
                    pe.wait_ge(w_in[n % 3], 16 * (n // 3))
                if n == F1_GT:
                    pe.wait_ge(built, len(DVE_TILES))
                    pe.wait_ge(pool_built, len(POOL_TILES))
                for h in range(2):
                    if n >= 1:
                        pe.wait_ge(h_ready, 2 * n + h - 1)
                    for d in range(KD):
                        out = nc.tensor.matmul(pg[h][:, :], w[n % 3][:, d * P:(d + 1) * P],
                                               k.xT[:, d, h * NC:(h + 1) * NC], start=(d == 0), stop=(d == KD - 1))
                    if n < F1_GT:
                        for d in range(KD):
                            out = nc.tensor.matmul(pu[h][:, :], w[n % 3][:, D + d * P:D + (d + 1) * P],
                                                   k.xT[:, d, h * NC:(h + 1) * NC], start=(d == 0), stop=(d == KD - 1))
                    else:
                        e = n - F1_GT
                        for t in range(4):
                            out = nc.tensor.transpose(pu[h][:, t * P:(t + 1) * P],
                                                      PW[:, 4 * h + t, e * P:(e + 1) * P], k.tile["ident"][:, :])
                    out.then_inc(gated, 1)

            def down(n):
                for h in range(2):
                    pe.wait_ge(h_ready, 2 * n + h + 1)
                    for t in range(h * NT // 2, (h + 1) * NT // 2):
                        out = nc.tensor.matmul(acc[t // 2][:, (t % 2) * D:(t % 2 + 1) * D],
                                               hT[n % 2][:, t * P:(t + 1) * P], w[n % 3][:, 2 * D:3 * D],
                                               start=False, stop=(n == TILES - 1), skip_group_check=True)
                out.then_inc(down_done, 1)

            pe.wait_ge(QI_ready, 4)
            for a in range(2):
                for j in range(NT):
                    rows_n = QI[:, a * NC + j * (P // 2):a * NC + (j + 1) * (P // 2), :].rearrange("r t s -> r (t s)")
                    out = nc.tensor.matmul(acc[a][:, j * F1_KEYS:(j + 1) * F1_KEYS], rows_n, keys[:, a, :],
                                           start=True, stop=True)
            out.then_inc(routed, 1)
            gate_up(0)
            pe.wait_ge(R_ready, 1)
            pe.wait_ge(zero_set, 1)
            for a in range(4):
                nc.tensor.matmul(acc[a][:, :], zeros[:, 0:P], zeros[:, :], start=True, stop=False, skip_group_check=True)
            for n in range(1, TILES):
                gate_up(n)
                down(n - 1)
            down(TILES - 1)


def load_x(nc, k, src, first):
    with ExitStack() as ctx:
        block = ctx.enter_context(nc.Block())

        @block.sync
        def _(sp):
            xr = src["x"].rearrange("(t p) d -> p t d", p=P)
            for t in range(NT):
                sp.dma_start(k.x[:, t, :], xr[:, t, :]).then_inc(k.x_in, 16)
            k.fetch(sp, src, *[g for g in AHEAD if first > 1 or g not in ("a1", "x1", "f1")])
            sp.wait_ge(k.x_in, 16 * NT)


def program(nc, src, out, start=0, stages=6):
    with ExitStack() as ctx:
        k = Kernel(nc, ctx)
        k.x_in = k.sem("x_in")
        subs = [lambda: attention_0(nc, k, src), lambda: cross_attention_0(nc, k, src),
                lambda: experts_0(nc, k, src), lambda: attention_1(nc, k, src),
                lambda: retention_1(nc, k, src), lambda: memory_1(nc, k, src)]
        if start:
            load_x(nc, k, src, start)
        for n, sub in enumerate(subs[start:stages]):
            if n == 3:
                k.clear_semaphores()
            sub()
        store_x(nc, k, out)



def layouts(a):
    f = np.float32
    out = {"x": a["x"].reshape(T, D)}
    out["ident"] = np.eye(P, dtype=f)
    half = A0_D // 2
    inv = 1.0 / 150000.0 ** (np.arange(half, dtype=np.float64) * 2.0 / A0_D)
    ang = (np.arange(S, dtype=f)[:, None] * inv.astype(f)[None, :]).astype(np.float64)
    scale = A0_D ** -0.25
    c, s = (np.cos(ang) * scale).T, (np.sin(ang) * scale).T
    out["a0_cos"] = np.concatenate([c] * 4).astype(f)
    out["a0_sin"] = np.concatenate([s, s, -s, -s]).astype(f)
    i = np.arange(S)
    far = np.abs(i[:, None] - i[None, :]) > A0_WIN
    out["a0_mask"] = np.where(far, MASKED, 0.0).astype(f).reshape(2, P, S).transpose(1, 0, 2).copy()
    slot = (np.arange(P) // 32) % 2
    out["a0_slot"] = np.stack([slot == 0, slot == 1], 1).astype(f)
    out["a0_bo"] = np.broadcast_to(a["L0_attn_bo"], (P, D))

    def pairs(w):
        lead = w.shape[:-2]
        w = w.reshape(*lead, w.shape[-2] // 2, 2, half, 2)
        n = len(lead)
        return w.transpose(*range(n), n, n + 3, n + 1, n + 2).reshape(*lead, -1, P)

    G = A0_G
    wq = pairs(a["L0_attn_Wq"]).reshape(KD, P, G, A0_PAIRS, P).transpose(2, 1, 0, 3, 4).reshape(G, P, A0_NQ)
    wk = pairs(np.repeat(a["L0_attn_Wk"], 2, axis=1)).reshape(KD, P, G, P).transpose(2, 1, 0, 3).reshape(G, P, A0_NK)
    out["a0_wv"] = a["L0_attn_Wv"].reshape(KD, P, G * A0_D).transpose(1, 0, 2)
    out["a0_bv"] = np.broadcast_to(a["L0_attn_bv"].reshape(-1), (P, G * A0_D))
    bq = pairs(a["L0_attn_bq"]).reshape(G, A0_PAIRS, P).transpose(0, 2, 1)
    bk = pairs(np.repeat(a["L0_attn_bk"], 2, axis=0)).reshape(G, 1, P).transpose(0, 2, 1)
    sk = np.broadcast_to(a["L0_attn_sinks"].reshape(G, 1, A0_R), (G, P, A0_R))
    out["a0_w"] = np.concatenate([wq, wk, bq, bk, sk], axis=2)
    out["a0_wo"] = a["L0_attn_Wo"].reshape(G, 2, P, D).transpose(0, 2, 1, 3)
    both = lambda v: np.broadcast_to(np.asarray(v), (P, v.shape[-1]))
    fm = lambda wt: wt.T.reshape(KD, P, -1).transpose(1, 0, 2)
    out["x0_w"] = np.stack([fm(a["L0_xattn_" + n]) for n in ("Wq", "Wk", "Wv", "Wo")], axis=1)
    out["ctxT"] = a["ctx_2048"].reshape(T, KD, P).transpose(2, 1, 0)
    out["x0_rows"] = np.stack([both(a["L0_xattn_" + n]) for n in ("bv", "bo", "ln_gamma", "ln_beta")], axis=1)
    out["x0_cols"] = np.concatenate([a["L0_xattn_bq"].reshape(KD, P).T, a["L0_xattn_bk"].reshape(KD, P).T], axis=1)
    out["x0_hmask"] = (np.arange(P)[:, None] // X0_D == np.arange(X0_HM)[None, :]).astype(f) * f(X0_D ** -0.5)
    out["x0_rs"] = np.broadcast_to(a["L0_xattn_residual_scale"].reshape(1, 1), (P, 1))
    out["x0_mask"] = a["mask_BxS2_ik0"].reshape(B, 2, P).transpose(2, 0, 1).reshape(P, NT)
    gate = np.concatenate([a["L0_ffn_gate_up_proj"][:, :M0_I].reshape(-1, D), a["L0_ffn_sh_gate_w"]])
    up = np.concatenate([a["L0_ffn_gate_up_proj"][:, M0_I:].reshape(-1, D), a["L0_ffn_sh_up_w"]])
    down = np.concatenate([a["L0_ffn_down_proj"].transpose(0, 2, 1).reshape(-1, D), a["L0_ffn_sh_down_w"].T])
    fill = np.zeros((M0_TILES * P - gate.shape[0], D), f)
    tiled = lambda wt: np.concatenate([wt, fill]).reshape(M0_TILES, P, KD, P).transpose(0, 3, 2, 1).reshape(M0_TILES, P, D)
    out["m0_gu"] = np.concatenate([tiled(gate), tiled(up)], axis=2)
    out["m0_dn"] = np.concatenate([down, fill]).reshape(M0_TILES, P, D)
    out["m0_rw"] = fm(np.concatenate([a["L0_ffn_router_weight"], a["L0_ffn_shared_gate_w"]]))
    out["m0_iota"] = np.broadcast_to(np.arange(M0_E, dtype=f), (P, M0_E))
    half = P // 2
    inv = (1.0 / 10000.0 ** (np.arange(0, P, 2, dtype=f) / P)).astype(f)
    ang = (np.arange(S, dtype=f)[:, None] * inv[None, :]).astype(np.float64)
    c, s = np.cos(ang).T, np.sin(ang).T
    tabs = []
    for scale in (P ** -0.5, 1.0):
        tabs += [np.concatenate([c, c]) * scale, np.concatenate([s, -s]) * scale]
    out["a1_cs"] = np.stack(tabs, axis=1).astype(f)
    above = np.where(np.arange(P)[None, :] > np.arange(P)[:, None], -1.0e30, 0.0).astype(f)
    out["a1_mask"] = np.concatenate([above, np.zeros((P, P), f), above], axis=1)
    out["a1_rows"] = np.stack([both(a["L1_attn_" + n]) for n in ("ln_g", "ln_b", "bo")], axis=1)
    hw = lambda wt: wt.reshape(A1_H, P, KD, P).transpose(0, 3, 2, 1).reshape(A1_H, P, KD * P)
    hb = lambda bb: bb.reshape(A1_H, P, 1)
    out["a1_w"] = np.concatenate([hw(a["L1_attn_" + n]) for n in ("wq", "wk", "wv")]
                                 + [hb(a["L1_attn_" + n]) for n in ("bq", "bk")], axis=2)
    bv = np.broadcast_to(a["L1_attn_bv"].reshape(A1_H, 1, P), (A1_H, P, P))
    out["a1_wo"] = np.concatenate([a["L1_attn_wo"].T.reshape(A1_H, P, D), bv], axis=2)
    out["x1_wh"] = a["L1_xattn_Wh"].transpose(1, 0, 2)
    rowm = lambda wt: wt.reshape(-1, P, wt.shape[1]).transpose(1, 0, 2)
    out["x1_wg"], out["x1_wo"] = rowm(a["L1_xattn_wg_w"]), rowm(a["L1_xattn_wo_w"])
    out["x1_rows"] = np.stack([both(a["L1_xattn_" + n]) for n in ("gn_gamma", "gn_beta")], axis=1)
    gam = (1.0 - 2.0 ** (-5.0 - np.arange(X1_H, dtype=f))).astype(f).astype(np.float64)
    ex = np.arange(S)[None, :] - np.arange(S)[:, None]
    dec = np.where(ex[None] <= 0, gam[:, None, None] ** ex[None], 0.0)
    dec = dec / np.sqrt(dec.sum(-1))[:, None, :] / np.sqrt(P)
    dT = dec.transpose(2, 0, 1).reshape(2, P, X1_H, S)
    out["x1_decay"] = np.concatenate([dT[0], dT[1][:, :, P:]], axis=2).astype(f)
    out["f1_wq"] = rowm(a["L1_ffn_W_q"])
    out["f1_keys"] = a["L1_ffn_keys"].transpose(1, 0, 2)
    out["f1_iota"] = np.broadcast_to(np.arange(F1_E, dtype=f), (P, F1_E))
    tl = lambda wt: wt.reshape(-1, P, KD, P).transpose(0, 3, 2, 1).reshape(-1, P, D)
    de, ue = a["L1_ffn_down_embed"], a["L1_ffn_up_embed"]
    up = np.concatenate([tl(a["L1_ffn_up_w"].T), np.zeros((F1_ET, P, D), f)])
    out["f1_w"] = np.concatenate([tl(np.concatenate([a["L1_ffn_gate_w"].T, de])), up,
                                  np.concatenate([a["L1_ffn_down_w"], ue]).reshape(-1, P, D)], axis=2)
    return {n: np.ascontiguousarray(v) for n, v in out.items()}


def kernel(**inputs):
    import concourse.bacc as bacc
    from concourse.bass_utils import run_bass_kernel_spmd

    arrays = layouts({n: np.asarray(v) for n, v in inputs.items()})
    nc = bacc.Bacc("TRN2", target_bir_lowering=False, num_devices=1)
    src = {n: nc.dram_tensor(n, v.shape, mybir.dt.from_np(v.dtype), kind="ExternalInput").ap()
           for n, v in arrays.items()}
    out = nc.dram_tensor("out", (T, D), F32, kind="ExternalOutput").ap()
    program(nc, src, out)
    got = run_bass_kernel_spmd(nc, [arrays], core_ids=[0])
    return got.results[0]["out"].reshape(B, S, D)
```

```python
from contextlib import ExitStack

import numpy as np

import concourse.bass as bass
import concourse.mybir as mybir
from concourse.alu_op_type import AluOpType as ALU

F32 = mybir.dt.float32
F32R = mybir.dt.float32r
BF16 = mybir.dt.bfloat16
U32 = mybir.dt.uint32
ACT = mybir.ActivationFunctionType
AX = mybir.AxisListType

P = 128
B, S, D = 4, 256, 256
T = B * S
NT = T // P
KD = D // P
NC = 512
NH2 = T // NC
LN_EPS = 1e-5


A0_G, A0_R, A0_D, A0_WIN = 8, 4, 64, 128
A0_PAIRS = A0_R // 2
A0_NQ = KD * A0_PAIRS * P
A0_NK = KD * P
A0_NB = A0_PAIRS + 1 + A0_R
A0_W = A0_NQ + A0_NK + A0_NB
A0_U = B * 2 * A0_PAIRS
MASKED = -1.0e9


A1_H = 16
A1_W = 2 * KD * P + 2
A1_U = B


AHEAD = {
    "ident": [("ident", [P, P], F32)],
    "ctx": [("ctxT", [P, KD, T], F32)],
    "a0": [("a0_cos", [P, S], F32), ("a0_sin", [P, S], F32), ("a0_mask", [P, 2, S], F32),
           ("a0_slot", [P, 2], F32), ("a0_bo", [P, D], F32)],
    "x0": [("x0_w", [P, 4, KD, D], F32), ("x0_rows", [P, 4, D], F32),
           ("x0_cols", [P, 4], F32), ("x0_hmask", [P, 8], F32), ("x0_rs", [P, 1], F32),
           ("x0_mask", [P, NT], mybir.dt.int32)],
    "m0": [("m0_rw", [P, KD, 9], F32), ("m0_iota", [P, 8], F32)]
          + [(f"m0_gu{i}", [P, 2 * D], F32) for i in range(2)] + [(f"m0_dn{i}", [P, D], F32) for i in range(2)],
    "a1": [("a1_rows", [P, 3, D], F32), ("a1_cs", [P, 4, S], F32), ("a1_mask", [P, 3 * P], F32)]
          + [(f"a1_w{i}", [P, A1_W], F32) for i in range(2)] + [("a1_wv0", [P, KD * 2 * P], F32), ("a1_wo0", [P, D + P], F32)],
    "x1": [("x1_wh", [P, 2, P], F32), ("x1_wg", [P, KD, D], F32), ("x1_wo", [P, KD, D], F32),
           ("x1_decay", [P, 2, 3 * P], F32), ("x1_rows", [P, 2, D], F32)],
    "f1": [("f1_wq", [P, KD, P], F32), ("f1_keys", [64, 2, 64], F32), ("f1_iota", [P, 512], F32)]
          + [(f"f1_w{i}", [P, 3 * D], F32) for i in range(3)],
}


class Kernel:

    def __init__(self, nc, ctx):
        self.nc, self.sems = nc, []
        self.x = self.sb(ctx, "x", [P, NT, D])
        self.xn = self.sb(ctx, "xn", [P, NT, D])
        self.xT = self.sb(ctx, "xT", [P, KD, T])
        self.xs = [self.sb(ctx, "x_" + part, [P, KD, T], F32R) for part in ("high", "low")]
        self.stats = self.sb(ctx, "stats", [P, NT, 6])
        self.mv = self.sb(ctx, "mv", [P, NT, 2])
        self.rstd = self.sb(ctx, "rstd", [P, NT])
        self.ve = self.sb(ctx, "ve", [P, NT])
        self.minus_half = self.sb(ctx, "minus_half", [P, NT])

        self.tile, self.arrived = {}, {}
        self.place(ctx, "ident", "ctx")

    def place(self, ctx, *groups, side=None):
        for group in groups:
            self.arrived[group] = self.nc.alloc_semaphore(name=group + "_arrived")
            for name, shape, dt in AHEAD[group]:
                self.tile[name] = ctx.enter_context(self.nc.sbuf_tensor("sb_" + name, shape, dt, side=side))

    def fetch(self, eng, src, *groups):
        for group in groups:
            for name, shape, _ in AHEAD[group]:
                tile = self.tile[name]
                where = src[name] if name in src else src[name[:-1]][int(name[-1])]
                eng.dma_start(tile[tuple([slice(None)] * len(shape))], where).then_inc(self.arrived[group], 16)

    def wait(self, eng, group):
        eng.wait_ge(self.arrived[group], 16 * len(AHEAD[group]))

    def sb(self, ctx, name, shape, dt=F32):
        return ctx.enter_context(self.nc.sbuf_tensor("sb_" + name, shape, dt))

    def ps(self, ctx, name, n=NC):
        return ctx.enter_context(self.nc.psum_tensor(name, [P, n], F32))

    def sem(self, name):
        s = self.nc.alloc_semaphore(name=name)
        self.sems.append(s)
        return s

    def clear_semaphores(self):
        self.nc.clear_and_free_semaphores(self.sems)
        self.nc.all_engine_barrier()
        self.sems = []


def spread(column, *dims):
    p = column.shape[0]
    if len(dims) == 1:
        return column.to_broadcast([p, dims[0]])
    return column.rearrange("p (o n) -> p o n", o=1).to_broadcast([p, *dims])


def high_of(nc, out, x):
    return nc.scalar.copy(out, x)


def low_of(nc, out, x, high):
    return nc.vector.tensor_tensor(out, x, high, ALU.subtract)


def split_product(nc, out, a, b, start, stop, **kw):
    for i, (p, q) in enumerate(((1, 0), (0, 1), (0, 0))):
        ins = nc.tensor.matmul(out, a[p], b[q], start=start and i == 0, stop=stop and i == 2, **kw)
    return ins


HALF = NT // 2


def row_stats(nc, dve, k, src, done, turn, half):
    tiles = range(half * HALF, (half + 1) * HALF)
    for t in tiles:
        nc.vector.bn_stats(k.stats[:, t, :], src[:, t, :]).then_inc(done, 1)
    dve.wait_ge(done, (turn * 2 + half) * 2 * HALF + HALF)
    for t in tiles:
        nc.vector.bn_aggr(k.mv[:, t, :], k.stats[:, t, :]).then_inc(done, 1)


def root_ready(turn, half):
    return 1 + 2 * (turn * 2 + half + 1)


def row_scale(nc, dve, k, src, dst, rstd_ready, turn, half, out_sem):
    dve.wait_ge(rstd_ready, root_ready(turn, half))
    for t in range(half * HALF, (half + 1) * HALF):
        nc.vector.tensor_scalar(dst[:, t, :], src[:, t, :], k.mv[:, t, 0:1], k.rstd[:, t:t + 1],
                                ALU.subtract, ALU.mult).then_inc(out_sem, 1)


def row_scale_by(nc, dve, k, src, by, plus, mid, dst, done, rstd_ready, turn, half, mid_sem, count, out_sem):
    tiles = range(half * HALF, (half + 1) * HALF)
    dve.wait_ge(done, (turn * 2 + half + 1) * 2 * HALF)
    for t in tiles:
        nc.vector.scalar_tensor_tensor(out=mid[:, t, :], in0=src[:, t, :], scalar=k.mv[:, t, 0:1], in1=by(t),
                                       op0=ALU.subtract, op1=ALU.mult).then_inc(mid_sem, 1)
    dve.wait_ge(rstd_ready, root_ready(turn, half))
    for n, t in enumerate(tiles):
        dve.wait_ge(mid_sem, count + n + 1)
        nc.vector.scalar_tensor_tensor(out=dst[:, t, :], in0=mid[:, t, :], scalar=k.rstd[:, t:t + 1], in1=plus(t),
                                       op0=ALU.mult, op1=ALU.add).then_inc(out_sem, 1)


def norm_rows(nc, dve, k, src, dst, done, rstd_ready, turn, out_sem):
    for half in range(2):
        row_stats(nc, dve, k, src, done, turn, half)
    for half in range(2):
        row_scale(nc, dve, k, src, dst, rstd_ready, turn, half, out_sem)


def set_exponent(nc, k, rstd_ready):
    nc.gpsimd.memset(k.minus_half[:, :], -0.5).then_inc(rstd_ready, 1)


def inverse_root(nc, pool, k, done, rstd_ready, turn, eps=LN_EPS, halves=range(2)):
    for half in halves:
        cols = slice(half * HALF, (half + 1) * HALF)
        pool.wait_ge(done, (turn * 2 + half + 1) * 2 * HALF)
        nc.gpsimd.tensor_scalar(k.ve[:, cols], k.mv[:, cols, 1], eps, None, ALU.add).then_inc(rstd_ready, 1)
        pool.wait_ge(rstd_ready, root_ready(turn, half) - 1)
        nc.gpsimd.tensor_tensor(k.rstd[:, cols], k.ve[:, cols], k.minus_half[:, cols], ALU.pow).then_inc(rstd_ready, 1)


def turn_rows(nc, pe, k, banks, xn_ready, base, turned):
    per = NC // P
    for h in range(NH2):
        for t in range(per):
            pe.wait_ge(xn_ready, base + h * per + t + 1)
            for d in range(KD):
                last = nc.tensor.transpose(banks[d * NH2 + h][:, t * P:(t + 1) * P],
                                           k.xn[:, h * per + t, d * P:(d + 1) * P], k.tile["ident"][:, :])
        last.then_inc(turned, 1)


def attention_0(nc, k, src):
    with ExitStack() as ctx:
        sb = lambda name, shape, dt=F32: k.sb(ctx, "a0_" + name, shape, dt)
        w = [sb(f"w{i}", [P, A0_W]) for i in range(2)]
        wo = [sb(f"wo{i}", [P, KD, D]) for i in range(2)]
        parts = lambda name, shape: [sb(f"{name}_{part}", shape, F32R) for part in ("high", "low")]
        wv = k.xT[:, 0, :]
        ws = [parts(f"w{i}", [P, A0_NQ + A0_NK]) for i in range(2)]
        wos = [parts(f"wo{i}", [P, KD * D]) for i in range(2)]
        wvs = parts("wv", [P, KD * A0_G * A0_D])
        bv = sb("bv", [P, A0_G * A0_D])
        cosq, sinq, wmask, slotm, bo = (k.tile["a0_" + n] for n in ("cos", "sin", "mask", "slot", "bo"))
        qT = [[parts(f"qT{i}{j}", [P, T]) for j in range(A0_PAIRS)] for i in range(2)]
        kz = parts("kz", [P, B, 2, S])
        kr = parts("kr", [P, 2, S])
        v = sb("v", [P, A0_G, NT, A0_D + 1])
        t1 = [sb(f"t1{i}", [P, 2, S]) for i in range(2)]
        t2 = [sb(f"t2{i}", [P, 2, S]) for i in range(2)]
        nsink = [sb(f"nsink{i}", [P, A0_R]) for i in range(2)]
        nS = [sb(f"nS{i}", [P, 2, S]) for i in range(2)]
        nm = [sb(f"nm{i}", [P, A0_R]) for i in range(4)]
        Pm = [k.xT[:, i // 2, (i % 2) * NC:(i % 2 + 1) * NC].rearrange("p (h s) -> p h s", h=2) for i in range(4)]
        PT = [sb(f"PT{i}", [P, 2, 2, P]) for i in range(2)]
        ds = sb("ds", [P, 2, A0_R])
        es = [sb(f"es{i}", [P, A0_R]) for i in range(4)]
        den = sb("den", [P, 2, A0_R])
        O = [sb(f"O{i}", [P, A0_R, A0_D]) for i in range(2)]
        OT = [parts(f"OT{i}", [P, 2 * P]) for i in range(2)]
        pp = k.ps(ctx, "a0_pp")
        pS = [k.ps(ctx, f"a0_pS{i}") for i in range(2)]
        pT = k.ps(ctx, "a0_pT")
        pO = [k.ps(ctx, f"a0_pO{i}") for i in range(2)]
        pOT = k.ps(ctx, "a0_pOT")
        pY = k.ps(ctx, "a0_pY")
        turn_banks = [pS[0], pS[1], pT, pOT]
        v_banks = [pS[0], pS[1], pO[0], pO[1]]

        sem = lambda name: k.sem("a0_" + name)
        wv_in, w_in, wo_in = sem("wv_in"), [sem("w_in0"), sem("w_in1")], [sem("wo_in0"), sem("wo_in1")]
        ln, xn_ready, turned, xT_ready = sem("ln"), sem("xn_ready"), sem("turned"), sem("xT_ready")
        proj, roped, chunk = sem("proj"), sem("roped"), sem("chunk")
        valued, v_ready, ns_ready = sem("valued"), sem("v_ready"), sem("ns_ready")
        scored, maxed, probs, turnedP, PT_ready = (sem("scored"), sem("maxed"), sem("probs"),
                                                   sem("turnedP"), sem("PT_ready"))
        pvd, shifted, es_ready, den_ready, O_ready = (sem("pvd"), sem("shifted"), sem("es_ready"),
                                                      sem("den_ready"), sem("O_ready"))
        turnedO, OT_ready, projected, added = sem("turnedO"), sem("OT_ready"), sem("projected"), sem("added")
        x_high, w_high, w_split, wo_high, wo_split, wv_high, wv_split, OT_high = (
            sem("x_high"), sem("w_high"), sem("w_split"), sem("wo_high"), sem("wo_split"), sem("wv_high"),
            sem("wv_split"), sem("OT_high"))
        rotated, rot_high, kr_low = sem("rotated"), sem("rot_high"), sem("kr_low")
        bo_in, ones_set, rstd_ready, gate = sem("bo_in"), sem("ones_set"), sem("rstd_ready"), sem("gate")

        NCH, KEYS = 6, 2

        def chunk_at(G, par, u, last):
            if u == 0:
                return (G, par, NCH - 1)
            return (G + 1, 1 - par, u // 2 - 1) if u % 2 == 0 and u < 2 * NCH and not last else None

        def groups(eng, first, step, last):
            first()
            with eng.Fori(0, (A0_G - 2) // 2) as i:
                for s in range(2):
                    step(i * 2 + (1 + s), (1 + s) % 2)
            last()

        def halves(G, par):
            if isinstance(G, int):
                return 16 * (G // 2 + 1)
            return G * 8 + (16 - 8 * par)

        def part_of(tile, j):
            return tile[:, j // NH2, (j % NH2) * NC:(j % NH2 + 1) * NC]

        block = ctx.enter_context(nc.Block())

        @block.sync
        def _(sp):
            xr = src["x"].rearrange("(t p) d -> p t d", p=P)
            for t in range(NT):
                sp.dma_start(k.x[:, t, :], xr[:, t, :]).then_inc(k.x_in, 16)
            k.fetch(sp, src, "ident")
            sp.dma_start(w[0][:, :], src["a0_w"][0]).then_inc(w_in[0], 16)
            k.fetch(sp, src, "a0")
            sp.dma_start(wv, src["a0_wv"]).then_inc(wv_in, 16)
            sp.dma_start(bv[:, :], src["a0_bv"]).then_inc(wv_in, 16)
            sp.dma_start(wo[0][:, :, :], src["a0_wo"][0]).then_inc(wo_in[0], 16)
            sp.dma_start(w[1][:, :], src["a0_w"][1]).then_inc(w_in[1], 16)
            sp.dma_start(wo[1][:, :, :], src["a0_wo"][1]).then_inc(wo_in[1], 16)
            k.fetch(sp, src, "ctx", "x0", "m0")
            with sp.Fori(0, (A0_G - 2) // 2) as i:
                for s in range(2):
                    g = i * 2 + (2 + s)
                    sp.wait_ge(roped, (g - 1) * NCH)
                    sp.dma_start(w[s][:, :], src["a0_w"][bass.ds(g, 1)].rearrange("g p n -> p (g n)"))\
                        .then_inc(w_in[s], 16)
                    sp.wait_ge(added, (g - 1) * NT)
                    sp.dma_start(wo[s][:, :, :], src["a0_wo"][bass.ds(g, 1)].rearrange("g p c n -> p (g c) n"))\
                        .then_inc(wo_in[s], 16)

        @block.gpsimd
        def _(pool):
            nc.gpsimd.memset(v[:, :, :, A0_D:A0_D + 1], 1.0).then_inc(ones_set, 1)
            set_exponent(nc, k, rstd_ready)
            inverse_root(nc, pool, k, ln, rstd_ready, 0)

            def project(G, par, c):
                pool.wait_ge(roped, G * 6 + c + 1)
                nc.gpsimd.tensor_tensor(t1[c % 2][:, :, :], t1[c % 2][:, :, :], t2[c % 2][:, :, :], ALU.add)\
                    .then_inc(rotated, 1)
                pool.wait_ge(rot_high, G * 6 + c + 1)
                what, half = c % 3, c // 3
                if what != KEYS:
                    cols = slice(half * NC, (half + 1) * NC)
                    high, low = (part[:, cols].rearrange("p (b s) -> p b s", b=2) for part in qT[par][what])
                    nc.gpsimd.tensor_tensor(low, t1[c % 2][:, :, :], high, ALU.subtract).then_inc(chunk, 1)
                else:
                    nc.gpsimd.tensor_tensor(kr[1][:, :, :], t1[c % 2][:, :, :], kr[0][:, :, :], ALU.subtract)\
                        .then_inc(kr_low, 1)
                    k.wait(pool, "a0")
                    pool.wait_ge(kr_low, G * 2 + half + 1)
                    if not (isinstance(G, int) and G == 0):
                        pool.wait_ge(scored, (G - 1) * A0_U + A0_U // 2 * (half + 1))
                    for part in range(2):
                        for slot in range(2):
                            out = nc.gpsimd.tensor_tensor(kz[part][:, 2 * half:2 * half + 2, slot, :], kr[part][:, :, :],
                                                          spread(slotm[:, slot:slot + 1], 2, S), ALU.mult)
                    out.then_inc(chunk, 1)

            def low(counter, n, whole, part, done):
                pool.wait_ge(counter, n)
                nc.gpsimd.tensor_tensor(part[1][:, :], whole, part[0][:, :], ALU.subtract).then_inc(done, 1)

            def w_low(G, par):
                low(w_high, G + 1, w[par][:, 0:A0_NQ + A0_NK], ws[par], w_split)

            def wo_low(G, par):
                low(wo_high, G + 1, wo[par][:, :, :].rearrange("p c n -> p (c n)"), wos[par], wo_split)

            def body(G, par, last=False):
                if not last:
                    w_low(G + 1, 1 - par)
                project(G, par, NCH - 1)
                wo_low(G, par)
                if not last:
                    for c in range(NCH - 1):
                        project(G + 1, 1 - par, c)

            w_low(0, 0)
            for c in range(NCH - 1):
                project(0, 0, c)
            groups(pool, lambda: body(0, 0), body, lambda: body(A0_G - 1, 1, last=True))

        @block.scalar
        def _(act):
            def w_to_high(G, par):
                act.wait_ge(w_in[par], halves(G, par))
                if not (isinstance(G, int) and G < 2):
                    act.wait_ge(proj, (G - 1) * NCH)
                high_of(nc, ws[par][0][:, :], w[par][:, 0:A0_NQ + A0_NK]).then_inc(w_high, 1)

            def wo_to_high(G, par):
                act.wait_ge(wo_in[par], halves(G, par))
                if not (isinstance(G, int) and G < 2):
                    act.wait_ge(projected, (G - 1) * NT)
                high_of(nc, wos[par][0][:, :], wo[par][:, :, :].rearrange("p c n -> p (c n)")).then_inc(wo_high, 1)

            w_to_high(0, 0)
            act.wait_ge(wv_in, 32)
            high_of(nc, wvs[0][:, :], wv).then_inc(wv_high, 1)
            for j in (0, 2, 1, 3):
                act.wait_ge(turned, (j % NH2) + 1)
                high_of(nc, part_of(k.xs[0], j), turn_banks[j][:, :]).then_inc(x_high, 1)

            def exps(G, par, u):
                U = G * A0_U + u
                act.wait_ge(maxed, U + 1)
                if not (isinstance(G, int) and G == 0 and u < 4):
                    act.wait_ge(turnedP, U - 3)
                for h in range(2):
                    out = nc.scalar.activation(Pm[u % 4][:, h, :], nS[u % 2][:, h, :], ACT.Exp,
                                               bias=nm[(u // 2) % 4][:, 2 * (u % 2) + h:2 * (u % 2) + h + 1],
                                               scale=-1.0)
                out.then_inc(probs, 1)

            def evac_PT(G, u):
                U = G * A0_U + u
                act.wait_ge(turnedP, U + 1)
                nc.scalar.copy(PT[u % 2][:, :, :, :].rearrange("p h c q -> p (h c q)"), pT[:, :])\
                    .then_inc(PT_ready, 1)

            def sink_exps(G, j):
                act.wait_ge(shifted, G * NT + j + 1)
                nc.scalar.activation(es[j % 4][:, :], ds[:, j % 2, :], ACT.Exp).then_inc(es_ready, 1)

            def evac_OT(G, j):
                act.wait_ge(turnedO, G * NT + j + 1)
                high_of(nc, OT[j % 2][0][:, :], pOT[:, 0:2 * P]).then_inc(OT_high, 1)

            def rotated_to_high(G, par, c):
                act.wait_ge(rotated, G * NCH + c + 1)
                what, half = c % 3, c // 3
                if what != KEYS:
                    out = qT[par][what][0][:, half * NC:(half + 1) * NC].rearrange("p (b s) -> p b s", b=2)
                else:
                    if not (isinstance(G, int) and G == 0 and half == 0):
                        act.wait_ge(chunk, G * NCH + 3 * half)
                    out = kr[0][:, :, :]
                high_of(nc, out, t1[c % 2][:, :, :]).then_inc(rot_high, 1)

            def body(G, par, first=False, last=False):
                if not last:
                    w_to_high(G + 1, 1 - par)
                wo_to_high(G, par)
                for u in range(A0_U):
                    if u >= 2 or not first:
                        evac_PT(G if u >= 2 else G - 1, (u - 2) % A0_U)
                    if u % 2 == 0 and (u >= 6 or not first):
                        evac_OT(G if u >= 6 else G - 1, (u // 2 - 3) % NT)
                    exps(G, par, u)
                    at = chunk_at(G, par, u - 2, last) if u % 2 == 0 and u >= 2 else None
                    if at:
                        rotated_to_high(*at)
                    if u % 2 == 1:
                        sink_exps(G, u // 2)

            for c in range(NCH - 1):
                rotated_to_high(0, 0, c)
            groups(act, lambda: body(0, 0, True), body, lambda: body(A0_G - 1, 1, last=True))
            for u in range(A0_U, A0_U + 6):
                if u < A0_U + 2:
                    evac_PT(A0_G - 1, u - 2)
                if u % 2 == 0:
                    evac_OT(A0_G - 1, u // 2 - 3)

        @block.vector
        def _(dve):
            dve.wait_ge(k.x_in, 16 * NT)
            norm_rows(nc, dve, k, k.x, k.xn, ln, rstd_ready, 0, xn_ready)
            for i, j in enumerate((0, 2, 1, 3)):
                dve.wait_ge(x_high, i + 1)
                low_of(nc, part_of(k.xs[1], j), turn_banks[j][:, :], part_of(k.xs[0], j)).then_inc(xT_ready, 1)
            dve.wait_ge(wv_high, 1)
            low_of(nc, wvs[1][:, :], wv, wvs[0][:, :]).then_inc(wv_split, 1)
            k.wait(dve, "a0")
            dve.wait_ge(xn_ready, NT)
            for t in range(NT):
                nc.vector.tensor_tensor(k.x[:, t, :], k.x[:, t, :], bo[:, :], ALU.add).then_inc(bo_in, 1)
            dve.wait_ge(bo_in, NT)

            def rope(G, par, c):
                n = c % 2
                bias = w[par][:, A0_W - A0_NB + c % 3:A0_W - A0_NB + c % 3 + 1]
                dve.wait_ge(w_in[par], halves(G, par))
                dve.wait_ge(proj, G * NCH + c + 1)
                if not (isinstance(G, int) and G == 0 and c < 2):
                    dve.wait_ge(chunk, G * NCH + (c - 1))
                a = pp[:, :].rearrange("p (b s) -> p b s", b=2)
                lo, hi = slice(0, 64), slice(64, 128)
                cs = lambda tab, rows: tab[rows, :].rearrange("p (o s) -> p o s", o=1).to_broadcast([rows.stop - rows.start, 2, S])
                nc.vector.scalar_tensor_tensor(out=t1[n][:, :, :], in0=a, scalar=bias,
                                               in1=cs(cosq, slice(0, 128)), op0=ALU.add, op1=ALU.mult)
                nc.vector.scalar_tensor_tensor(out=t2[n][lo, :, :], in0=a[hi], scalar=bias[hi],
                                               in1=cs(sinq, hi), op0=ALU.add, op1=ALU.mult)
                nc.vector.scalar_tensor_tensor(out=t2[n][hi, :, :], in0=a[lo], scalar=bias[lo],
                                               in1=cs(sinq, lo), op0=ALU.add, op1=ALU.mult).then_inc(roped, 1)

            def values(t):
                dve.wait_ge(valued, t + 1)
                nc.vector.tensor_tensor(v[:, :, t, 0:A0_D], v_banks[t % 4][:, :].rearrange("p (g n) -> p g n", g=A0_G),
                                        bv[:, :].rearrange("p (g n) -> p g n", g=A0_G), ALU.add).then_inc(v_ready, 1)

            def sinks(G, par):
                if not (isinstance(G, int) and G < 2):
                    dve.wait_ge(ns_ready, G)
                sink = A0_W - A0_R
                nc.vector.tensor_scalar(nsink[par][:, :], w[par][:, sink:sink + A0_R], -1.0, None,
                                        ALU.mult).then_inc(ns_ready, 1)

            def maxima(G, par, u):
                U, j = G * A0_U + u, u // 2
                k.wait(dve, "a0")
                dve.wait_ge(scored, U + 1)
                if u == 0:
                    dve.wait_ge(ns_ready, G + 1)
                if not (isinstance(G, int) and G == 0 and u < 2):
                    dve.wait_ge(probs, U - 1)
                dve.sem_inc(gate, 1)
                for h in range(2):
                    c = 2 * (u % 2) + h
                    out = nc.vector.tensor_tensor_reduce(
                        nS[u % 2][:, h, :], pS[u % 2][:, h * S:(h + 1) * S], wmask[:, j % 2, :], -1.0,
                        nsink[par][:, c:c + 1], ALU.add, ALU.min, nm[j % 4][:, c:c + 1])
                out.then_inc(maxed, 1)

            def shift(G, par, j):
                dve.wait_ge(maxed, G * A0_U + 2 * j + 2)
                if not (isinstance(G, int) and G == 0 and j < 2):
                    dve.wait_ge(es_ready, G * NT + j - 1)
                nc.vector.tensor_tensor(ds[:, j % 2, :], nm[j % 4][:, :], nsink[par][:, :], ALU.subtract)\
                    .then_inc(shifted, 1)

            def outputs(G, j):
                dve.wait_ge(pvd, G * A0_U + 2 * j + 2)
                dve.wait_ge(es_ready, G * NT + j + 1)
                o = pO[j % 2][:, 0:A0_R * (A0_D + 1)].rearrange("p (h n) -> p h n", h=A0_R)
                nc.vector.tensor_tensor(den[:, 0, :], o[:, :, A0_D], es[j % 4][:, :], ALU.add).then_inc(den_ready, 1)
                dve.wait_ge(den_ready, (G * NT + j) * 2 + 1)
                nc.vector.reciprocal(den[:, 1, :], den[:, 0, :]).then_inc(den_ready, 1)
                dve.wait_ge(den_ready, (G * NT + j) * 2 + 2)
                if not (isinstance(G, int) and G == 0 and j < 2):
                    dve.wait_ge(turnedO, G * NT + j - 1)
                nc.vector.tensor_tensor(O[j % 2][:, :, :], o[:, :, 0:A0_D],
                                        den[:, 1, :].rearrange("p (h o) -> p h o", o=1).to_broadcast([P, A0_R, A0_D]),
                                        ALU.mult).then_inc(O_ready, 1)

            def add_y(G, j):
                dve.wait_ge(projected, G * NT + j + 1)
                if not (isinstance(G, int) and G == 0):
                    dve.wait_ge(added, G * NT + j)
                nc.vector.tensor_tensor(k.x[:, j, :], pY[:, 0:D], k.x[:, j, :], ALU.add).then_inc(added, 1)

            def low_OT(G, j):
                dve.wait_ge(OT_high, G * NT + j + 1)
                low_of(nc, OT[j % 2][1][:, :], pOT[:, 0:2 * P], OT[j % 2][0][:, :]).then_inc(OT_ready, 1)

            def body(G, par, first=False, last=False):
                for u in range(A0_U):
                    maxima(G, par, u)
                    if u % 2 == 1:
                        shift(G, par, u // 2)
                    if u % 2 == 0 and (u >= 4 or not first):
                        outputs(G if u >= 4 else G - 1, (u // 2 - 2) % NT)
                    if u % 2 == 0 and (u >= 6 or not first):
                        low_OT(G if u >= 6 else G - 1, (u // 2 - 3) % NT)
                    if u % 2 == 1 and (u >= 7 or not first):
                        add_y(G if u >= 7 else G - 1, ((u - 1) // 2 - 3) % NT)
                    at = chunk_at(G, par, u, last)
                    if at:
                        rope(*at)
                    if u == 14 and not last:
                        sinks(G + 1, 1 - par)

            dve.wait_ge(wv_in, 32)
            dve.wait_ge(w_in[0], 16)
            sinks(0, 0)
            for t in range(NT):
                if t < NCH - 1:
                    rope(0, 0, t)
                values(t)
            groups(dve, lambda: body(0, 0, True), body, lambda: body(A0_G - 1, 1, last=True))
            for u in range(A0_U, A0_U + 8):
                if u % 2 == 0 and u // 2 - 2 < NT:
                    outputs(A0_G - 1, u // 2 - 2)
                if u % 2 == 0 and u // 2 - 3 < NT:
                    low_OT(A0_G - 1, u // 2 - 3)
                if u % 2 == 1 and (u - 1) // 2 - 3 < NT:
                    add_y(A0_G - 1, (u - 1) // 2 - 3)
            dve.wait_ge(added, A0_G * NT)

        @block.tensor
        def _(pe):
            k.wait(pe, "ident")
            turn_rows(nc, pe, k, turn_banks, xn_ready, 0, turned)

            def chunk_of(G, par, c):
                if c == 0:
                    pe.wait_ge(w_split, G + 1)
                if not (isinstance(G, int) and G == 0 and c == 0):
                    pe.wait_ge(roped, G * NCH + c)
                what, half = c % 3, c // 3
                for d in range(KD):
                    off = (d * A0_PAIRS + what) * P if what != KEYS else A0_NQ + d * P
                    out = split_product(nc, pp[:, :], [g[:, off:off + P] for g in ws[par]],
                                        [x[:, d, half * NC:(half + 1) * NC] for x in k.xs],
                                        start=(d == 0), stop=(d == KD - 1))
                out.then_inc(proj, 1)

            def values_of(t):
                if t >= 4:
                    pe.wait_ge(v_ready, t - 3)
                for d in range(KD):
                    out = split_product(nc, v_banks[t % 4][:, :], [x[:, d, t * P:(t + 1) * P] for x in k.xs],
                                        [g[:, d * NC:(d + 1) * NC] for g in wvs],
                                        start=(d == 0), stop=(d == KD - 1))
                out.then_inc(valued, 1)

            def scores(G, par, u):
                U, b, qt, pair = G * A0_U + u, u // 4, (u // 2) % 2, u % 2
                if u == 0:
                    pe.wait_ge(chunk, G * NCH + 3)
                if u == A0_U // 2:
                    pe.wait_ge(chunk, G * NCH + NCH)
                if not (isinstance(G, int) and G == 0 and u < 2):
                    pe.wait_ge(maxed, U - 1)
                c = b * S + qt * P
                split_product(nc, pS[u % 2][:, :], [g[:, c:c + P] for g in qT[par][pair]],
                              [g[:, b, :, :].rearrange("p h s -> p (h s)") for g in kz],
                              start=True, stop=True).then_inc(scored, 1)

            def values_at(G, t):
                return v[:, G, t, :] if isinstance(G, int) else v[:, bass.ds(G, 1), t, :].rearrange("p g n -> p (g n)")

            def turn_P(G, u):
                U = G * A0_U + u
                pe.wait_ge(probs, U + 1)
                if not (isinstance(G, int) and G == 0 and u < 1):
                    pe.wait_ge(PT_ready, U)
                for h in range(2):
                    for c in range(2):
                        out = nc.tensor.transpose(pT[:, (2 * h + c) * P:(2 * h + c + 1) * P],
                                                  Pm[u % 4][:, h, c * P:(c + 1) * P], k.tile["ident"][:, :])
                out.then_inc(turnedP, 1)

            def weigh(G, par, u):
                U, b, j, pair = G * A0_U + u, u // 4, u // 2, u % 2
                pe.wait_ge(PT_ready, U + 1)
                if pair == 0 and not (isinstance(G, int) and G == 0 and j < 2):
                    pe.wait_ge(O_ready, G * NT + j - 1)
                for h in range(2):
                    c0 = (2 * pair + h) * (A0_D + 1)
                    for c in range(2):
                        out = nc.tensor.matmul(pO[j % 2][:, c0:c0 + A0_D + 1], PT[u % 2][:, h, c, :],
                                               values_at(G, 2 * b + c), start=(c == 0), stop=(c == 1))
                out.then_inc(pvd, 1)

            def turn_O(G, j):
                pe.wait_ge(O_ready, G * NT + j + 1)
                if not (isinstance(G, int) and G == 0 and j < 1):
                    pe.wait_ge(OT_ready, G * NT + j)
                for c in range(2):
                    out = nc.tensor.transpose(pOT[:, c * P:(c + 1) * P],
                                              O[j % 2][:, 2 * c:2 * c + 2, :].rearrange("p h n -> p (h n)"),
                                              k.tile["ident"][:, :])
                out.then_inc(turnedO, 1)

            def project_out(G, par, j):
                if j == 0:
                    pe.wait_ge(wo_split, G + 1)
                pe.wait_ge(OT_ready, G * NT + j + 1)
                if not (isinstance(G, int) and G == 0 and j < 1):
                    pe.wait_ge(added, G * NT + j)
                for c in range(2):
                    out = split_product(nc, pY[:, 0:D], [g[:, c * P:(c + 1) * P] for g in OT[j % 2]],
                                        [g[:, c * D:(c + 1) * D] for g in wos[par]], start=(c == 0), stop=(c == 1))
                out.then_inc(projected, 1)

            def body(G, par, first=False, last=False):
                for u in range(A0_U):
                    scores(G, par, u)
                    if u >= 2 or not first:
                        turn_P(G if u >= 2 else G - 1, (u - 2) % A0_U)
                    if u >= 3 or not first:
                        weigh(G if u >= 3 else G - 1, par if u >= 3 else 1 - par, (u - 3) % A0_U)
                    if u % 2 == 0 and (u >= 6 or not first):
                        turn_O(G if u >= 6 else G - 1, (u // 2 - 3) % NT)
                    at = chunk_at(G, par, u, last)
                    if at:
                        chunk_of(*at)
                    if u % 2 == 1 and (u >= 7 or not first):
                        project_out(G if u >= 7 else G - 1, par if u >= 7 else 1 - par, ((u - 1) // 2 - 3) % NT)

            pe.wait_ge(wv_split, 1)
            pe.wait_ge(xT_ready, 4)
            for t in range(NT):
                if t < NCH - 1:
                    chunk_of(0, 0, t)
                values_of(t)
            pe.wait_ge(ones_set, 1)
            pe.wait_ge(v_ready, NT)
            groups(pe, lambda: body(0, 0, True), body, lambda: body(A0_G - 1, 1, last=True))
            for u in range(A0_U, A0_U + 8):
                if u < A0_U + 2:
                    turn_P(A0_G - 1, u - 2)
                if u < A0_U + 3:
                    weigh(A0_G - 1, 1, u - 3)
                if u % 2 == 0 and u < A0_U + 6:
                    turn_O(A0_G - 1, u // 2 - 3)
                if u % 2 == 1 and u < A0_U + 7:
                    project_out(A0_G - 1, 1, (u - 1) // 2 - 3)


def norm_and_turn(nc, k, ctx, tag, banks, eps=LN_EPS, split=False, whole=True):
    sem = lambda name: k.sem(f"{tag}_{name}")
    ln, rstd_ready, xn_ready, turned, xT_ready = (sem("ln"), sem("rstd_ready"), sem("xn_ready"),
                                                  sem("turned"), sem("xT_ready"))

    def on_vector(dve):
        norm_rows(nc, dve, k, k.x, k.xn, ln, rstd_ready, 0, xn_ready)

    def on_gpsimd(pool):
        set_exponent(nc, k, rstd_ready)
        inverse_root(nc, pool, k, ln, rstd_ready, 0, eps)

    def on_tensor(pe):
        turn_rows(nc, pe, k, banks, xn_ready, 0, turned)
        if whole:
            pe.wait_ge(xT_ready, 4)

    high_ready, low_ready = (sem("high_ready"), sem("low_ready")) if split else (None, None)

    def part(tile, j):
        return tile[:, j // NH2, (j % NH2) * NC:(j % NH2 + 1) * NC]

    BY_HALF = (0, 2, 1, 3)

    def on_scalar(act):
        for j in BY_HALF:
            act.wait_ge(turned, (j % NH2) + 1)
            if whole:
                nc.scalar.copy(part(k.xT, j), banks[j][:, :]).then_inc(xT_ready, 1)
            if split:
                high_of(nc, part(k.xs[0], j), banks[j][:, :]).then_inc(high_ready, 1)

    def lows_on_vector(dve):
        for i, j in enumerate(BY_HALF):
            dve.wait_ge(high_ready, i + 1)
            low_of(nc, part(k.xs[1], j), part(k.xT, j) if whole else banks[j][:, :], part(k.xs[0], j))\
                .then_inc(low_ready, 1)

    if split:
        return on_vector, on_gpsimd, on_tensor, on_scalar, lows_on_vector, low_ready
    return on_vector, on_gpsimd, on_tensor, on_scalar, (ln, rstd_ready, xn_ready, xT_ready)


X0_H, X0_D = 16, 16
X0_HM = P // X0_D
X0_U = 2 * X0_H // 2
X0_CLIP = 50.0


def cross_attention_0(nc, k, src):
    with ExitStack() as ctx:
        sb = lambda name, shape, dt=F32: k.sb(ctx, "x0_" + name, shape, dt)
        w = k.tile["x0_w"]
        cT = k.tile["ctxT"]
        cols = k.tile["x0_cols"]
        rows = k.tile["x0_rows"]
        hmask, rs, mask = k.tile["x0_hmask"], k.tile["x0_rs"], k.tile["x0_mask"]
        keep = sb("keep", [P, NT])
        drop = sb("drop", [P, NT])
        parts = lambda name, shape: [sb(f"{name}_{part}", shape, F32R) for part in ("high", "low")]
        qT = [parts(f"qT{i}", [P, KD, S]) for i in range(2)]
        qz = [parts(f"qz{m}", [P, X0_HM, S]) for m in range(KD)]
        kT = parts("kT", [P, KD, T])
        v = sb("v", [P, NT, X0_H, X0_D + 1])
        clipped = [sb(f"clipped{i}", [P, 2, S]) for i in range(2)]
        PT = [sb(f"PT{i}", [P, 2, S]) for i in range(6)]
        rec = sb("rec", [P, 2, X0_H])
        O = [sb(f"O{i}", [P, X0_H, X0_D]) for i in range(2)]
        OT = [sb(f"OT{i}", [P, KD, P]) for i in range(2)]
        delta = k.xn
        pp = k.ps(ctx, "x0_pp")
        pS = [k.ps(ctx, f"x0_pS{i}") for i in range(2)]
        pO = [k.ps(ctx, f"x0_pO{i}") for i in range(2)]
        pOT = k.ps(ctx, "x0_pOT")
        pY = [k.ps(ctx, f"x0_pY{i}") for i in range(2)]

        sem = lambda name: k.sem("x0_" + name)
        on_vector, on_gpsimd, on_tensor, on_scalar, (ln, rstd_ready, xn_ready, _) = \
            norm_and_turn(nc, k, ctx, "x0", [pS[0], pS[1], pO[0], pO[1]])
        front, back = [pS[0], pS[1], pO[0], pO[1]], [pp, pOT, pY[0], pY[1]]
        ones_set = sem("ones_set")
        k_high, q_high, qz_first = sem("k_high"), sem("q_high"), sem("qz_first")
        consts, keyed, k_out, valued, v_out = sem("consts"), sem("keyed"), sem("k_out"), sem("valued"), sem("v_out")
        proj, q_out, qz_ready = sem("proj"), sem("q_out"), sem("qz_ready")
        scored, clip_done, probs, weighed = sem("scored"), sem("clip_done"), sem("probs"), sem("weighed")
        rec_ready, O_ready, turnedO, OT_ready = sem("rec_ready"), sem("O_ready"), sem("turnedO"), sem("OT_ready")
        projected, shaped, scaled, dn, summed = (sem("projected"), sem("shaped"), sem("scaled"), sem("dn"),
                                                 sem("summed"))
        block = ctx.enter_context(nc.Block())

        @block.sync
        def _(sp):
            k.fetch(sp, src, "a1", "x1", "f1")

        def spread_heads(eng, b, m, done):
            for part in range(2):
                eng.tensor_tensor(qz[m][part][:, :, :],
                                  qT[b % 2][part][:, m:m + 1, :].to_broadcast([P, X0_HM, S]),
                                  hmask[:, :].rearrange("p (h o) -> p h o", o=1).to_broadcast([P, X0_HM, S]),
                                  ALU.mult).then_inc(done, 1)

        @block.gpsimd
        def _(pool):
            nc.gpsimd.memset(v[:, :, :, X0_D:X0_D + 1], 1.0).then_inc(ones_set, 1)
            on_gpsimd(pool)
            k.wait(pool, "x0")
            for b in range(B):
                for m in range(KD):
                    if (b, m) != (0, 0):
                        if m == 0 or b == 0:
                            pool.wait_ge(q_out, b + 1)
                        if b >= 1:
                            pool.wait_ge(scored, X0_U * (b - 1) + X0_U // 2 * (m + 1))
                        spread_heads(nc.gpsimd, b, m, qz_ready)
            inverse_root(nc, pool, k, ln, rstd_ready, 1)

        @block.scalar
        def _(act):
            k.wait(act, "x0")
            for m in range(KD):
                for half in range(NH2):
                    act.wait_ge(keyed, 2 * m + half + 1)
                    nc.scalar.activation(kT[0][:, m, half * NC:(half + 1) * NC], front[2 * m + half][:, :], ACT.Identity,
                                         bias=cols[:, 2 + m:3 + m]).then_inc(k_high, 1)
            on_scalar(act)

            def queries_out(b):
                act.wait_ge(proj, b + 1)
                if b >= 2:
                    act.wait_ge(qz_ready, 4 * (b - 1) - 2)
                    if b == 2:
                        act.wait_ge(qz_first, 2)
                for m in range(KD):
                    nc.scalar.activation(qT[b % 2][0][:, m, :], pp[:, m * S:(m + 1) * S], ACT.Identity,
                                         bias=cols[:, m:m + 1]).then_inc(q_high, 1)

            queries_out(0)
            for U in range(B * X0_U + 10):
                b, u = U // X0_U, U % X0_U
                if U < B * X0_U:
                    kt = u % 2
                    act.wait_ge(clip_done, U + 1)
                    if U == 0:
                        act.wait_ge(consts, 3)
                    if U >= 6:
                        act.wait_ge(weighed, (U - 6) // 2 + 1)
                    nc.scalar.activation(PT[U % 6][:, :, :], clipped[U % 2][:, :, :], ACT.Exp,
                                         scale=keep[:, 2 * b + kt:2 * b + kt + 1],
                                         bias=drop[:, 2 * b + kt:2 * b + kt + 1]).then_inc(probs, 1)
                    if u == 4 and b + 1 < B:
                        queries_out(b + 1)
                for qt in range(2):
                    r = U - X0_U - 8 - qt
                    if r >= 0 and r % X0_U == 0:
                        j = 2 * (r // X0_U) + qt
                        act.wait_ge(turnedO, j + 1)
                        nc.scalar.copy(OT[qt][:, :, :].rearrange("p c q -> p (c q)"), pOT[:, 0:2 * P])\
                            .then_inc(OT_ready, 1)

        @block.vector
        def _(dve):
            on_vector(dve)
            k.wait(dve, "x0")
            for m in range(KD):
                for half in range(NH2):
                    dve.wait_ge(k_high, 2 * m + half + 1)
                    tokens = slice(half * NC, (half + 1) * NC)
                    nc.vector.scalar_tensor_tensor(out=kT[1][:, m, tokens], in0=front[2 * m + half][:, :],
                                                   scalar=cols[:, 2 + m:3 + m], in1=kT[0][:, m, tokens],
                                                   op0=ALU.add, op1=ALU.subtract).then_inc(k_out, 1)
            nc.vector.tensor_scalar(rs[:, :], rs[:, :], 0.0, 0.3, ALU.max, ALU.min).then_inc(consts, 1)
            nc.vector.tensor_scalar(keep[:, :], mask[:, :], 0.5, None, ALU.is_gt).then_inc(consts, 1)
            dve.wait_ge(consts, 2)
            nc.vector.tensor_scalar(drop[:, :], keep[:, :], 1.0, X0_CLIP, ALU.subtract, ALU.mult).then_inc(consts, 1)
            dve.wait_ge(xn_ready, NT)
            for t in range(NT):
                nc.vector.tensor_tensor(k.x[:, t, :], k.x[:, t, :], rows[:, 3, :], ALU.add).then_inc(shaped, 1)

            def normalise(b, qt):
                j = 2 * b + qt
                dve.wait_ge(weighed, X0_H // 2 * (b + 1))
                o = pO[qt][:, 0:X0_H * (X0_D + 1)].rearrange("p (h n) -> p h n", h=X0_H)
                nc.vector.reciprocal(rec[:, qt, :], o[:, :, X0_D]).then_inc(rec_ready, 1)
                dve.wait_ge(rec_ready, j + 1)
                if b >= 1:
                    dve.wait_ge(turnedO, j - 1)
                nc.vector.tensor_tensor(O[qt][:, :, :], o[:, :, 0:X0_D],
                                        rec[:, qt, :].rearrange("p (h o) -> p h o", o=1).to_broadcast([P, X0_H, X0_D]),
                                        ALU.mult).then_inc(O_ready, 1)

            def scale_delta(b, qt):
                j = 2 * b + qt
                dve.wait_ge(projected, j + 1)
                nc.vector.tensor_tensor(delta[:, j, :], pY[qt][:, 0:D], rows[:, 1, :],
                                        ALU.add).then_inc(scaled, 1)
                dve.wait_ge(scaled, 2 * j + 1)
                nc.vector.tensor_scalar(delta[:, j, :], delta[:, j, :], rs[:, 0:1], None, ALU.mult)\
                    .then_inc(scaled, 1)

            def add_normed(half):
                dve.wait_ge(scaled, (half + 1) * NT)
                row_stats(nc, dve, k, delta, ln, 1, half)
                if half == 0:
                    dve.wait_ge(shaped, NT)
                row_scale_by(nc, dve, k, delta, lambda t: rows[:, 2, :], lambda t: k.x[:, t, :], delta, k.x,
                             ln, rstd_ready, 1, half, summed, half * HALF, dn)
                dve.wait_ge(dn, (half + 1) * HALF)

            def queries_low(b):
                dve.wait_ge(q_high, 2 * b + 2)
                for m in range(KD):
                    out = nc.vector.scalar_tensor_tensor(out=qT[b % 2][1][:, m, :], in0=pp[:, m * S:(m + 1) * S],
                                                         scalar=cols[:, m:m + 1], in1=qT[b % 2][0][:, m, :],
                                                         op0=ALU.add, op1=ALU.subtract)
                out.then_inc(q_out, 1)

            bv = rows[:, 0, :].rearrange("p (h n) -> p h n", h=X0_H)
            def values_out(t):
                dve.wait_ge(valued, t // 2 + 1)
                nc.vector.tensor_tensor(v[:, t, :, 0:X0_D],
                                        back[t // 2][:, (t % 2) * D:(t % 2 + 1) * D].rearrange("p (h n) -> p h n", h=X0_H),
                                        bv, ALU.add).then_inc(v_out, 1)

            values_out(0)
            values_out(1)
            queries_low(0)
            dve.wait_ge(q_out, 1)
            spread_heads(nc.vector, 0, 0, qz_first)
            for t in range(2, NT):
                values_out(t)
            for U in range(B * X0_U + 12):
                b, u = U // X0_U, U % X0_U
                if u == 6 and b + 1 < B:
                    queries_low(b + 1)
                if U == (B - 1) * X0_U + 4:
                    add_normed(0)
                if U < B * X0_U:
                    dve.wait_ge(scored, U + 1)
                    if U >= 2:
                        dve.wait_ge(probs, U - 1)
                    nc.vector.tensor_scalar(clipped[U % 2][:, :, :].rearrange("p h s -> p (h s)"), pS[U % 2][:, :],
                                            X0_CLIP, -X0_CLIP, ALU.min, ALU.max).then_inc(clip_done, 1)
                for qt in range(2):
                    r = U - X0_U - 3
                    if r >= 0 and r % X0_U == 0:
                        normalise(r // X0_U, qt)
                    r = U - X0_U - 10 - qt
                    if r >= 0 and r % X0_U == 0:
                        scale_delta(r // X0_U, qt)
            add_normed(1)

        @block.tensor
        def _(pe):
            k.wait(pe, "x0")
            k.wait(pe, "ctx")
            for m in range(KD):
                for half in range(NH2):
                    for d in range(KD):
                        out = nc.tensor.matmul(front[2 * m + half][:, :], w[:, 1, d, m * P:(m + 1) * P],
                                               cT[:, d, half * NC:(half + 1) * NC], start=(d == 0), stop=(d == KD - 1))
                    out.then_inc(keyed, 1)
            for t in range(NT):
                for d in range(KD):
                    out = nc.tensor.matmul(back[t // 2][:, (t % 2) * D:(t % 2 + 1) * D], cT[:, d, t * P:(t + 1) * P],
                                           w[:, 2, d, :], start=(d == 0), stop=(d == KD - 1))
                if t % 2 == 1:
                    out.then_inc(valued, 1)
            pe.wait_ge(k_out, 4)
            on_tensor(pe)

            def project_queries(b):
                if b == 0:
                    pe.wait_ge(v_out, 2)
                else:
                    pe.wait_ge(q_out, b)
                for m in range(KD):
                    for d in range(KD):
                        out = nc.tensor.matmul(pp[:, m * S:(m + 1) * S], w[:, 0, d, m * P:(m + 1) * P],
                                               k.xT[:, d, b * S:(b + 1) * S], start=(d == 0), stop=(d == KD - 1))
                out.then_inc(proj, 1)

            def scores(U):
                b, u = U // X0_U, U % X0_U
                h, kt = 2 * (u // 2), u % 2
                if u % (X0_U // 2) == 0:
                    if U == 0:
                        pe.wait_ge(qz_first, 2)
                    else:
                        pe.wait_ge(qz_ready, 4 * b + 2 * (u // (X0_U // 2)))
                if U >= 2:
                    pe.wait_ge(clip_done, U - 1)
                m = h // X0_HM
                split_product(nc, pS[U % 2][:, :], [g[:, m, b * S + kt * P:b * S + (kt + 1) * P] for g in kT],
                              [g[:, h % X0_HM:h % X0_HM + 2, :].rearrange("p h s -> p (h s)") for g in qz[m]],
                              start=True, stop=True).then_inc(scored, 1)

            def weigh(n):
                b, pair = n // (X0_H // 2), n % (X0_H // 2)
                pe.wait_ge(probs, 2 * n + 2)
                if n == 0:
                    pe.wait_ge(v_out, NT)
                    pe.wait_ge(ones_set, 1)
                if pair == 0:
                    if b >= 1:
                        pe.wait_ge(O_ready, 2 * b)
                for h in range(2):
                    c0 = (2 * pair + h) * (X0_D + 1)
                    for qt in range(2):
                        for kt in range(2):
                            out = nc.tensor.matmul(pO[qt][:, c0:c0 + X0_D + 1],
                                                   PT[(2 * n + kt) % 6][:, h, qt * P:(qt + 1) * P],
                                                   v[:, 2 * b + kt, 2 * pair + h, :], start=(kt == 0), stop=(kt == 1))
                out.then_inc(weighed, 1)

            def turn_O(b, qt):
                j = 2 * b + qt
                pe.wait_ge(O_ready, j + 1)
                if j >= 1:
                    pe.wait_ge(OT_ready, j)
                for c in range(KD):
                    out = nc.tensor.transpose(pOT[:, c * P:(c + 1) * P],
                                              O[qt][:, c * X0_HM:(c + 1) * X0_HM, :].rearrange("p h n -> p (h n)"),
                                              k.tile["ident"][:, :])
                out.then_inc(turnedO, 1)

            def project_out(b, qt):
                j = 2 * b + qt
                pe.wait_ge(OT_ready, j + 1)
                if b >= 1:
                    pe.wait_ge(scaled, 2 * (j - 2) + 1)
                for c in range(KD):
                    out = nc.tensor.matmul(pY[qt][:, 0:D], OT[qt][:, c, :], w[:, 3, c, :],
                                           start=(c == 0), stop=(c == KD - 1))
                out.then_inc(projected, 1)

            project_queries(0)
            for U in range(B * X0_U + 12):
                b, u = U // X0_U, U % X0_U
                if U < B * X0_U:
                    scores(U)
                    if u == 4 and b + 1 < B:
                        project_queries(b + 1)
                if U % 2 == 0 and 0 <= (U - 4) // 2 < B * X0_H // 2 and U >= 4:
                    weigh((U - 4) // 2)
                for qt in range(2):
                    r = U - X0_U - 8 - qt
                    if r >= 0 and r % X0_U == 0:
                        turn_O(r // X0_U, qt)
                    r = U - X0_U - 9 - qt
                    if r >= 0 and r % X0_U == 0:
                        project_out(r // X0_U, qt)


M0_E, M0_I, M0_SH = 8, 176, 704
M0_GRAN = 16
M0_PER = M0_I // M0_GRAN
M0_TILES = -(-(M0_E * M0_I + M0_SH) // P)
M0_COLS = -(-M0_TILES * P // M0_I)
WT = 3 * D


def experts_0(nc, k, src):
    with ExitStack() as ctx:
        sb = lambda name, shape, dt=F32: k.sb(ctx, "m0_" + name, shape, dt)
        rw, iota = k.tile["m0_rw"], k.tile["m0_iota"]
        lg = sb("lg", [P, NT, M0_E + 1])
        top = sb("top", [P, NT, 8])
        at = sb("at", [P, NT, 8], U32)
        atf = sb("atf", [P, NT, 2])
        gap = sb("gap", [P, NT, 2])
        eg = sb("eg", [P, NT, 2])
        share = sb("share", [P, NT, 3])
        hot = sb("hot", [P, NT, 2, M0_E])
        comb = sb("comb", [P, NT, M0_COLS])
        combT = sb("combT", [M0_COLS, T])
        zeros = sb("zeros", [P, NC], BF16)
        gu = [k.tile[f"m0_gu{i}"] for i in range(2)]
        dn = [k.tile[f"m0_dn{i}"] for i in range(2)]
        cw = [sb(f"cw{i}", [P, T]) for i in range(2)]
        parts = lambda name, shape: [sb(f"{name}_{part}", shape, F32R) for part in ("high", "low")]
        gus = [parts(f"gu{i}", [P, 2 * D]) for i in range(2)]
        dns = [parts(f"dn{i}", [P, D]) for i in range(2)]
        sg = [sb(f"sg{i}", [P, NC]) for i in range(2)]
        hu = [sb(f"hu{h}", [P, NC]) for h in range(2)]
        hT = [sb(f"hT{h}", [P, NC]) for h in range(2)]
        hs = [parts(f"h{i}", [P, T]) for i in range(2)]
        pg = [k.ps(ctx, f"m0_pg{i}") for i in range(2)]
        pu = [k.ps(ctx, f"m0_pu{i}") for i in range(2)]
        acc = [k.ps(ctx, f"m0_acc{i}") for i in range(4)]
        table = nc.dram_tensor("m0_table", (M0_COLS, M0_PER, T), F32, kind="Internal").ap()

        sem = lambda name: k.sem("m0_" + name)
        on_vector, on_gpsimd, on_tensor, on_scalar, lows_on_vector, x_split = \
            norm_and_turn(nc, k, ctx, "m0", [pg[0], pg[1], pu[0], pu[1]], split=True)
        zero_set = sem("zero_set")
        gu_in, dn_in = [sem(f"gu_in{i}") for i in range(2)], [sem(f"dn_in{i}") for i in range(2)]
        cw_in = [sem(f"cw_in{i}") for i in range(2)]
        logits, lg_ready, routed, gates, comb_ready = (sem("logits"), sem("lg_ready"), sem("routed"),
                                                       sem("gates"), sem("comb_ready"))
        turnedC, combT_ready, table_out = sem("turnedC"), sem("combT_ready"), sem("table_out")
        gated, silu_done, up_done, h_ready, down_done, added = (sem("gated"), sem("silu_done"), sem("up_done"),
                                                                sem("h_ready"), sem("down_done"), sem("added"))
        gu_high, gu_split, dn_high, dn_split = sem("gu_high"), sem("gu_split"), sem("dn_high"), sem("dn_split")
        h_high, h_split = sem("h_high"), sem("h_split")
        block = ctx.enter_context(nc.Block())
        LAST = M0_TILES - 1
        PAIRS = (M0_TILES - 3) // 2
        assert M0_TILES == 3 + 2 * PAIRS

        def tiles(eng, step):
            step(0, 0)
            step(1, 1)
            with eng.Fori(0, PAIRS) as i:
                for s in range(2):
                    step(i * 2 + (2 + s), s)
            step(LAST, LAST % 2)

        def early(n, count):
            return isinstance(n, int) and n < count

        def arrivals(n, par, ahead=1):
            return 16 * (n // 2 + 1 - ahead) if isinstance(n, int) else n * 8 + (16 - 16 * ahead - 8 * par)

        @block.sync
        def _(sp):
            sp.wait_ge(combT_ready, 2)
            spread_rows = combT[:, :].rearrange("e (o t) -> e o t", o=1).to_broadcast([M0_COLS, M0_PER, T])
            sp.dma_start(table, spread_rows).then_inc(table_out, 16)
            sp.wait_ge(table_out, 16)
            rows = table.rearrange("e g t -> (e g) t")

            def weights_of(n, par):
                sp.dma_start(cw[par][:, :], per_granule(rows, n)).then_inc(cw_in[par], 16)

            def step(n, par):
                sp.wait_ge(gu_split, n + 1)
                sp.dma_start(gu[par][:, :], src["m0_gu"][bass.ds(n + 2, 1)].rearrange("g p n -> p (g n)"))\
                    .then_inc(gu_in[par], 16)
                sp.wait_ge(h_ready, 2 * n + 2)
                weights_of(n + 2, par)
                sp.wait_ge(dn_split, n + 1)
                sp.dma_start(dn[par][:, :], src["m0_dn"][bass.ds(n + 2, 1)].rearrange("g p n -> p (g n)"))\
                    .then_inc(dn_in[par], 16)

            def per_granule(rows, n):
                g = rows[bass.ds(n * (P // M0_GRAN), P // M0_GRAN)]
                return g.rearrange("(g o) t -> g o t", o=1).to_broadcast([P // M0_GRAN, M0_GRAN, T])

            weights_of(0, 0)
            weights_of(1, 1)
            with sp.Fori(0, PAIRS) as i:
                for s in range(2):
                    step(i * 2 + s, s)
            step(LAST - 2, LAST % 2)

        @block.gpsimd
        def _(pool):
            nc.gpsimd.memset(zeros[:, :], 0.0).then_inc(zero_set, 1)
            on_gpsimd(pool)

        @block.scalar
        def _(act):
            def gate_up_high(n, par):
                if early(n, 2):
                    k.wait(act, "m0")
                else:
                    act.wait_ge(gu_in[par], arrivals(n, par))
                    act.wait_ge(gated, 2 * n - 2)
                high_of(nc, gus[par][0][:, :], gu[par][:, :]).then_inc(gu_high, 1)

            def down_high(n, par):
                if early(n, 2):
                    k.wait(act, "m0")
                else:
                    act.wait_ge(dn_in[par], arrivals(n, par))
                    act.wait_ge(down_done, n - 1)
                high_of(nc, dns[par][0][:, :], dn[par][:, :]).then_inc(dn_high, 1)

            gate_up_high(0, 0)
            on_scalar(act)
            act.wait_ge(gates, 1)
            nc.scalar.activation(eg[:, :, :], gap[:, :, :], ACT.Exp).then_inc(gates, 1)
            for h in range(2):
                act.wait_ge(turnedC, 1)
                nc.scalar.copy(combT[:, h * NC:(h + 1) * NC], acc[1 + h][0:M0_COLS, :]).then_inc(combT_ready, 1)

            def step(n, par):
                if not (isinstance(n, int) and n == LAST):
                    gate_up_high(n + 1, 1 - par)
                for h in range(2):
                    act.wait_ge(gated, 2 * n + h + 1)
                    if not early(n, 1):
                        act.wait_ge(up_done, 2 * n + h - 1)
                    nc.scalar.activation(sg[h][:, :], pg[h][:, :], ACT.Silu).then_inc(silu_done, 1)
                down_high(n, par)
                for h in range(2):
                    act.wait_ge(h_ready, 2 * n + h + 1)
                    high_of(nc, hs[par][0][:, h * NC:(h + 1) * NC], hT[h][:, :]).then_inc(h_high, 1)

            tiles(act, step)

        @block.vector
        def _(dve):
            def gate_up_low(n, par):
                dve.wait_ge(gu_high, n + 1)
                low_of(nc, gus[par][1][:, :], gu[par][:, :], gus[par][0][:, :]).then_inc(gu_split, 1)

            def down_low(n, par):
                dve.wait_ge(dn_high, n + 1)
                low_of(nc, dns[par][1][:, :], dn[par][:, :], dns[par][0][:, :]).then_inc(dn_split, 1)

            def h_low(n, par):
                for h in range(2):
                    dve.wait_ge(h_high, 2 * n + h + 1)
                    half = slice(h * NC, (h + 1) * NC)
                    low_of(nc, hs[par][1][:, half], hT[h][:, :], hs[par][0][:, half]).then_inc(h_split, 1)

            on_vector(dve)
            gate_up_low(0, 0)
            lows_on_vector(dve)
            k.wait(dve, "m0")
            dve.wait_ge(logits, 1)
            nc.vector.tensor_copy(lg[:, :, :], acc[0][:, 0:NT * (M0_E + 1)].rearrange("p (t e) -> p t e", t=NT))\
                .then_inc(lg_ready, 1)
            dve.wait_ge(lg_ready, 1)
            for t in range(NT):
                nc.vector.max(top[:, t, :], lg[:, t, 0:M0_E]).then_inc(routed, 1)
            for t in range(NT):
                dve.wait_ge(routed, t + 1)
                nc.vector.max_index(at[:, t, :], top[:, t, :], lg[:, t, 0:M0_E]).then_inc(lg_ready, 1)
            dve.wait_ge(lg_ready, 1 + NT)
            nc.vector.tensor_tensor(gap[:, :, 0:1], top[:, :, 1:2], top[:, :, 0:1], ALU.subtract)
            nc.vector.tensor_scalar(gap[:, :, 1:2], lg[:, :, M0_E:M0_E + 1], -1.0, None, ALU.mult).then_inc(gates, 1)
            nc.vector.tensor_copy(atf[:, :, :], at[:, :, 0:2]).then_inc(comb_ready, 1)
            dve.wait_ge(comb_ready, 1)
            for c in range(2):
                nc.vector.tensor_tensor(hot[:, :, c, :], iota[:, :].rearrange("p (o e) -> p o e", o=1).to_broadcast([P, NT, M0_E]),
                                        atf[:, :, c:c + 1].to_broadcast([P, NT, M0_E]), ALU.is_equal)\
                    .then_inc(comb_ready, 1)
            dve.wait_ge(gates, 2)
            nc.vector.tensor_scalar(eg[:, :, :], eg[:, :, :], 1.0, None, ALU.add).then_inc(comb_ready, 1)
            dve.wait_ge(comb_ready, 4)
            nc.vector.reciprocal(share[:, :, 0:2], eg[:, :, :]).then_inc(comb_ready, 1)
            dve.wait_ge(comb_ready, 5)
            nc.vector.tensor_scalar(eg[:, :, 0:1], eg[:, :, 0:1], 1.0, None, ALU.subtract).then_inc(comb_ready, 1)
            dve.wait_ge(comb_ready, 6)
            nc.vector.tensor_tensor(share[:, :, 2:3], eg[:, :, 0:1], share[:, :, 0:1], ALU.mult).then_inc(comb_ready, 1)
            dve.wait_ge(comb_ready, 7)
            for c, s in ((0, 0), (1, 2)):
                nc.vector.tensor_tensor(hot[:, :, c, :], hot[:, :, c, :],
                                        share[:, :, s:s + 1].to_broadcast([P, NT, M0_E]), ALU.mult)\
                    .then_inc(comb_ready, 1)
            nc.vector.tensor_copy(comb[:, :, M0_E:M0_COLS], share[:, :, 1:2].to_broadcast([P, NT, M0_COLS - M0_E]))\
                .then_inc(comb_ready, 1)
            dve.wait_ge(comb_ready, 10)
            nc.vector.tensor_tensor(comb[:, :, 0:M0_E], hot[:, :, 0, :], hot[:, :, 1, :], ALU.add).then_inc(comb_ready, 1)

            def times_up(n, par):
                for h in range(2):
                    dve.wait_ge(silu_done, 2 * n + h + 1)
                    if not early(n, 1):
                        dve.wait_ge(h_ready, 2 * n + h - 1)
                    nc.vector.tensor_tensor(hu[h][:, :], sg[h][:, :], pu[h][:, :], ALU.mult).then_inc(up_done, 1)

            def times_combine(n, par):
                dve.wait_ge(cw_in[par], arrivals(n, par, 0))
                for h in range(2):
                    dve.wait_ge(up_done, 2 * n + h + 1)
                    if not early(n, 1):
                        dve.wait_ge(h_split, 2 * n + h - 1)
                    nc.vector.tensor_tensor(hT[h][:, :], hu[h][:, :], cw[par][:, h * NC:(h + 1) * NC],
                                            ALU.mult).then_inc(h_ready, 1)

            def step(n, par):
                if not (isinstance(n, int) and n == LAST):
                    gate_up_low(n + 1, 1 - par)
                times_up(n, par)
                times_combine(n, par)
                down_low(n, par)
                h_low(n, par)

            tiles(dve, step)
            dve.wait_ge(down_done, M0_TILES)
            for a in range(4):
                nc.vector.tensor_tensor(k.x[:, 2 * a:2 * a + 2, :], acc[a][:, :].rearrange("p (t n) -> p t n", t=2),
                                        k.x[:, 2 * a:2 * a + 2, :], ALU.add).then_inc(added, 1)
            dve.wait_ge(added, 4)

        @block.tensor
        def _(pe):
            k.wait(pe, "m0")
            on_tensor(pe)
            for t in range(NT):
                for d in range(KD):
                    out = nc.tensor.matmul(acc[0][:, t * (M0_E + 1):(t + 1) * (M0_E + 1)], k.xT[:, d, t * P:(t + 1) * P],
                                           rw[:, d, :], start=(d == 0), stop=(d == KD - 1))
            out.then_inc(logits, 1)

            def gate_up(n, par):
                pe.wait_ge(gu_split, n + 1)
                for h in range(2):
                    if early(n, 1):
                        pe.wait_ge(x_split, 2 * h + 2)
                    else:
                        pe.wait_ge(up_done, 2 * n + h - 1)
                    for bank, off in ((pg[h], 0), (pu[h], D)):
                        for d in range(KD):
                            out = split_product(nc, bank[:, :], [g[:, off + d * P:off + (d + 1) * P] for g in gus[par]],
                                                [x[:, d, h * NC:(h + 1) * NC] for x in k.xs],
                                                start=(d == 0), stop=(d == KD - 1))
                    out.then_inc(gated, 1)

            def down(n, par, last=False):
                pe.wait_ge(dn_split, n + 1)
                for h in range(2):
                    pe.wait_ge(h_split, 2 * n + h + 1)
                    for t in range(h * NT // 2, (h + 1) * NT // 2):
                        out = split_product(nc, acc[t // 2][:, (t % 2) * D:(t % 2 + 1) * D],
                                            [g[:, t * P:(t + 1) * P] for g in hs[par]], [g[:, :] for g in dns[par]],
                                            start=False, stop=last, skip_group_check=True)
                out.then_inc(down_done, 1)

            gate_up(0, 0)
            pe.wait_ge(comb_ready, 11)
            for t in range(NT):
                out = nc.tensor.transpose(acc[1 + t // 4][0:M0_COLS, (t % 4) * P:(t % 4 + 1) * P], comb[:, t, :], k.tile["ident"][:, :])
            out.then_inc(turnedC, 1)
            pe.wait_ge(combT_ready, 2)
            pe.wait_ge(lg_ready, 1)
            pe.wait_ge(zero_set, 1)
            for a in range(4):
                nc.tensor.matmul(acc[a][:, :], zeros[:, 0:P], zeros[:, :], start=True, stop=False, skip_group_check=True)
            gate_up(1, 1)
            down(0, 0)
            with pe.Fori(0, PAIRS) as i:
                for s in range(2):
                    gate_up(i * 2 + (2 + s), s)
                    down(i * 2 + (1 + s), 1 - s)
            gate_up(LAST, LAST % 2)
            down(LAST - 1, 1 - LAST % 2)
            down(LAST, LAST % 2, last=True)


def store_x(nc, k, out):
    with ExitStack() as ctx:
        stored = k.sem("stored")
        block = ctx.enter_context(nc.Block())

        @block.sync
        def _(sp):
            for t in range(NT):
                sp.dma_start(out.rearrange("(t p) d -> p t d", p=P)[:, t, :], k.x[:, t, :]).then_inc(stored, 16)
            sp.wait_ge(stored, 16 * NT)


def attention_1(nc, k, src):
    with ExitStack() as ctx:
        sb = lambda name, shape, dt=F32: k.sb(ctx, "a1_" + name, shape, dt)
        w = [k.tile[f"a1_w{i}"] for i in range(2)]
        wv = k.tile["a1_wv0"]
        wo = [k.tile["a1_wo0"], sb("wo1", [P, D + P])]
        parts = lambda name, shape: [sb(f"{name}_{part}", shape, F32R) for part in ("high", "low")]
        ws = [parts(f"w{i}", [P, 2 * KD * P]) for i in range(2)]
        wvs = parts("wv", [P, KD * 2 * P])
        wos = [parts(f"wo{i}", [P, D]) for i in range(2)]
        cs = k.tile["a1_cs"]
        cmask = k.tile["a1_mask"]
        rows = k.tile["a1_rows"]
        qT = [sb(f"qT{i}", [P, T]) for i in range(2)]
        kT = [sb(f"kT{i}", [P, T]) for i in range(2)]
        v = sb("v", [P, 2, NT, P + 1])
        t1 = [sb(f"t1{i}", [P, 2, S]) for i in range(2)]
        t2 = [sb(f"t2{i}", [P, 2, S]) for i in range(2)]
        hn = sb("hn", [P, NT, D])
        nS = [sb(f"nS{i}", [P, 3 * P]) for i in range(2)]
        nm = [sb(f"nm{i}", [P, 2]) for i in range(2)]
        Pm = [sb(f"Pm{i}", [P, 3 * P]) for i in range(2)]
        PT = [sb(f"PT{i}", [P, 3, P]) for i in range(2)]
        rec = sb("rec", [P, 2])
        O = [sb(f"O{i}", [P, 2, P]) for i in range(2)]
        OT = [parts(f"OT{i}", [P, 2 * P]) for i in range(2)]
        pp = [k.ps(ctx, f"a1_pp{i}") for i in range(2)]
        pS = [k.ps(ctx, f"a1_pS{i}") for i in range(2)]
        pT = k.ps(ctx, "a1_pT")
        pO = k.ps(ctx, "a1_pO")
        pOT = k.ps(ctx, "a1_pOT")
        pY = k.ps(ctx, "a1_pY")
        turn_banks = [pS[0], pS[1], pT, pO]

        sem = lambda name: k.sem("a1_" + name)
        ones_set, gate = sem("ones_set"), sem("gate")
        w_in, wo_in, wv_in = [sem("w_in0"), sem("w_in1")], [sem("wo_in0"), sem("wo_in1")], sem("wv_in")
        w_high, w_split, wo_high, wo_split, wv_high, wv_split = (sem("w_high"), sem("w_split"), sem("wo_high"),
                                                                 sem("wo_split"), sem("wv_high"), sem("wv_split"))
        swapped, OT_high, x_high = sem("swapped"), sem("OT_high"), sem("x_high")
        ln, rstd_ready, h_ready, xn_ready = sem("ln"), sem("rstd_ready"), sem("h_ready"), sem("xn_ready")
        turned, xT_ready, based = sem("turned"), sem("xT_ready"), sem("based")
        proj, roped, chunk, v_ready = sem("proj"), sem("roped"), sem("chunk"), sem("v_ready")
        scored, maxed, probs, turnedP, PT_ready = (sem("scored"), sem("maxed"), sem("probs"),
                                                   sem("turnedP"), sem("PT_ready"))
        weighed, rec_ready, O_ready = sem("weighed"), sem("rec_ready"), sem("O_ready")
        turnedO, OT_ready, projected, added = sem("turnedO"), sem("OT_ready"), sem("projected"), sem("added")

        def heads(eng, step):
            step(0, 0, first=True)
            with eng.Fori(0, (A1_H - 2) // 2) as i:
                for s in range(2):
                    step(i * 2 + (1 + s), (1 + s) % 2)
            step(A1_H - 1, 1, last=True)
            step(A1_H, 0, drain=True)

        def after(H, b, lag):
            if b >= lag:
                return H, b - lag, 0
            return H - 1, b - lag + A1_U, 1

        def part_of(tile, j):
            return tile[:, j // NH2, (j % NH2) * NC:(j % NH2 + 1) * NC]

        def exists(H, b, lag, first, drain):
            return not ((first and b < lag) or (drain and b >= lag))

        def before(H, c, n):
            return isinstance(H, int) and A1_U * H + c < n

        def w_arrived(eng, H, par):
            if isinstance(H, int):
                assert H >= 2
                eng.wait_ge(w_in[par], 16 * (H // 2))
            else:
                eng.wait_ge(w_in[par], H * 8 - 8 * par)

        def wo_arrived(eng, H, par):
            if not isinstance(H, int):
                eng.wait_ge(wo_in[par], H * 8 + 8 * par)
            elif H >= 1:
                eng.wait_ge(wo_in[par], 16 * (H // 2) + 16 * par)

        CHUNKS = {1: {0: (0, 1), 1: (2, 3), 2: (4,), 3: (5,)},
                  0: {0: (0, 1), 1: (2, 3), 2: (6,), 3: (7,)}}

        def chunks(par, b, last, drain):
            return () if last or drain else CHUNKS[par][b]

        def filled(X, c):
            return X * 6 + (c + 1 if c < 6 else c - 1)

        block = ctx.enter_context(nc.Block())

        @block.sync
        def _(sp):
            sp.dma_start(wo[1][:, :], src["a1_wo"][1]).then_inc(wo_in[1], 16)
            with sp.Fori(0, (A1_H - 2) // 2) as i:
                sp.wait_ge(wv_split, i * 2 + 2)
                sp.dma_start(wv[:, :], src["a1_wv"][bass.ds(i + 1, 1)].rearrange("g p n -> p (g n)")).then_inc(wv_in, 16)
                for s in range(2):
                    h = i * 2 + (2 + s)
                    sp.wait_ge(chunk, (h - 1) * 4)
                    sp.dma_start(w[s][:, :], src["a1_w"][bass.ds(h, 1)].rearrange("g p n -> p (g n)"))\
                        .then_inc(w_in[s], 16)
                    sp.wait_ge(added, (h - 1) * A1_U)
                    sp.dma_start(wo[s][:, :], src["a1_wo"][bass.ds(h, 1)].rearrange("g p n -> p (g n)"))\
                        .then_inc(wo_in[s], 16)

        @block.gpsimd
        def _(pool):
            nc.gpsimd.memset(v[:, :, :, P:P + 1], 1.0).then_inc(ones_set, 1)
            set_exponent(nc, k, rstd_ready)
            for turn in range(2):
                inverse_root(nc, pool, k, ln, rstd_ready, turn)

            def low(counter, n, whole, part, done, by=1):
                pool.wait_ge(counter, n)
                nc.gpsimd.tensor_tensor(part[1][:, :], whole, part[0][:, :], ALU.subtract).then_inc(done, by)

            def w_low(X, par):
                low(w_high, X + 1, w[par][:, 0:2 * KD * P], ws[par], w_split)

            def project(X, par):
                for c in range(4):
                    pool.wait_ge(roped, X * 4 + (c + 1))
                    dst, half = (qT, kT)[c // 2][par], c % 2
                    nc.gpsimd.tensor_tensor(dst[:, half * NC:(half + 1) * NC],
                                            t1[c % 2][:, :, :].rearrange("p b s -> p (b s)"),
                                            t2[c % 2][:, :, :].rearrange("p b s -> p (b s)"),
                                            ALU.add).then_inc(chunk, 1)

            def step(H, par, first=False, last=False, drain=False):
                if drain:
                    return
                if not last:
                    w_low(H + 1, 1 - par)
                    if par == 1:
                        low(wv_high, H + 3, wv[:, :], wvs, wv_split, 2)
                low(wo_high, H + 1, wo[par][:, 0:D], wos[par], wo_split)
                if not last:
                    project(H + 1, 1 - par)

            w_low(0, 0)
            low(wv_high, 2, wv[:, :], wvs, wv_split, 2)
            project(0, 0)
            heads(pool, step)

        @block.scalar
        def _(act):
            def w_to_high(X, par):
                if isinstance(X, int) and X < 2:
                    k.wait(act, "a1")
                else:
                    w_arrived(act, X, par)
                    act.wait_ge(proj, (X - 2) * 6 + 4)
                high_of(nc, ws[par][0][:, :], w[par][:, 0:2 * KD * P]).then_inc(w_high, 1)

            def wo_to_high(H, par):
                wo_arrived(act, H, par)
                if not (isinstance(H, int) and H < 2):
                    act.wait_ge(projected, (H - 1) * A1_U)
                high_of(nc, wos[par][0][:, :], wo[par][:, 0:D]).then_inc(wo_high, 1)

            w_to_high(0, 0)
            high_of(nc, wvs[0][:, :], wv[:, :]).then_inc(wv_high, 2)
            for j in (0, 2, 1, 3):
                act.wait_ge(turned, (j % NH2) + 1)
                high_of(nc, part_of(k.xs[0], j), turn_banks[j][:, :]).then_inc(x_high, 1)

            def values(X, c):
                act.wait_ge(proj, filled(X, c))
                n = c - 4
                if not (isinstance(X, int) and X < 2):
                    act.wait_ge(weighed, (X * A1_U + (n - 3)) if c < 6 else (X * A1_U + (n - 7)))
                nc.scalar.copy(v[:, :, 2 * n:2 * n + 2, 0:P],
                               pp[c % 2][:, :].rearrange("p (t h n) -> p h t n", t=2, h=2)).then_inc(v_ready, 1)

            def swap(X, par, c):
                n, kind = c % 2, c // 2
                act.wait_ge(proj, filled(X, c))
                if not before(X, c, 2):
                    act.wait_ge(chunk, X * 4 + (c - 1))
                bias = w[par][:, A1_W - 2 + kind:A1_W - 1 + kind]
                lo, hi = slice(0, 64), slice(64, 128)
                for a, b in ((lo, hi), (hi, lo)):
                    out = nc.scalar.activation(t2[n][a, :, :].rearrange("p b s -> p (b s)"), pp[n][b, :], ACT.Identity,
                                               bias=bias[b])
                out.then_inc(swapped, 1)

            def step(H, par, first=False, last=False, drain=False):
                if not drain:
                    if not last:
                        w_to_high(H + 1, 1 - par)
                        if par == 1:
                            act.wait_ge(wv_in, H * 8 + 8)
                            act.wait_ge(proj, H * 6 + 6)
                            high_of(nc, wvs[0][:, :], wv[:, :]).then_inc(wv_high, 2)
                    wo_to_high(H, par)
                for b in range(A1_U if not drain else 2):
                    cc = chunks(par, b, last, drain)
                    if exists(H, b, 1, first, drain):
                        h, u, _ = after(H, b, 1)
                        act.wait_ge(turnedP, h * A1_U + (u + 1))
                        nc.scalar.copy(PT[u % 2][:, :, :].rearrange("p c q -> p (c q)"), pT[:, 0:3 * P])\
                            .then_inc(PT_ready, 1)
                    if not drain:
                        act.wait_ge(maxed, H * A1_U + (b + 1))
                        nc.scalar.activation(Pm[b % 2][:, 0:P], nS[b % 2][:, 0:P], ACT.Exp,
                                             bias=nm[b % 2][:, 0:1], scale=-1.0)
                        nc.scalar.activation(Pm[b % 2][:, P:3 * P], nS[b % 2][:, P:3 * P], ACT.Exp,
                                             bias=nm[b % 2][:, 1:2], scale=-1.0).then_inc(probs, 1)
                    if len(cc) > 0:
                        (values(H + 1, cc[0]) if cc[0] >= 4 else swap(H + 1, 1 - par, cc[0]))
                    if exists(H, b, 2, first, drain):
                        h, u, _ = after(H, b, 2)
                        act.wait_ge(turnedO, h * A1_U + (u + 1))
                        high_of(nc, OT[u % 2][0][:, :], pOT[:, 0:2 * P]).then_inc(OT_high, 1)
                    if len(cc) > 1:
                        (values(H + 1, cc[1]) if cc[1] >= 4 else swap(H + 1, 1 - par, cc[1]))

            for c in range(6):
                if c < 4:
                    swap(0, 0, c)
                else:
                    values(0, c)
            heads(act, step)

        @block.vector
        def _(dve):
            for half in range(2):
                row_stats(nc, dve, k, k.x, ln, 0, half)
            k.wait(dve, "a1")
            for half in range(2):
                row_scale(nc, dve, k, k.x, hn, rstd_ready, 0, half, h_ready)
                dve.wait_ge(h_ready, (half + 1) * HALF)
                row_stats(nc, dve, k, hn, ln, 1, half)
            for half in range(2):
                row_scale_by(nc, dve, k, hn, lambda t: rows[:, 0, :], lambda t: rows[:, 1, :], k.xn, k.xn,
                             ln, rstd_ready, 1, half, based, half * HALF, xn_ready)
            for i, j in enumerate((0, 2, 1, 3)):
                dve.wait_ge(x_high, i + 1)
                low_of(nc, part_of(k.xs[1], j), turn_banks[j][:, :], part_of(k.xs[0], j)).then_inc(xT_ready, 1)

            def base_tile(t):
                nc.vector.tensor_tensor(k.x[:, t, :], k.x[:, t, :], rows[:, 2, :], ALU.add).then_inc(based, 1)
                dve.wait_ge(based, NT + 2 * t + 1)
                nc.vector.tensor_tensor(k.x[:, t, :], k.x[:, t, :], hn[:, t, :], ALU.add).then_inc(based, 1)

            def rope(X, par, c):
                n, kind = c % 2, c // 2
                bias = w[par][:, A1_W - 2 + kind:A1_W - 1 + kind]
                dve.wait_ge(swapped, X * 4 + (c + 1))
                table = lambda i: cs[:, 2 * kind + i:2 * kind + i + 1, :].to_broadcast([P, 2, S])
                nc.vector.scalar_tensor_tensor(out=t1[n][:, :, :], in0=pp[n][:, :].rearrange("p (b s) -> p b s", b=2),
                                               scalar=bias, in1=table(0), op0=ALU.add, op1=ALU.mult)
                nc.vector.tensor_tensor(t2[n][:, :, :], t2[n][:, :, :], table(1), ALU.mult).then_inc(roped, 1)

            def maxima(H, b):
                dve.wait_ge(scored, H * A1_U + (b + 1))
                if not before(H, b, 2):
                    dve.wait_ge(probs, H * A1_U + (b - 1))
                dve.sem_inc(gate, 1)
                nc.vector.tensor_tensor_reduce(nS[b % 2][:, 0:P], pS[b % 2][:, 0:P], cmask[:, 0:P], -1.0, 3.0e38,
                                               ALU.add, ALU.min, nm[b % 2][:, 0:1])
                nc.vector.tensor_tensor_reduce(nS[b % 2][:, P:3 * P], pS[b % 2][:, P:3 * P], cmask[:, P:3 * P], -1.0,
                                               3.0e38, ALU.add, ALU.min, nm[b % 2][:, 1:2]).then_inc(maxed, 1)

            def normalise(H, u, par):
                dve.wait_ge(weighed, H * A1_U + (u + 1))
                o = pO[:, 0:2 * (P + 1)].rearrange("p (c n) -> p c n", c=2)
                nc.vector.reciprocal(rec[:, :], o[:, :, P]).then_inc(rec_ready, 1)
                if u == 0:
                    wo_arrived(dve, H, par)
                dve.wait_ge(rec_ready, H * A1_U + (u + 1))
                if not before(H, u, 2):
                    dve.wait_ge(turnedO, H * A1_U + (u - 1))
                for c in range(2):
                    out = nc.vector.scalar_tensor_tensor(out=O[u % 2][:, c, :], in0=o[:, c, 0:P],
                                                         scalar=rec[:, c:c + 1], in1=wo[par][:, D:D + P],
                                                         op0=ALU.mult, op1=ALU.add)
                out.then_inc(O_ready, 1)

            def add_y(H, u):
                dve.wait_ge(projected, H * A1_U + (u + 1))
                if not before(H, u, A1_U):
                    dve.wait_ge(added, H * A1_U + u)
                nc.vector.tensor_tensor(k.x[:, 2 * u:2 * u + 2, :], pY[:, :].rearrange("p (c n) -> p c n", c=2),
                                        k.x[:, 2 * u:2 * u + 2, :], ALU.add).then_inc(added, 1)

            def low_OT(H, u):
                dve.wait_ge(OT_high, H * A1_U + (u + 1))
                low_of(nc, OT[u % 2][1][:, :], pOT[:, 0:2 * P], OT[u % 2][0][:, :]).then_inc(OT_ready, 1)

            def step(H, par, first=False, last=False, drain=False):
                ready = []
                for b in range(A1_U if not drain else 3):
                    cc = [c for c in chunks(par, b, last, drain) if c < 4]
                    if not drain:
                        maxima(H, b)
                    for c in ready:
                        rope(H + 1, 1 - par, c)
                    if exists(H, b, 3, first, drain):
                        h, u, _ = after(H, b, 3)
                        add_y(h, u)
                    if exists(H, b, 1, first, drain):
                        h, u, x = after(H, b, 1)
                        normalise(h, u, par ^ x)
                    if exists(H, b, 2, first, drain):
                        h, u, _ = after(H, b, 2)
                        low_OT(h, u)
                    for c in cc[:1]:
                        rope(H + 1, 1 - par, c)
                    ready = cc[1:]

            for c in range(4):
                rope(0, 0, c)
                base_tile(2 * c)
                base_tile(2 * c + 1)
            dve.wait_ge(based, 3 * NT)
            heads(dve, step)
            dve.wait_ge(added, A1_H * A1_U)

        @block.tensor
        def _(pe):
            k.wait(pe, "a1")
            turn_rows(nc, pe, k, turn_banks, xn_ready, 0, turned)

            def chunk_of(X, par, c):
                if c < 2:
                    if not before(X, c, 2):
                        pe.wait_ge(v_ready, X * 2 + (c - 1))
                else:
                    pe.wait_ge(roped, X * 4 + (c - 1 if c < 6 else c - 3))
                if c == 0:
                    pe.wait_ge(w_split, X + 1)
                if c == 4:
                    pe.wait_ge(wv_split, X + 2)
                if c < 4:
                    for d in range(KD):
                        off = ((c // 2) * KD + d) * P
                        out = split_product(nc, pp[c % 2][:, :], [g[:, off:off + P] for g in ws[par]],
                                            [x[:, d, (c % 2) * NC:(c % 2 + 1) * NC] for x in k.xs],
                                            start=(d == 0), stop=(d == KD - 1))
                else:
                    for t in range(2):
                        for d in range(KD):
                            tt = 2 * (c - 4) + t
                            out = split_product(nc, pp[c % 2][:, t * 2 * P:(t + 1) * 2 * P],
                                                [x[:, d, tt * P:(tt + 1) * P] for x in k.xs],
                                                [g[:, d * 2 * P:(d + 1) * 2 * P] for g in wvs],
                                                start=(d == 0), stop=(d == KD - 1))
                out.then_inc(proj, 1)

            def scores(H, par, b):
                if b == 0:
                    pe.wait_ge(chunk, (H + 1) * 4)
                if not before(H, b, 2):
                    pe.wait_ge(maxed, H * A1_U + (b - 1))
                c = b * S
                nc.tensor.matmul(pS[b % 2][:, 0:P], qT[par][:, c:c + P], kT[par][:, c:c + P], start=True, stop=True)
                nc.tensor.matmul(pS[b % 2][:, P:3 * P], qT[par][:, c + P:c + S], kT[par][:, c:c + S],
                                 start=True, stop=True).then_inc(scored, 1)

            def turn_P(H, u):
                pe.wait_ge(probs, H * A1_U + (u + 1))
                if not before(H, u, 1):
                    pe.wait_ge(PT_ready, H * A1_U + u)
                for c in range(3):
                    out = nc.tensor.transpose(pT[:, c * P:(c + 1) * P], Pm[u % 2][:, c * P:(c + 1) * P], k.tile["ident"][:, :])
                out.then_inc(turnedP, 1)

            def weigh(H, par, u):
                pe.wait_ge(PT_ready, H * A1_U + (u + 1))
                pe.wait_ge(v_ready, H * 2 + (u + 1 - 2 * par))
                if isinstance(H, int) and H == 0 and u == 0:
                    pe.wait_ge(ones_set, 1)
                if not before(H, u, 1):
                    pe.wait_ge(O_ready, H * A1_U + u)
                nc.tensor.matmul(pO[:, 0:P + 1], PT[u % 2][:, 0, :], v[:, par, 2 * u, :], start=True, stop=True)
                for c in range(2):
                    out = nc.tensor.matmul(pO[:, P + 1:2 * (P + 1)], PT[u % 2][:, 1 + c, :], v[:, par, 2 * u + c, :],
                                           start=(c == 0), stop=(c == 1))
                out.then_inc(weighed, 1)

            def turn_O(H, u):
                pe.wait_ge(O_ready, H * A1_U + (u + 1))
                if not before(H, u, 1):
                    pe.wait_ge(OT_ready, H * A1_U + u)
                for c in range(2):
                    out = nc.tensor.transpose(pOT[:, c * P:(c + 1) * P], O[u % 2][:, c, :], k.tile["ident"][:, :])
                out.then_inc(turnedO, 1)

            def project_out(H, par, u):
                pe.wait_ge(OT_ready, H * A1_U + (u + 1))
                if u == 0:
                    pe.wait_ge(wo_split, H + 1)
                if not before(H, u, 1):
                    pe.wait_ge(added, H * A1_U + u)
                for c in range(2):
                    out = split_product(nc, pY[:, c * D:(c + 1) * D], [g[:, c * P:(c + 1) * P] for g in OT[u % 2]],
                                        [g[:, :] for g in wos[par]], start=True, stop=True)
                out.then_inc(projected, 1)

            def step(H, par, first=False, last=False, drain=False):
                for b in range(A1_U if not drain else 3):
                    cc = chunks(par, b, last, drain)
                    if not drain:
                        scores(H, par, b)
                    if exists(H, b, 1, first, drain):
                        h, u, _ = after(H, b, 1)
                        turn_P(h, u)
                    if exists(H, b, 3, first, drain):
                        h, u, x = after(H, b, 3)
                        project_out(h, par ^ x, u)
                    if len(cc):
                        chunk_of(H + 1, 1 - par, cc[0])
                    if exists(H, b, 1, first, drain):
                        h, u, x = after(H, b, 1)
                        weigh(h, par ^ x, u)
                    if exists(H, b, 2, first, drain):
                        h, u, _ = after(H, b, 2)
                        turn_O(h, u)
                    if len(cc) > 1:
                        chunk_of(H + 1, 1 - par, cc[1])

            for c in range(6):
                if c < 2:
                    pe.wait_ge(xT_ready, 2 * c + 2)
                chunk_of(0, 0, c)
            heads(pe, step)


X1_H = 2
X1_EPS = 1e-3


def retention_1(nc, k, src):
    with ExitStack() as ctx:
        sb = lambda name, shape, dt=F32: k.sb(ctx, "x1_" + name, shape, dt)
        wh, wg, wo, cT = k.tile["x1_wh"], k.tile["x1_wg"], k.tile["x1_wo"], k.tile["ctxT"]
        decay = k.tile["x1_decay"]
        rows = k.tile["x1_rows"]
        QT = sb("QT", [P, X1_H, T])
        KT = sb("KT", [P, X1_H, T])
        V = sb("V", [P, 2, X1_H, B, P])
        W = sb("W", [P, NT, D])
        Wg, Wb = sb("Wg", [P, NT, D]), sb("Wb", [P, NT, D])
        A = sb("A", [P, X1_H, 4 * P])
        raw = sb("raw", [P, X1_H, 3 * P])
        O = sb("O", [P, NT, D])
        ba = [k.ps(ctx, f"x1_ba{i}") for i in range(4)]
        bb = [k.ps(ctx, f"x1_bb{i}") for i in range(4)]

        sem = lambda name: k.sem("x1_" + name)
        on_vector, on_gpsimd, on_tensor, on_scalar, (ln, rstd_ready, _, _) = \
            norm_and_turn(nc, k, ctx, "x1", bb)
        filled, moved, ones_set = sem("filled"), sem("moved"), sem("ones_set")
        scored, raw_ready, A_ready, weighed, O_ready = (sem("scored"), sem("raw_ready"), sem("A_ready"),
                                                        sem("weighed"), sem("O_ready"))
        normed, shaped, mixed, turned, mT_ready = (sem("normed"), sem("shaped"), sem("mixed"), sem("turnedM"),
                                                   sem("mT_ready"))
        projected, added = sem("projected"), sem("added")
        block = ctx.enter_context(nc.Block())

        @block.gpsimd
        def _(pool):
            nc.gpsimd.memset(A[:, :, 3 * P:4 * P], 1.0).then_inc(ones_set, 1)
            on_gpsimd(pool)
            inverse_root(nc, pool, k, ln, rstd_ready, 1, X1_EPS)

        @block.scalar
        def _(act):
            def move(j, out, func=ACT.Copy):
                act.wait_ge(filled, j + 1)
                bank = ba[j % 4][:, :]
                if len(out.shape) == 3:
                    bank = bank.rearrange("p (t n) -> p t n", t=out.shape[1])
                nc.scalar.activation(out, bank, func).then_inc(moved, 1)

            for h in range(X1_H):
                for half in range(NH2):
                    move(2 * h + half, KT[:, h, half * NC:(half + 1) * NC])
            for h in range(X1_H):
                for kt in range(2):
                    move(4 + 2 * h + kt, V[:, kt, h, :, :])
            on_scalar(act)
            for h in range(X1_H):
                for half in range(NH2):
                    move(8 + 2 * h + half, QT[:, h, half * NC:(half + 1) * NC])
            for g in range(4):
                move(12 + g, W[:, 2 * g:2 * g + 2, :], ACT.Relu)
            for h in range(X1_H):
                for st in range(2):
                    act.wait_ge(weighed, 2 * h + st + 1)
                    nc.scalar.copy(O[:, st:NT:2, h * P:(h + 1) * P],
                                   ba[2 * h + st][:, :].rearrange("p (b n) -> p b n", b=B)).then_inc(O_ready, 1)
            for j in (0, 2, 1, 3):
                act.wait_ge(turned, (j % NH2) + 1)
                nc.scalar.copy(k.xT[:, j // NH2, (j % NH2) * NC:(j % NH2 + 1) * NC], bb[j][:, :]).then_inc(mT_ready, 1)

        @block.vector
        def _(dve):
            on_vector(dve)
            k.wait(dve, "x1")
            for h in range(X1_H):
                dve.wait_ge(scored, h + 1)
                nc.vector.tensor_tensor(raw[:, h, :], bb[h][:, 0:3 * P], decay[:, h, :], ALU.mult).then_inc(raw_ready, 1)
                dve.wait_ge(raw_ready, 2 * h + 1)
                nc.vector.scalar_tensor_tensor(out=A[:, h, 0:3 * P], in0=raw[:, h, :], scalar=-1.0, in1=raw[:, h, :],
                                               op0=ALU.mult, op1=ALU.max).then_inc(raw_ready, 1)
                dve.wait_ge(raw_ready, 2 * h + 2)
                nc.vector.tensor_scalar(A[:, h, 0:3 * P], A[:, h, 0:3 * P], 1.0, None, ALU.max).then_inc(A_ready, 1)
            dve.wait_ge(moved, 16)
            for t in range(NT):
                nc.vector.tensor_tensor(Wg[:, t, :], W[:, t, :], rows[:, 0, :], ALU.mult).then_inc(shaped, 1)
                nc.vector.tensor_tensor(Wb[:, t, :], W[:, t, :], rows[:, 1, :], ALU.mult).then_inc(shaped, 1)
            dve.wait_ge(shaped, 2 * NT)
            dve.wait_ge(O_ready, 4)
            for half in range(2):
                row_stats(nc, dve, k, O, ln, 1, half)
            for half in range(2):
                row_scale_by(nc, dve, k, O, lambda t: Wg[:, t, :], lambda t: Wb[:, t, :], k.xn, k.xn,
                             ln, rstd_ready, 1, half, normed, half * HALF, mixed)
            for g in range(4):
                dve.wait_ge(projected, g + 1)
                nc.vector.tensor_tensor(k.x[:, 2 * g:2 * g + 2, :], ba[g][:, :].rearrange("p (t n) -> p t n", t=2),
                                        k.x[:, 2 * g:2 * g + 2, :], ALU.add).then_inc(added, 1)
            dve.wait_ge(added, 4)

        @block.tensor
        def _(pe):
            k.wait(pe, "x1")
            k.wait(pe, "ctx")

            def free(j):
                if j >= 4:
                    pe.wait_ge(moved, j - 3)

            for h in range(X1_H):
                for half in range(NH2):
                    j = 2 * h + half
                    free(j)
                    nc.tensor.matmul(ba[j % 4][:, :], wh[:, h, :], cT[:, h, half * NC:(half + 1) * NC],
                                     start=True, stop=True).then_inc(filled, 1)
            for h in range(X1_H):
                for kt in range(2):
                    j = 4 + 2 * h + kt
                    free(j)
                    for b in range(B):
                        out = nc.tensor.matmul(ba[j % 4][:, b * P:(b + 1) * P], cT[:, h, (2 * b + kt) * P:(2 * b + kt + 1) * P],
                                               wh[:, h, :], start=True, stop=True)
                    out.then_inc(filled, 1)
            on_tensor(pe)
            for h in range(X1_H):
                for half in range(NH2):
                    j = 8 + 2 * h + half
                    free(j)
                    nc.tensor.matmul(ba[j % 4][:, :], wh[:, h, :], k.xT[:, h, half * NC:(half + 1) * NC],
                                     start=True, stop=True).then_inc(filled, 1)
            for g in range(4):
                free(12 + g)
                for t in range(2):
                    for d in range(KD):
                        tt = 2 * g + t
                        out = nc.tensor.matmul(ba[g][:, t * D:(t + 1) * D], k.xT[:, d, tt * P:(tt + 1) * P], wg[:, d, :],
                                               start=(d == 0), stop=(d == KD - 1))
                out.then_inc(filled, 1)
            pe.wait_ge(moved, 12)
            for h in range(X1_H):
                for b in range(B):
                    nc.tensor.matmul(bb[h][:, 0:2 * P], KT[:, h, b * S:b * S + P], QT[:, h, b * S:(b + 1) * S],
                                     start=(b == 0), stop=(b == B - 1))
                for b in range(B):
                    out = nc.tensor.matmul(bb[h][:, 2 * P:3 * P], KT[:, h, b * S + P:(b + 1) * S],
                                           QT[:, h, b * S + P:(b + 1) * S], start=(b == 0), stop=(b == B - 1))
                out.then_inc(scored, 1)
            pe.wait_ge(moved, 16)
            pe.wait_ge(ones_set, 1)
            for h in range(X1_H):
                pe.wait_ge(A_ready, h + 1)
                for st in range(2):
                    for kt in range(2):
                        block_at = st if kt == 0 else (3 if st == 0 else 2)
                        out = nc.tensor.matmul(ba[2 * h + st][:, :], A[:, h, block_at * P:(block_at + 1) * P],
                                               V[:, kt, h, :, :].rearrange("p b n -> p (b n)"),
                                               start=(kt == 0), stop=(kt == 1))
                    out.then_inc(weighed, 1)
            pe.wait_ge(A_ready, 2)
            turn_rows(nc, pe, k, bb, mixed, 0, turned)
            pe.wait_ge(mT_ready, 4)
            pe.wait_ge(O_ready, 4)
            for g in range(4):
                for t in range(2):
                    for d in range(KD):
                        tt = 2 * g + t
                        out = nc.tensor.matmul(ba[g][:, t * D:(t + 1) * D], k.xT[:, d, tt * P:(tt + 1) * P], wo[:, d, :],
                                               start=(d == 0), stop=(d == KD - 1))
                out.then_inc(projected, 1)


F1_GT, F1_ET = 1024 // P, 512 // P
F1_KEYS, F1_TOP, F1_E, F1_R = 64, 8, 512, 64


def memory_1(nc, k, src):
    with ExitStack() as ctx:
        sb = lambda name, shape, dt=F32: k.sb(ctx, "f1_" + name, shape, dt)
        wq, keys, iota = k.tile["f1_wq"], k.tile["f1_keys"], k.tile["f1_iota"]
        QI = sb("QI", [F1_R, T, 2])
        R = sb("R", [P, 2, NT, F1_KEYS])
        top = sb("top", [P, 2, NT, F1_TOP])
        at = sb("at", [P, 2, NT, F1_TOP], U32)
        atf = sb("atf", [P, 2, NT, F1_TOP])
        rank = sb("rank", [P, NT, F1_TOP, F1_TOP])
        best = sb("best", [P, NT, F1_TOP])
        place = sb("place", [P, NT, F1_TOP], U32)
        row_col = sb("row_col", [P, 2, NT, F1_TOP], U32)
        row_colf = sb("row_colf", [P, 2, NT, F1_TOP])
        sel = sb("sel", [P, 2, NT, F1_TOP, F1_TOP])
        key = sb("key", [P, 2, NT, F1_TOP])
        expert = sb("expert", [P, NT, F1_TOP])
        nexpert = sb("nexpert", [P, NT, F1_TOP])
        ex = sb("ex", [P, NT, F1_TOP])
        nex = sb("nex", [P, NT, F1_TOP])
        tot = sb("tot", [P, NT, 2])
        PW = sb("PW", [P, NT, F1_E])
        hotv = [sb(f"hotv{i}", [P, F1_E]) for i in range(3)]
        hotp = [sb(f"hotp{i}", [P, F1_E]) for i in range(2)]
        far = sb("far", [P, F1_E])
        hota = [sb(f"hota{i}", [P, F1_E]) for i in range(3)]
        zeros = sb("zeros", [P, NC], BF16)
        w = [k.tile[f"f1_w{i}"] for i in range(3)]
        sg = [sb(f"sg{i}", [P, NC]) for i in range(2)]
        parts = lambda name, shape: [sb(f"{name}_{part}", shape, F32R) for part in ("high", "low")]
        ws = [parts(f"w{i}", [P, WT]) for i in range(2)]
        wqs = parts("wq", [P, KD * P])
        hT = [sb(f"hT{h}", [P, NC]) for h in range(2)]
        hs = [parts(f"h{i}", [P, T]) for i in range(2)]
        pg = [k.ps(ctx, f"f1_pg{i}") for i in range(2)]
        pu = [k.ps(ctx, f"f1_pu{i}") for i in range(2)]
        acc = [k.ps(ctx, f"f1_acc{i}") for i in range(4)]

        sem = lambda name: k.sem("f1_" + name)
        on_vector, on_gpsimd, on_tensor, on_scalar, lows_on_vector, x_split = \
            norm_and_turn(nc, k, ctx, "f1", [pg[0], pg[1], pu[0], pu[1]], split=True, whole=False)
        zero_set = sem("zero_set")
        w_in = [sem(f"w_in{i}") for i in range(3)]
        queried, QI_ready, routed, R_ready = sem("queried"), sem("QI_ready"), sem("routed"), sem("R_ready")
        step_done, best_ready, ex_ready, mix_ready = sem("step_done"), sem("best_ready"), sem("ex_ready"), sem("mix_ready")
        built, pool_step, pool_built = sem("built"), sem("pool_step"), sem("pool_built")
        wq_high, wq_split, w_high, w_split, h_high, h_split = (sem("wq_high"), sem("wq_split"), sem("w_high"),
                                                               sem("w_split"), sem("h_high"), sem("h_split"))
        dn_high, dn_split = sem("dn_high"), sem("dn_split")
        far_ready, hot_ready, hot_used = sem("far_ready"), sem("hot_ready"), sem("hot_used")
        gated, silu_done, h_ready, down_done, added = (sem("gated"), sem("silu_done"), sem("h_ready"),
                                                       sem("down_done"), sem("added"))
        TILES = F1_GT + F1_ET
        EXP_AT, ACT_SHARE = 1, 3
        CUTS, SHARES = (0, 2, 4, 6), 6
        DVE_TILES, POOL_TILES, ACT_TILES = (0, 1, 2, 3, 4), (7,), (5, 6)

        def columns(n):
            return slice(0, 2 * D) if n < F1_GT else slice(0, D)

        DOWN = slice(2 * D, 3 * D)

        block = ctx.enter_context(nc.Block())

        @block.sync
        def _(sp):
            for n in range(3, TILES):
                sp.wait_ge(dn_split, n - 2)
                sp.dma_start(w[n % 3][:, :], src["f1_w"][n]).then_inc(w_in[n % 3], 16)

        @block.gpsimd
        def _(pool):
            nc.gpsimd.memset(zeros[:, :], 0.0).then_inc(zero_set, 1)
            on_gpsimd(pool)
            k.wait(pool, "f1")
            pool.wait_ge(mix_ready, 1)
            def sum_of_scalars(i):
                j, c = ACT_TILES[i // F1_TOP], i % F1_TOP
                pool.wait_ge(hot_ready, i + 1)
                if c == 0:
                    nc.gpsimd.tensor_copy(PW[:, j, :], hota[i % 3][:, :]).then_inc(hot_used, 1)
                else:
                    pool.wait_ge(hot_used, i)
                    nc.gpsimd.tensor_tensor(PW[:, j, :], PW[:, j, :], hota[i % 3][:, :], ALU.add).then_inc(hot_used, 1)

            n = 0
            of_scalar = 0
            for j in POOL_TILES:
                for c in range(F1_TOP):
                    out = PW[:, j, :] if c == 0 else hotp[c % 2][:, :]
                    nc.gpsimd.tensor_scalar(out, iota[:, :], expert[:, j, c:c + 1], ex[:, j, c:c + 1],
                                            ALU.is_equal, ALU.mult).then_inc(pool_step, 1)
                    n += 1
                    if c:
                        pool.wait_ge(pool_step, n)
                        nc.gpsimd.tensor_tensor(PW[:, j, :], PW[:, j, :], hotp[c % 2][:, :], ALU.add)\
                            .then_inc(pool_step, 1)
                        n += 1
                        pool.wait_ge(pool_step, n)
                    for _ in range(len(ACT_TILES)):
                        sum_of_scalars(of_scalar)
                        of_scalar += 1
            pool.sem_inc(pool_built, 1)

        @block.scalar
        def _(act):
            def w_to_high(n):
                if n >= 3:
                    act.wait_ge(w_in[n % 3], 16 * (n // 3))
                if n >= 2:
                    act.wait_ge(gated, 2 * n - 2)
                high_of(nc, ws[n % 2][0][:, columns(n)], w[n % 3][:, columns(n)]).then_inc(w_high, 1)

            def down_to_high(n):
                if n >= 2:
                    act.wait_ge(down_done, n - 1)
                high_of(nc, ws[n % 2][0][:, DOWN], w[n % 3][:, DOWN]).then_inc(dn_high, 1)

            def spread_on_scalar(i):
                j, c = ACT_TILES[i // F1_TOP], i % F1_TOP
                if i:
                    act.wait_ge(hot_ready, i)
                nc.scalar.activation(far[:, :], iota[:, :], ACT.Abs, bias=nexpert[:, j, c:c + 1])\
                    .then_inc(far_ready, 1)
                act.wait_ge(far_ready, i + 1)
                if i >= 3:
                    act.wait_ge(hot_used, i - 2)
                nc.scalar.activation(hota[i % 3][:, :], far[:, :], ACT.Relu, bias=ex[:, j, c:c + 1],
                                     scale=nex[:, j, c:c + 1]).then_inc(hot_ready, 1)

            k.wait(act, "f1")
            high_of(nc, wqs[0][:, :], wq[:, :, :].rearrange("p d n -> p (d n)")).then_inc(wq_high, 1)
            w_to_high(0)
            on_scalar(act)
            for s in range(2):
                for half in range(NH2):
                    act.wait_ge(queried, 2 * s + half + 1)
                    nc.scalar.copy(QI[:, half * NC:(half + 1) * NC, s], acc[2 * s + half][0:F1_R, :]).then_inc(QI_ready, 1)
            spread = 0
            for n in range(TILES):
                if n == EXP_AT:
                    act.wait_ge(best_ready, 1)
                    nc.scalar.activation(ex[:, :, :], ex[:, :, :], ACT.Exp).then_inc(ex_ready, 1)
                if n + 1 < TILES:
                    w_to_high(n + 1)
                for h in range(2):
                    i = 2 * n + h
                    act.wait_ge(gated, i + 1)
                    if i >= 2:
                        act.wait_ge(h_ready, i - 1)
                    nc.scalar.activation(sg[h][:, :], pg[h][:, :], ACT.Silu).then_inc(silu_done, 1)
                down_to_high(n)
                for h in range(2):
                    act.wait_ge(h_ready, 2 * n + h + 1)
                    high_of(nc, hs[n % 2][0][:, h * NC:(h + 1) * NC], hT[h][:, :]).then_inc(h_high, 1)
                if n > EXP_AT and n < F1_GT:
                    if spread == 0:
                        act.wait_ge(mix_ready, 1)
                    for _ in range(ACT_SHARE):
                        if spread < len(ACT_TILES) * F1_TOP:
                            spread_on_scalar(spread)
                            spread += 1

        @block.vector
        def _(dve):
            on_vector(dve)
            k.wait(dve, "f1")
            done = [0]

            def link(ins, wait=True):
                done[0] += 1
                ins.then_inc(step_done, 1)
                if wait:
                    dve.wait_ge(step_done, done[0])
                return done[0]

            def w_low(n):
                dve.wait_ge(w_high, n + 1)
                low_of(nc, ws[n % 2][1][:, columns(n)], w[n % 3][:, columns(n)], ws[n % 2][0][:, columns(n)]).then_inc(w_split, 1)

            def tile_of(n, between=lambda part: None):
                if n + 1 < TILES:
                    w_low(n + 1)
                between(0)
                for h in range(2):
                    i = 2 * n + h
                    dve.wait_ge(silu_done, i + 1)
                    if n >= 1:
                        dve.wait_ge(h_split, i - 1)
                    nc.vector.tensor_tensor(hT[h][:, :], sg[h][:, :], pu[h][:, :], ALU.mult).then_inc(h_ready, 1)
                dve.wait_ge(dn_high, n + 1)
                low_of(nc, ws[n % 2][1][:, DOWN], w[n % 3][:, DOWN], ws[n % 2][0][:, DOWN]).then_inc(dn_split, 1)
                between(1)
                for h in range(2):
                    dve.wait_ge(h_high, 2 * n + h + 1)
                    half = slice(h * NC, (h + 1) * NC)
                    low_of(nc, hs[n % 2][1][:, half], hT[h][:, :], hs[n % 2][0][:, half]).then_inc(h_split, 1)
                between(2)

            def top_keys(j):
                for a in range(2):
                    out = nc.vector.max(top[:, a, j, :], R[:, a, j, :])
                link(out)
                for a in range(2):
                    out = nc.vector.max_index(at[:, a, j, :], top[:, a, j, :], R[:, a, j, :])
                out.then_inc(step_done, 1)
                done[0] += 1

            by_first = lambda x: x[:, :, :].rearrange("p t (a o) -> p t a o", o=1).to_broadcast([P, NT, F1_TOP, F1_TOP])
            by_second = lambda x: x[:, :, :].rearrange("p t (o b) -> p t o b", o=1).to_broadcast([P, NT, F1_TOP, F1_TOP])

            def best_sums():
                dve.wait_ge(step_done, done[0])
                nc.vector.tensor_copy(atf[:, :, :, :], at[:, :, :, :])
                link(nc.vector.tensor_tensor(rank[:, :, :, :], by_first(top[:, 0, :, :]), by_second(top[:, 1, :, :]), ALU.add))
                flat = lambda j: rank[:, j, :, :].rearrange("p a b -> p (a b)")
                for j in range(NT):
                    out = nc.vector.max(best[:, j, :], flat(j))
                link(out)
                nc.vector.tensor_tensor(ex[:, :, :], best[:, :, :], best[:, :, 0:1].to_broadcast([P, NT, F1_TOP]),
                                        ALU.subtract).then_inc(best_ready, 1)
                for j in range(NT):
                    out = nc.vector.max_index(place[:, j, :], best[:, j, :], flat(j))
                link(out)

            def experts_of():
                nc.vector.tensor_scalar(row_col[:, 0, :, :], place[:, :, :], 3, None, ALU.logical_shift_right)
                link(nc.vector.tensor_scalar(row_col[:, 1, :, :], place[:, :, :], 7, None, ALU.bitwise_and))
                link(nc.vector.tensor_copy(row_colf[:, :, :, :], row_col[:, :, :, :]))
                step8 = iota[:, 0:F1_TOP].rearrange("p (o q n) -> p o q n", o=1, q=1).to_broadcast([P, NT, F1_TOP, F1_TOP])
                for a in range(2):
                    out = nc.vector.tensor_tensor(sel[:, a, :, :, :], by_first(row_colf[:, a, :, :]), step8, ALU.is_equal)
                link(out)
                for a in range(2):
                    out = nc.vector.tensor_tensor(sel[:, a, :, :, :], sel[:, a, :, :, :], by_second(atf[:, a, :, :]), ALU.mult)
                link(out)
                for a in range(2):
                    out = nc.vector.tensor_reduce(key[:, a, :, :], sel[:, a, :, :, :], AX.X, ALU.add)
                link(out)
                link(nc.vector.scalar_tensor_tensor(out=expert[:, :, :], in0=key[:, 0, :, :], scalar=float(F1_KEYS),
                                                    in1=key[:, 1, :, :], op0=ALU.mult, op1=ALU.add))
                link(nc.vector.tensor_scalar(expert[:, :, :], expert[:, :, :], float(F1_E - 1), None, ALU.min))
                link(nc.vector.tensor_scalar(nexpert[:, :, :], expert[:, :, :], -1.0, None, ALU.mult))

            def mix():
                dve.wait_ge(ex_ready, 1)
                link(nc.vector.tensor_reduce(tot[:, :, 0], ex[:, :, :], AX.X, ALU.add))
                link(nc.vector.reciprocal(tot[:, :, 1], tot[:, :, 0]))
                link(nc.vector.tensor_tensor(ex[:, :, :], ex[:, :, :], tot[:, :, 1:2].to_broadcast([P, NT, F1_TOP]),
                                             ALU.mult))
                nc.vector.tensor_scalar(nex[:, :, :], ex[:, :, :], -1.0, None, ALU.mult).then_inc(mix_ready, 1)
                dve.wait_ge(mix_ready, 1)

            summed = [0, 0]

            def spread_weight(i):
                j, c = DVE_TILES[i // F1_TOP], i % F1_TOP
                if summed[0]:
                    dve.wait_ge(step_done, summed[0])
                link(nc.vector.tensor_scalar(hotv[i % 3][:, :], iota[:, :], expert[:, j, c:c + 1], ex[:, j, c:c + 1],
                                             ALU.is_equal, ALU.mult), wait=False)

            def add_weight(i, after):
                j, c = DVE_TILES[i // F1_TOP], i % F1_TOP
                dve.wait_ge(step_done, after)
                if c:
                    out = nc.vector.tensor_tensor(PW[:, j, :], PW[:, j, :], hotv[i % 3][:, :], ALU.add)
                else:
                    out = nc.vector.tensor_copy(PW[:, j, :], hotv[i % 3][:, :])
                summed[:] = [summed[1], link(out, wait=False)]
                if c == F1_TOP - 1:
                    dve.wait_ge(step_done, done[0])
                    dve.sem_inc(built, 1)

            def spread_weights(first, last):
                dve.wait_ge(step_done, done[0])
                for i in range(first, last):
                    spread_weight(i)
                    if i > first:
                        add_weight(i - 1, done[0] - 1)
                if last > first:
                    add_weight(last - 1, done[0])

            dve.wait_ge(wq_high, 1)
            low_of(nc, wqs[1][:, :], wq[:, :, :].rearrange("p d n -> p (d n)"), wqs[0][:, :]).then_inc(wq_split, 1)
            lows_on_vector(dve)
            w_low(0)
            dve.wait_ge(routed, 1)
            for a in range(2):
                out = nc.vector.tensor_copy(R[:, a, :, :], acc[a][:, :].rearrange("p (t n) -> p t n", t=NT))
            out.then_inc(R_ready, 1)
            dve.wait_ge(R_ready, 1)
            for j in range(NT):
                top_keys(j)
                if j == NT // 2 - 1:
                    tile_of(0)
            best_sums()
            tile_of(1)
            experts_of()
            mix()
            WEIGHTS = len(DVE_TILES) * F1_TOP
            at_part = lambda i: min(WEIGHTS, i * WEIGHTS // (SHARES * (F1_GT - 2)))
            for n in range(2, TILES):
                base = (n - 2) * SHARES
                if n < F1_GT:
                    tile_of(n, lambda part: spread_weights(at_part(base + CUTS[part]), at_part(base + CUTS[part + 1])))
                else:
                    tile_of(n)
            dve.wait_ge(down_done, TILES)
            for a in range(4):
                nc.vector.tensor_tensor(k.x[:, 2 * a:2 * a + 2, :], acc[a][:, :].rearrange("p (t n) -> p t n", t=2),
                                        k.x[:, 2 * a:2 * a + 2, :], ALU.add).then_inc(added, 1)
            dve.wait_ge(added, 4)

        @block.tensor
        def _(pe):
            k.wait(pe, "f1")
            on_tensor(pe)
            pe.wait_ge(wq_split, 1)
            for s in range(2):
                for half in range(NH2):
                    pe.wait_ge(x_split, 2 * half + 2)
                    for d in range(KD):
                        out = split_product(nc, acc[2 * s + half][0:F1_R, :],
                                            [g[:, d * P + s * F1_R:d * P + (s + 1) * F1_R] for g in wqs],
                                            [x[:, d, half * NC:(half + 1) * NC] for x in k.xs],
                                            start=(d == 0), stop=(d == KD - 1))
                    out.then_inc(queried, 1)

            def gate_up(n):
                pe.wait_ge(w_split, n + 1)
                for h in range(2):
                    if n >= 1:
                        pe.wait_ge(h_ready, 2 * n + h - 1)
                    for bank, off in ((pg[h], 0), (pu[h], D)):
                        if off and n >= F1_GT:
                            continue
                        for d in range(KD):
                            out = split_product(nc, bank[:, :], [g[:, off + d * P:off + (d + 1) * P] for g in ws[n % 2]],
                                                [x[:, d, h * NC:(h + 1) * NC] for x in k.xs],
                                                start=(d == 0), stop=(d == KD - 1))
                    if n >= F1_GT:
                        if n == F1_GT and h == 0:
                            pe.wait_ge(built, len(DVE_TILES))
                            pe.wait_ge(hot_used, len(ACT_TILES) * F1_TOP)
                            pe.wait_ge(pool_built, 1)
                        e = n - F1_GT
                        for t in range(4):
                            out = nc.tensor.transpose(pu[h][:, t * P:(t + 1) * P],
                                                      PW[:, 4 * h + t, e * P:(e + 1) * P], k.tile["ident"][:, :])
                    out.then_inc(gated, 1)

            def down(n):
                for h in range(2):
                    if h == 0:
                        pe.wait_ge(dn_split, n + 1)
                    pe.wait_ge(h_split, 2 * n + h + 1)
                    for t in range(h * NT // 2, (h + 1) * NT // 2):
                        out = split_product(nc, acc[t // 2][:, (t % 2) * D:(t % 2 + 1) * D],
                                            [g[:, t * P:(t + 1) * P] for g in hs[n % 2]],
                                            [g[:, 2 * D:3 * D] for g in ws[n % 2]],
                                            start=False, stop=(n == TILES - 1), skip_group_check=True)
                out.then_inc(down_done, 1)

            pe.wait_ge(QI_ready, 4)
            for a in range(2):
                for j in range(NT):
                    rows_n = QI[:, a * NC + j * (P // 2):a * NC + (j + 1) * (P // 2), :].rearrange("r t s -> r (t s)")
                    out = nc.tensor.matmul(acc[a][:, j * F1_KEYS:(j + 1) * F1_KEYS], rows_n, keys[:, a, :],
                                           start=True, stop=True)
            out.then_inc(routed, 1)
            gate_up(0)
            pe.wait_ge(R_ready, 1)
            pe.wait_ge(zero_set, 1)
            for a in range(4):
                nc.tensor.matmul(acc[a][:, :], zeros[:, 0:P], zeros[:, :], start=True, stop=False, skip_group_check=True)
            for n in range(1, TILES):
                gate_up(n)
                down(n - 1)
            down(TILES - 1)


def program(nc, src, out):
    with ExitStack() as ctx:
        k = Kernel(nc, ctx)
        k.x_in = k.sem("x_in")
        first_layer = ctx.enter_context(ExitStack())
        k.place(first_layer, "a0", "x0", "m0", side="right")
        attention_0(nc, k, src)
        k.place(ctx, "a1", "x1", "f1")
        cross_attention_0(nc, k, src)
        experts_0(nc, k, src)
        first_layer.close()
        k.clear_semaphores()
        attention_1(nc, k, src)
        retention_1(nc, k, src)
        memory_1(nc, k, src)
        store_x(nc, k, out)




def layouts(a):
    f = np.float32
    out = {"x": a["x"].reshape(T, D)}
    out["ident"] = np.eye(P, dtype=f)
    half = A0_D // 2
    inv = 1.0 / 150000.0 ** (np.arange(half, dtype=np.float64) * 2.0 / A0_D)
    ang = (np.arange(S, dtype=f)[:, None] * inv.astype(f)[None, :]).astype(np.float64)
    scale = A0_D ** -0.25
    c, s = (np.cos(ang) * scale).T, (np.sin(ang) * scale).T
    out["a0_cos"] = np.concatenate([c] * 4).astype(f)
    out["a0_sin"] = np.concatenate([s, s, -s, -s]).astype(f)
    i = np.arange(S)
    far = np.abs(i[:, None] - i[None, :]) > A0_WIN
    out["a0_mask"] = np.where(far, MASKED, 0.0).astype(f).reshape(2, P, S).transpose(1, 0, 2).copy()
    slot = (np.arange(P) // 32) % 2
    out["a0_slot"] = np.stack([slot == 0, slot == 1], 1).astype(f)
    out["a0_bo"] = np.broadcast_to(a["L0_attn_bo"], (P, D))

    def pairs(w):
        lead = w.shape[:-2]
        w = w.reshape(*lead, w.shape[-2] // 2, 2, half, 2)
        n = len(lead)
        return w.transpose(*range(n), n, n + 3, n + 1, n + 2).reshape(*lead, -1, P)

    G = A0_G
    wq = pairs(a["L0_attn_Wq"]).reshape(KD, P, G, A0_PAIRS, P).transpose(2, 1, 0, 3, 4).reshape(G, P, A0_NQ)
    wk = pairs(np.repeat(a["L0_attn_Wk"], 2, axis=1)).reshape(KD, P, G, P).transpose(2, 1, 0, 3).reshape(G, P, A0_NK)
    out["a0_wv"] = a["L0_attn_Wv"].reshape(KD, P, G * A0_D).transpose(1, 0, 2).reshape(P, -1)
    out["a0_bv"] = np.broadcast_to(a["L0_attn_bv"].reshape(-1), (P, G * A0_D))
    bq = pairs(a["L0_attn_bq"]).reshape(G, A0_PAIRS, P).transpose(0, 2, 1)
    bk = pairs(np.repeat(a["L0_attn_bk"], 2, axis=0)).reshape(G, 1, P).transpose(0, 2, 1)
    sk = np.broadcast_to(a["L0_attn_sinks"].reshape(G, 1, A0_R), (G, P, A0_R))
    out["a0_w"] = np.concatenate([wq, wk, bq, bk, sk], axis=2)
    out["a0_wo"] = a["L0_attn_Wo"].reshape(G, 2, P, D).transpose(0, 2, 1, 3)
    both = lambda v: np.broadcast_to(np.asarray(v), (P, v.shape[-1]))
    fm = lambda wt: wt.T.reshape(KD, P, -1).transpose(1, 0, 2)
    out["x0_w"] = np.stack([fm(a["L0_xattn_" + n]) for n in ("Wq", "Wk", "Wv", "Wo")], axis=1)
    out["ctxT"] = a["ctx_2048"].reshape(T, KD, P).transpose(2, 1, 0)
    out["x0_rows"] = np.stack([both(a["L0_xattn_" + n]) for n in ("bv", "bo", "ln_gamma", "ln_beta")], axis=1)
    out["x0_cols"] = np.concatenate([a["L0_xattn_bq"].reshape(KD, P).T, a["L0_xattn_bk"].reshape(KD, P).T], axis=1)
    out["x0_hmask"] = (np.arange(P)[:, None] // X0_D == np.arange(X0_HM)[None, :]).astype(f) * f(X0_D ** -0.5)
    out["x0_rs"] = np.broadcast_to(a["L0_xattn_residual_scale"].reshape(1, 1), (P, 1))
    out["x0_mask"] = a["mask_BxS2_ik0"].reshape(B, 2, P).transpose(2, 0, 1).reshape(P, NT)
    gate = np.concatenate([a["L0_ffn_gate_up_proj"][:, :M0_I].reshape(-1, D), a["L0_ffn_sh_gate_w"]])
    up = np.concatenate([a["L0_ffn_gate_up_proj"][:, M0_I:].reshape(-1, D), a["L0_ffn_sh_up_w"]])
    down = np.concatenate([a["L0_ffn_down_proj"].transpose(0, 2, 1).reshape(-1, D), a["L0_ffn_sh_down_w"].T])
    fill = np.zeros((M0_TILES * P - gate.shape[0], D), f)
    tiled = lambda wt: np.concatenate([wt, fill]).reshape(M0_TILES, P, KD, P).transpose(0, 3, 2, 1).reshape(M0_TILES, P, D)
    out["m0_gu"] = np.concatenate([tiled(gate), tiled(up)], axis=2)
    out["m0_dn"] = np.concatenate([down, fill]).reshape(M0_TILES, P, D)
    out["m0_rw"] = fm(np.concatenate([a["L0_ffn_router_weight"], a["L0_ffn_shared_gate_w"]]))
    out["m0_iota"] = np.broadcast_to(np.arange(M0_E, dtype=f), (P, M0_E))
    half = P // 2
    inv = (1.0 / 10000.0 ** (np.arange(0, P, 2, dtype=f) / P)).astype(f)
    ang = (np.arange(S, dtype=f)[:, None] * inv[None, :]).astype(np.float64)
    c, s = np.cos(ang).T, np.sin(ang).T
    tabs = []
    for scale in (P ** -0.5, 1.0):
        tabs += [np.concatenate([c, c]) * scale, np.concatenate([-s, s]) * scale]
    out["a1_cs"] = np.stack(tabs, axis=1).astype(f)
    above = np.where(np.arange(P)[None, :] > np.arange(P)[:, None], -1.0e30, 0.0).astype(f)
    out["a1_mask"] = np.concatenate([above, np.zeros((P, P), f), above], axis=1)
    out["a1_rows"] = np.stack([both(a["L1_attn_" + n]) for n in ("ln_g", "ln_b", "bo")], axis=1)
    hw = lambda wt: wt.reshape(A1_H, P, KD, P).transpose(0, 3, 2, 1).reshape(A1_H, P, KD * P)
    hb = lambda bb: bb.reshape(A1_H, P, 1)
    out["a1_w"] = np.concatenate([hw(a["L1_attn_" + n]) for n in ("wq", "wk")]
                                 + [hb(a["L1_attn_" + n]) for n in ("bq", "bk")], axis=2)
    wv = a["L1_attn_wv"].reshape(A1_H // 2, 2 * P, KD, P)
    out["a1_wv"] = wv.transpose(0, 3, 2, 1).reshape(A1_H // 2, P, KD * 2 * P)
    bv = np.broadcast_to(a["L1_attn_bv"].reshape(A1_H, 1, P), (A1_H, P, P))
    out["a1_wo"] = np.concatenate([a["L1_attn_wo"].T.reshape(A1_H, P, D), bv], axis=2)
    out["x1_wh"] = a["L1_xattn_Wh"].transpose(1, 0, 2)
    rowm = lambda wt: wt.reshape(-1, P, wt.shape[1]).transpose(1, 0, 2)
    out["x1_wg"], out["x1_wo"] = rowm(a["L1_xattn_wg_w"]), rowm(a["L1_xattn_wo_w"])
    out["x1_rows"] = np.stack([both(a["L1_xattn_" + n]) for n in ("gn_gamma", "gn_beta")], axis=1)
    gam = (1.0 - 2.0 ** (-5.0 - np.arange(X1_H, dtype=f))).astype(f).astype(np.float64)
    ex = np.arange(S)[None, :] - np.arange(S)[:, None]
    dec = np.where(ex[None] <= 0, gam[:, None, None] ** ex[None], 0.0)
    dec = dec / np.sqrt(dec.sum(-1))[:, None, :] / np.sqrt(P)
    dT = dec.transpose(2, 0, 1).reshape(2, P, X1_H, S)
    out["x1_decay"] = np.concatenate([dT[0], dT[1][:, :, P:]], axis=2).astype(f)
    out["f1_wq"] = rowm(a["L1_ffn_W_q"])
    out["f1_keys"] = a["L1_ffn_keys"].transpose(1, 0, 2)
    out["f1_iota"] = np.broadcast_to(np.arange(F1_E, dtype=f), (P, F1_E))
    tl = lambda wt: wt.reshape(-1, P, KD, P).transpose(0, 3, 2, 1).reshape(-1, P, D)
    de, ue = a["L1_ffn_down_embed"], a["L1_ffn_up_embed"]
    up = np.concatenate([tl(a["L1_ffn_up_w"].T), np.zeros((F1_ET, P, D), f)])
    out["f1_w"] = np.concatenate([tl(np.concatenate([a["L1_ffn_gate_w"].T, de])), up,
                                  np.concatenate([a["L1_ffn_down_w"], ue]).reshape(-1, P, D)], axis=2)
    return {n: np.ascontiguousarray(v) for n, v in out.items()}


def kernel(**inputs):
    import concourse.bacc as bacc
    from concourse.bass_utils import run_bass_kernel_spmd

    arrays = layouts({n: np.asarray(v) for n, v in inputs.items()})
    nc = bacc.Bacc("TRN2", target_bir_lowering=False, num_devices=1)
    src = {n: nc.dram_tensor(n, v.shape, mybir.dt.from_np(v.dtype), kind="ExternalInput").ap()
           for n, v in arrays.items()}
    out = nc.dram_tensor("out", (T, D), F32, kind="ExternalOutput").ap()
    program(nc, src, out)
    got = run_bass_kernel_spmd(nc, [arrays], core_ids=[0])
    return got.results[0]["out"].reshape(B, S, D)
```
